# Optimizing a Trainium2 kernel written in Bass

```python
import numpy as np
import jax
import jax.numpy as jnp

def _softmax(x, axis=-1):
    return jax.nn.softmax(x, axis=axis)

def _gelu(x):
    return jax.nn.gelu(x, approximate=True)

def _silu(x):
    return jax.nn.silu(x)

def _sigmoid(x):
    return jax.nn.sigmoid(x)

def _layernorm(x, axis=-1, eps=1e-05):
    m = jnp.mean(x, axis=axis, keepdims=True)
    v = jnp.var(x, axis=axis, keepdims=True)
    return (x - m) / jnp.sqrt(v + eps)

def _scatter_add(tgt, idx, src, axis=0):
    return tgt.at[idx].add(src)

def _segment_sum(src, seg, n):
    return jax.ops.segment_sum(src, seg, n)
kernel_name = 'mk_vit_tower_d2_tok_img768_r4_2f2452'

def setup_inputs(seed: int=0):
    np.random.seed(seed)
    _w = jnp.asarray

    def _rec_inputs():
        import jax
        import jax.numpy as jnp
        _rk = jax.random.key(seed)
        x = -0.00016672 + 0.999947 * jax.random.normal(jax.random.fold_in(_rk, 1), (16, 3, 128, 128), jnp.float32)
        return x
    x = _rec_inputs()

    def _L0_tok_setup():
        import jax, jax.numpy as jnp
        import numpy as np
        IMG = 96
        PATCH = 16
        CH = 3
        EMB = 192
        key = jax.random.key(seed)
        k1, k2, k3 = jax.random.split(key, 3)
        lidar_batch = jax.random.normal(k1, (64, CH, IMG, IMG), dtype=jnp.float32)
        in_feat = PATCH * PATCH * CH
        bound = 1.0 / np.sqrt(in_feat)
        W = jax.random.uniform(k2, (EMB, in_feat), dtype=jnp.float32, minval=-bound, maxval=bound)
        b = jax.random.uniform(k3, (EMB,), dtype=jnp.float32, minval=-bound, maxval=bound)
        return {'lidar_batch': lidar_batch, 'W': W, 'b': b}
    _L0_tok_all = _L0_tok_setup()
    _L0_tok_in = {k: v for k, v in _L0_tok_all.items() if k in ('W', 'b')}
    del _L0_tok_all

    def _L0_attn_setup():
        import jax, jax.numpy as jnp
        import numpy as np
        N_HEAD = 12
        N_EMBD = 192
        BLOCK = 512
        THETA = 10000.0

        def _rope_tables(head_dim, end, theta=THETA):
            half = head_dim // 2
            freqs = 1.0 / theta ** (jnp.arange(0, head_dim, 2, dtype=jnp.float32) / head_dim)
            t = jnp.arange(end, dtype=jnp.float32)
            ang = jnp.outer(t, freqs)
            return (jnp.cos(ang), jnp.sin(ang))

        def _apply_rope(x, cos, sin):
            B, H, T, hd = x.shape
            xr = x.reshape(B, H, T, hd // 2, 2)
            x0, x1 = (xr[..., 0], xr[..., 1])
            c = cos[None, None, :T, :]
            s = sin[None, None, :T, :]
            o0 = x0 * c - x1 * s
            o1 = x0 * s + x1 * c
            return jnp.stack([o0, o1], axis=-1).reshape(B, H, T, hd)
        key = jax.random.key(seed)
        ks = jax.random.split(key, 9)
        B, T, C = (2, 512, N_EMBD)
        std = 0.02
        return {'x': jax.random.normal(ks[0], (B, T, C), jnp.float32), 'norm_scale': jnp.ones((C,), jnp.float32), 'norm_bias': jnp.zeros((C,), jnp.float32), 'W_attn': jax.random.normal(ks[1], (C, 3 * C), jnp.float32) * std, 'b_attn': jax.random.normal(ks[2], (3 * C,), jnp.float32) * std, 'W_proj': jax.random.normal(ks[3], (C, C), jnp.float32) * std, 'b_proj': jax.random.normal(ks[4], (C,), jnp.float32) * std, 'sinks': jax.random.normal(ks[5], (N_HEAD,), jnp.float32) * 0.5, 'rezero': jax.random.normal(ks[6], (1,), jnp.float32) * 0.1}
    _L0_attn_all = _L0_attn_setup()
    _L0_attn_in = {k: v for k, v in _L0_attn_all.items() if k in ('norm_scale', 'norm_bias', 'W_attn', 'b_attn', 'W_proj', 'b_proj', 'sinks', 'rezero')}
    del _L0_attn_all

    def _L0_ffn_setup():
        import jax, jax.numpy as jnp
        import numpy as np
        B, T, E = (2, 256, 192)
        H = 768
        N_EXP = 4
        key = jax.random.key(seed)
        ks = jax.random.split(key, 8)
        s_e = 1.0 / np.sqrt(E)
        s_h = 1.0 / np.sqrt(H)
        return {'x': jax.random.normal(ks[0], (B, T, E), dtype=jnp.float32), 'Wg': jax.random.uniform(ks[1], (E, N_EXP), minval=-s_e, maxval=s_e, dtype=jnp.float32), 'bg': jax.random.uniform(ks[2], (N_EXP,), minval=-s_e, maxval=s_e, dtype=jnp.float32), 'W1': jax.random.uniform(ks[3], (N_EXP, E, H), minval=-s_e, maxval=s_e, dtype=jnp.float32), 'b1': jax.random.uniform(ks[4], (N_EXP, H), minval=-s_e, maxval=s_e, dtype=jnp.float32), 'W2': jax.random.uniform(ks[5], (N_EXP, H, E), minval=-s_h, maxval=s_h, dtype=jnp.float32), 'b2': jax.random.uniform(ks[6], (N_EXP, E), minval=-s_h, maxval=s_h, dtype=jnp.float32)}
    _L0_ffn_all = _L0_ffn_setup()
    _L0_ffn_in = {k: v for k, v in _L0_ffn_all.items() if k in ('Wg', 'bg', 'W1', 'b1', 'W2', 'b2')}
    del _L0_ffn_all

    def _L1_attn_setup():
        import jax, jax.numpy as jnp
        import numpy as np
        B, L = (4, 256)
        D_MODEL, D_INNER, D_STATE, D_CONV, DT_RANK = (192, 384, 16, 4, 48)
        N_EXP, D_FF = (4, 768)
        EPS = 1e-06

        def _rmsnorm(v, w):
            return v * jax.lax.rsqrt(jnp.mean(v * v, axis=-1, keepdims=True) + EPS) * w

        def _ssm(x, in_proj_w, conv_w, conv_b, x_proj_w, dt_proj_w, dt_proj_b, A_log, D_param, out_proj_w):
            xz = x @ in_proj_w
            xs, z = jnp.split(xz, 2, axis=-1)
            xc = jnp.transpose(xs, (0, 2, 1))
            xc = jax.lax.conv_general_dilated(xc, conv_w[:, None, :], (1,), [(D_CONV - 1, 0)], feature_group_count=D_INNER, dimension_numbers=('NCH', 'OIH', 'NCH'))
            xc = jax.nn.silu(jnp.transpose(xc, (0, 2, 1)) + conv_b)
            dbc = xc @ x_proj_w
            dt, Bm, Cm = jnp.split(dbc, [DT_RANK, DT_RANK + D_STATE], axis=-1)
            delta = jax.nn.softplus(dt @ dt_proj_w + dt_proj_b)
            A = -jnp.exp(A_log)

            def step(h, inp):
                d, b, c, u = inp
                h = h * jnp.exp(d[..., None] * A) + (d * u)[..., None] * b[:, None, :]
                y = jnp.einsum('bds,bs->bd', h, c)
                return (h, y)
            h0 = jnp.zeros((x.shape[0], D_INNER, D_STATE), xs.dtype)
            inputs = (jnp.swapaxes(delta, 0, 1), jnp.swapaxes(Bm, 0, 1), jnp.swapaxes(Cm, 0, 1), jnp.swapaxes(xc, 0, 1))
            _, ys = jax.lax.scan(step, h0, inputs)
            y = jnp.swapaxes(ys, 0, 1) + xc * D_param
            y = y * jax.nn.silu(z)
            return y @ out_proj_w

        def _top1_moe(x, gate_w, w1, w3, w2):
            logits = x @ gate_w
            probs = jax.nn.softmax(logits, axis=-1)
            one_hot = jax.nn.one_hot(jnp.argmax(probs, axis=-1), N_EXP, dtype=x.dtype)
            gate = jnp.max(probs, axis=-1)
            h = jax.nn.silu(jnp.einsum('bld,edf->blef', x, w1)) * jnp.einsum('bld,edf->blef', x, w3)
            eo = jnp.einsum('blef,efd->bled', h, w2)
            out = jnp.einsum('ble,bled->bld', one_hot * gate[..., None], eo)
            f = jnp.mean(one_hot, axis=(0, 1))
            p = jnp.mean(probs, axis=(0, 1))
            aux = N_EXP * jnp.sum(f * p)
            return (out, aux)

        def _reference_tuple_inner(x, norm1_w, norm2_w, in_proj_w, conv_w, conv_b, x_proj_w, dt_proj_w, dt_proj_b, A_log, D_param, out_proj_w, ls_ssm_g, ls_ffn_g, gate_w, w1, w3, w2):
            ssm_out = _ssm(_rmsnorm(x, norm1_w), in_proj_w, conv_w, conv_b, x_proj_w, dt_proj_w, dt_proj_b, A_log, D_param, out_proj_w)
            h = x + ls_ssm_g * ssm_out
            ffn_out, aux = _top1_moe(_rmsnorm(h, norm2_w), gate_w, w1, w3, w2)
            out = h + ls_ffn_g * ffn_out
            return (out, aux)
        key = jax.random.key(seed)
        ks = jax.random.split(key, 12)
        n = lambda k, shape, s=0.02: jax.random.normal(k, shape, dtype=jnp.float32) * s
        return {'x': jax.random.normal(ks[0], (B, L, D_MODEL), dtype=jnp.float32), 'norm1_w': jnp.ones((D_MODEL,), jnp.float32), 'norm2_w': jnp.ones((D_MODEL,), jnp.float32), 'in_proj_w': n(ks[1], (D_MODEL, 2 * D_INNER)), 'conv_w': n(ks[2], (D_INNER, D_CONV), 0.1), 'conv_b': jnp.zeros((D_INNER,), jnp.float32), 'x_proj_w': n(ks[3], (D_INNER, DT_RANK + 2 * D_STATE)), 'dt_proj_w': n(ks[4], (DT_RANK, D_INNER)), 'dt_proj_b': jnp.full((D_INNER,), -4.6, jnp.float32), 'A_log': jnp.broadcast_to(jnp.log(jnp.arange(1, D_STATE + 1, dtype=jnp.float32)), (D_INNER, D_STATE)) + jnp.zeros((D_INNER, D_STATE), jnp.float32), 'D_param': jnp.ones((D_INNER,), jnp.float32), 'out_proj_w': n(ks[5], (D_INNER, D_MODEL)), 'ls_ssm_g': jnp.full((D_MODEL,), 1e-05, jnp.float32), 'ls_ffn_g': jnp.full((D_MODEL,), 1e-05, jnp.float32), 'gate_w': n(ks[6], (D_MODEL, N_EXP)), 'w1': n(ks[7], (N_EXP, D_MODEL, D_FF)), 'w3': n(ks[8], (N_EXP, D_MODEL, D_FF)), 'w2': n(ks[9], (N_EXP, D_FF, D_MODEL))}
    _L1_attn_all = _L1_attn_setup()
    _L1_attn_in = {k: v for k, v in _L1_attn_all.items() if k in ('norm1_w', 'norm2_w', 'in_proj_w', 'conv_w', 'conv_b', 'x_proj_w', 'dt_proj_w', 'dt_proj_b', 'A_log', 'D_param', 'out_proj_w', 'ls_ssm_g', 'ls_ffn_g', 'gate_w', 'w1', 'w3', 'w2')}
    del _L1_attn_all

    def _L1_ffn_setup():
        import jax, jax.numpy as jnp
        import numpy as np
        B, M, D = (32, 196, 192)
        N, P, H = (64, 1, 768)
        EPS = 1e-12

        def _l2norm(v, axis):
            n = jnp.sqrt(jnp.sum(v * v, axis=axis, keepdims=True))
            return v / jnp.maximum(n, EPS)
        key = jax.random.key(seed)
        ks = jax.random.split(key, 7)
        x = jax.random.normal(ks[0], (B, M, D), dtype=jnp.float32)
        phi = jax.random.normal(ks[1], (D, N, P), dtype=jnp.float32) * (1.0 / D ** 0.5)
        scale = jnp.ones((1,), dtype=jnp.float32)
        w1 = jax.random.normal(ks[2], (N, D, H), dtype=jnp.float32) * (1.0 / D ** 0.5)
        b1 = jnp.zeros((N, H), dtype=jnp.float32)
        w2 = jax.random.normal(ks[3], (N, H, D), dtype=jnp.float32) * (1.0 / H ** 0.5)
        b2 = jnp.zeros((N, D), dtype=jnp.float32)
        return {'x': x, 'phi': phi, 'scale': scale, 'w1': w1, 'b1': b1, 'w2': w2, 'b2': b2}
    _L1_ffn_all = _L1_ffn_setup()
    _L1_ffn_in = {k: v for k, v in _L1_ffn_all.items() if k in ('phi', 'scale', 'w1', 'b1', 'w2', 'b2')}
    del _L1_ffn_all
    return {'x': x, 'L0_tok_W': _L0_tok_in['W'], 'L0_tok_b': _L0_tok_in['b'], 'L0_attn_norm_scale': _L0_attn_in['norm_scale'], 'L0_attn_norm_bias': _L0_attn_in['norm_bias'], 'L0_attn_W_attn': _L0_attn_in['W_attn'], 'L0_attn_b_attn': _L0_attn_in['b_attn'], 'L0_attn_W_proj': _L0_attn_in['W_proj'], 'L0_attn_b_proj': _L0_attn_in['b_proj'], 'L0_attn_sinks': _L0_attn_in['sinks'], 'L0_attn_rezero': _L0_attn_in['rezero'], 'L0_ffn_Wg': _L0_ffn_in['Wg'], 'L0_ffn_bg': _L0_ffn_in['bg'], 'L0_ffn_W1': _L0_ffn_in['W1'], 'L0_ffn_b1': _L0_ffn_in['b1'], 'L0_ffn_W2': _L0_ffn_in['W2'], 'L0_ffn_b2': _L0_ffn_in['b2'], 'L1_attn_norm1_w': _L1_attn_in['norm1_w'], 'L1_attn_norm2_w': _L1_attn_in['norm2_w'], 'L1_attn_in_proj_w': _L1_attn_in['in_proj_w'], 'L1_attn_conv_w': _L1_attn_in['conv_w'], 'L1_attn_conv_b': _L1_attn_in['conv_b'], 'L1_attn_x_proj_w': _L1_attn_in['x_proj_w'], 'L1_attn_dt_proj_w': _L1_attn_in['dt_proj_w'], 'L1_attn_dt_proj_b': _L1_attn_in['dt_proj_b'], 'L1_attn_A_log': _L1_attn_in['A_log'], 'L1_attn_D_param': _L1_attn_in['D_param'], 'L1_attn_out_proj_w': _L1_attn_in['out_proj_w'], 'L1_attn_ls_ssm_g': _L1_attn_in['ls_ssm_g'], 'L1_attn_ls_ffn_g': _L1_attn_in['ls_ffn_g'], 'L1_attn_gate_w': _L1_attn_in['gate_w'], 'L1_attn_w1': _L1_attn_in['w1'], 'L1_attn_w3': _L1_attn_in['w3'], 'L1_attn_w2': _L1_attn_in['w2'], 'L1_ffn_phi': _L1_ffn_in['phi'], 'L1_ffn_scale': _L1_ffn_in['scale'], 'L1_ffn_w1': _L1_ffn_in['w1'], 'L1_ffn_b1': _L1_ffn_in['b1'], 'L1_ffn_w2': _L1_ffn_in['w2'], 'L1_ffn_b2': _L1_ffn_in['b2']}

def reference(x, L0_tok_W, L0_tok_b, L0_attn_norm_scale, L0_attn_norm_bias, L0_attn_W_attn, L0_attn_b_attn, L0_attn_W_proj, L0_attn_b_proj, L0_attn_sinks, L0_attn_rezero, L0_ffn_Wg, L0_ffn_bg, L0_ffn_W1, L0_ffn_b1, L0_ffn_W2, L0_ffn_b2, L1_attn_norm1_w, L1_attn_norm2_w, L1_attn_in_proj_w, L1_attn_conv_w, L1_attn_conv_b, L1_attn_x_proj_w, L1_attn_dt_proj_w, L1_attn_dt_proj_b, L1_attn_A_log, L1_attn_D_param, L1_attn_out_proj_w, L1_attn_ls_ssm_g, L1_attn_ls_ffn_g, L1_attn_gate_w, L1_attn_w1, L1_attn_w3, L1_attn_w2, L1_ffn_phi, L1_ffn_scale, L1_ffn_w1, L1_ffn_b1, L1_ffn_w2, L1_ffn_b2):
    import jax
    import jax.numpy as jnp

    def _L0_tok_ref(lidar_batch, W, b):
        import jax, jax.numpy as jnp
        import numpy as np
        IMG = 96
        PATCH = 16
        CH = 3
        EMB = 192
        B, C, H, Wd = lidar_batch.shape
        p = PATCH
        hp, wp = (H // p, Wd // p)
        x = lidar_batch.reshape(B, C, hp, p, wp, p)
        x = x.transpose(0, 2, 4, 3, 5, 1)
        x = x.reshape(B, hp * wp, p * p * C)
        out = jnp.einsum('bnf,ef->bne', x, W) + b
        return out

    def _L0_attn_ref(x, norm_scale, norm_bias, W_attn, b_attn, W_proj, b_proj, sinks, rezero):
        import jax, jax.numpy as jnp
        import numpy as np
        N_HEAD = 12
        N_EMBD = 192
        BLOCK = 512
        THETA = 10000.0

        def _rope_tables(head_dim, end, theta=THETA):
            half = head_dim // 2
            freqs = 1.0 / theta ** (jnp.arange(0, head_dim, 2, dtype=jnp.float32) / head_dim)
            t = jnp.arange(end, dtype=jnp.float32)
            ang = jnp.outer(t, freqs)
            return (jnp.cos(ang), jnp.sin(ang))

        def _apply_rope(x, cos, sin):
            B, H, T, hd = x.shape
            xr = x.reshape(B, H, T, hd // 2, 2)
            x0, x1 = (xr[..., 0], xr[..., 1])
            c = cos[None, None, :T, :]
            s = sin[None, None, :T, :]
            o0 = x0 * c - x1 * s
            o1 = x0 * s + x1 * c
            return jnp.stack([o0, o1], axis=-1).reshape(B, H, T, hd)
        B, T, C = x.shape
        H = N_HEAD
        hd = C // H
        xn = norm_scale * x + norm_bias
        qkv = xn @ W_attn + b_attn
        q, k, v = jnp.split(qkv, 3, axis=-1)
        q = q.reshape(B, T, H, hd).transpose(0, 2, 1, 3)
        k = k.reshape(B, T, H, hd).transpose(0, 2, 1, 3)
        v = v.reshape(B, T, H, hd).transpose(0, 2, 1, 3)
        cos, sin = _rope_tables(hd, T)
        q = _apply_rope(q, cos, sin)
        k = _apply_rope(k, cos, sin)
        scale = 1.0 / jnp.sqrt(jnp.float32(hd))
        att = jnp.einsum('bhqd,bhkd->bhqk', q, k) * scale
        causal = jnp.tril(jnp.ones((T, T), dtype=bool))
        att = jnp.where(causal[None, None], att, -jnp.inf)
        sink_col = jnp.broadcast_to(sinks.reshape(1, H, 1, 1), (B, H, T, 1))
        att = jnp.concatenate([sink_col, att], axis=-1)
        att = jax.nn.softmax(att, axis=-1)[..., 1:]
        y = jnp.einsum('bhqk,bhkd->bhqd', att, v)
        y = y.transpose(0, 2, 1, 3).reshape(B, T, C)
        y = (y @ W_proj + b_proj) * rezero
        return y

    def _L0_ffn_ref(x, Wg, bg, W1, b1, W2, b2):
        import jax, jax.numpy as jnp
        import numpy as np
        B, T, E = (2, 256, 192)
        H = 768
        N_EXP = 4
        gate_logits = jnp.einsum('bte,en->btn', x, Wg) + bg
        top = jnp.argmax(gate_logits, axis=-1)
        h = jax.nn.gelu(jnp.einsum('bte,neh->nbth', x, W1) + b1[:, None, None, :], approximate=False)
        y = jnp.einsum('nbth,nhe->nbte', h, W2) + b2[:, None, None, :]
        onehot = jax.nn.one_hot(top, N_EXP, dtype=x.dtype)
        out = jnp.einsum('nbte,btn->bte', y, onehot)
        return out

    def _L1_attn_ref(x, norm1_w, norm2_w, in_proj_w, conv_w, conv_b, x_proj_w, dt_proj_w, dt_proj_b, A_log, D_param, out_proj_w, ls_ssm_g, ls_ffn_g, gate_w, w1, w3, w2):
        import jax, jax.numpy as jnp
        import numpy as np
        B, L = (4, 256)
        D_MODEL, D_INNER, D_STATE, D_CONV, DT_RANK = (192, 384, 16, 4, 48)
        N_EXP, D_FF = (4, 768)
        EPS = 1e-06

        def _rmsnorm(v, w):
            return v * jax.lax.rsqrt(jnp.mean(v * v, axis=-1, keepdims=True) + EPS) * w

        def _ssm(x, in_proj_w, conv_w, conv_b, x_proj_w, dt_proj_w, dt_proj_b, A_log, D_param, out_proj_w):
            xz = x @ in_proj_w
            xs, z = jnp.split(xz, 2, axis=-1)
            xc = jnp.transpose(xs, (0, 2, 1))
            xc = jax.lax.conv_general_dilated(xc, conv_w[:, None, :], (1,), [(D_CONV - 1, 0)], feature_group_count=D_INNER, dimension_numbers=('NCH', 'OIH', 'NCH'))
            xc = jax.nn.silu(jnp.transpose(xc, (0, 2, 1)) + conv_b)
            dbc = xc @ x_proj_w
            dt, Bm, Cm = jnp.split(dbc, [DT_RANK, DT_RANK + D_STATE], axis=-1)
            delta = jax.nn.softplus(dt @ dt_proj_w + dt_proj_b)
            A = -jnp.exp(A_log)

            def step(h, inp):
                d, b, c, u = inp
                h = h * jnp.exp(d[..., None] * A) + (d * u)[..., None] * b[:, None, :]
                y = jnp.einsum('bds,bs->bd', h, c)
                return (h, y)
            h0 = jnp.zeros((x.shape[0], D_INNER, D_STATE), xs.dtype)
            inputs = (jnp.swapaxes(delta, 0, 1), jnp.swapaxes(Bm, 0, 1), jnp.swapaxes(Cm, 0, 1), jnp.swapaxes(xc, 0, 1))
            _, ys = jax.lax.scan(step, h0, inputs)
            y = jnp.swapaxes(ys, 0, 1) + xc * D_param
            y = y * jax.nn.silu(z)
            return y @ out_proj_w

        def _top1_moe(x, gate_w, w1, w3, w2):
            logits = x @ gate_w
            probs = jax.nn.softmax(logits, axis=-1)
            one_hot = jax.nn.one_hot(jnp.argmax(probs, axis=-1), N_EXP, dtype=x.dtype)
            gate = jnp.max(probs, axis=-1)
            h = jax.nn.silu(jnp.einsum('bld,edf->blef', x, w1)) * jnp.einsum('bld,edf->blef', x, w3)
            eo = jnp.einsum('blef,efd->bled', h, w2)
            out = jnp.einsum('ble,bled->bld', one_hot * gate[..., None], eo)
            f = jnp.mean(one_hot, axis=(0, 1))
            p = jnp.mean(probs, axis=(0, 1))
            aux = N_EXP * jnp.sum(f * p)
            return (out, aux)

        def _reference_tuple_inner(x, norm1_w, norm2_w, in_proj_w, conv_w, conv_b, x_proj_w, dt_proj_w, dt_proj_b, A_log, D_param, out_proj_w, ls_ssm_g, ls_ffn_g, gate_w, w1, w3, w2):
            ssm_out = _ssm(_rmsnorm(x, norm1_w), in_proj_w, conv_w, conv_b, x_proj_w, dt_proj_w, dt_proj_b, A_log, D_param, out_proj_w)
            h = x + ls_ssm_g * ssm_out
            ffn_out, aux = _top1_moe(_rmsnorm(h, norm2_w), gate_w, w1, w3, w2)
            out = h + ls_ffn_g * ffn_out
            return (out, aux)
        return _reference_tuple_inner(x, norm1_w, norm2_w, in_proj_w, conv_w, conv_b, x_proj_w, dt_proj_w, dt_proj_b, A_log, D_param, out_proj_w, ls_ssm_g, ls_ffn_g, gate_w, w1, w3, w2)[0]

    def _L1_ffn_ref(x, phi, scale, w1, b1, w2, b2):
        import jax, jax.numpy as jnp
        import numpy as np
        B, M, D = (32, 196, 192)
        N, P, H = (64, 1, 768)
        EPS = 1e-12

        def _l2norm(v, axis):
            n = jnp.sqrt(jnp.sum(v * v, axis=axis, keepdims=True))
            return v / jnp.maximum(n, EPS)
        xn = _l2norm(x, axis=2)
        phin = scale * _l2norm(phi, axis=0)
        logits = jnp.einsum('bmd,dnp->bmnp', xn, phin)
        d = jax.nn.softmax(logits, axis=1)
        b_, m_, n_, p_ = logits.shape
        c = jax.nn.softmax(logits.reshape(b_, m_, n_ * p_), axis=-1).reshape(b_, m_, n_, p_)
        xs = jnp.einsum('bmd,bmnp->bnpd', xn, d)
        h = jax.nn.gelu(jnp.einsum('bnpd,ndh->bnph', xs, w1) + b1[None, :, None, :], approximate=False)
        ys = jnp.einsum('bnph,nhd->bnpd', h, w2) + b2[None, :, None, :]
        y = jnp.einsum('bnpd,bmnp->bmd', ys, c)
        return y
    h = _L0_tok_ref(x, L0_tok_W, L0_tok_b)
    h = h + _L0_attn_ref(_layernorm(h, axis=-1), L0_attn_norm_scale, L0_attn_norm_bias, L0_attn_W_attn, L0_attn_b_attn, L0_attn_W_proj, L0_attn_b_proj, L0_attn_sinks, L0_attn_rezero)
    h = h + _L0_ffn_ref(_layernorm(h, axis=-1), L0_ffn_Wg, L0_ffn_bg, L0_ffn_W1, L0_ffn_b1, L0_ffn_W2, L0_ffn_b2)
    h = h + _L1_attn_ref(_layernorm(h, axis=-1), L1_attn_norm1_w, L1_attn_norm2_w, L1_attn_in_proj_w, L1_attn_conv_w, L1_attn_conv_b, L1_attn_x_proj_w, L1_attn_dt_proj_w, L1_attn_dt_proj_b, L1_attn_A_log, L1_attn_D_param, L1_attn_out_proj_w, L1_attn_ls_ssm_g, L1_attn_ls_ffn_g, L1_attn_gate_w, L1_attn_w1, L1_attn_w3, L1_attn_w2)
    h = h + _L1_ffn_ref(_layernorm(h, axis=-1), L1_ffn_phi, L1_ffn_scale, L1_ffn_w1, L1_ffn_b1, L1_ffn_w2, L1_ffn_b2)
    return h

_drawn_inputs = setup_inputs


def setup_inputs(seed=0):
    import zlib

    import numpy as np

    out = dict(_drawn_inputs(seed))
    spreads = {'L0_attn_norm_scale': (1.0, 0.6),
     'L0_attn_norm_bias': (0.0, 0.8),
     'L1_attn_norm1_w': (1.0, 0.6),
     'L1_attn_norm2_w': (1.0, 0.6),
     'L1_attn_conv_b': (0.0, 2.0),
     'L1_attn_dt_proj_b': (-4.599999904632568, 0.6),
     'L1_attn_D_param': (1.0, 0.6),
     'L1_attn_ls_ssm_g': (9.999999747378752e-06, 0.6),
     'L1_attn_ls_ffn_g': (9.999999747378752e-06, 0.6),
     'L1_ffn_b1': (0.0, 0.8),
     'L1_ffn_b2': (0.0, 0.8)}
    factors = {'L0_attn_W_attn': 4.915,
     'L0_attn_b_attn': 5.751,
     'L0_attn_W_proj': 8.0,
     'L0_attn_b_proj': 2.856,
     'L0_attn_sinks': 8.0,
     'L1_attn_in_proj_w': 8.0,
     'L1_attn_conv_w': 8.0,
     'L1_attn_x_proj_w': 8.0,
     'L1_attn_out_proj_w': 8.0,
     'L1_attn_gate_w': 64.0,
     'L1_attn_w1': 64.0,
     'L1_attn_w3': 64.0,
     'L1_attn_w2': 64.0,
     'L1_ffn_phi': 21.517,
     'L1_ffn_w1': 8.0,
     'L1_ffn_w2': 8.0,
     'L0_ffn_b1': 2.972,
     'L1_attn_A_log': 3.835}
    for name, (base, spread) in spreads.items():
        noise = np.random.default_rng([zlib.crc32(name.encode()), seed]).standard_normal(out[name].shape)
        drawn = base * np.exp(spread * noise) if base else spread * noise
        out[name] = jnp.asarray(drawn.astype(out[name].dtype))
    for name, factor in factors.items():
        out[name] = (out[name] * factor).astype(out[name].dtype)
    return out
```

```python
from contextlib import ExitStack

import concourse.bass as bass
from concourse import mybir

F32 = mybir.dt.float32
BF16 = mybir.dt.bfloat16
I32 = mybir.dt.int32
U16 = mybir.dt.uint16
U32 = mybir.dt.uint32
ALU = mybir.AluOpType
ACT = mybir.ActivationFunctionType
AX = mybir.AxisListType.X

P = 128
EMB = 192
EB = EMB - P
NIMG, TOK = 16, 64
NTOK = NIMG * TOK
NT = NTOK // P
PATCH_F = 768
NPC = PATCH_F // P
NH, HD = 12, 16
NHA = P // HD
NHB = NH - NHA
NEXP = 4
HID = 768
NFC = HID // P
NBLK = NT + NEXP - 1
DIN = 384
NCH = DIN // P
NST = 16
DTR = 48
BC0 = 64
XPJ = BC0 + 2 * NST
HALF = NTOK // 2
HIMG = NIMG // 2
NX = 64
NPAIR = NX // 2
GRP = 8
NGRP = NX // GRP
QP = 4
NSLOT = 8
PAIR_W = 2 * HID + HID + 2 * NFC * EMB
TAIL = 9472
BIG = 1.0e30
LN_EPS, RMS_EPS, L2_EPS = 1e-5, 1e-6, 1e-12


def columns(parts):
    at, out = 0, {}
    for name, n in parts:
        out[name] = (at, at + n)
        at += n
    return out, at


CST, NCST = columns([("ident", P), ("upper", P), ("ones", P), ("causal", TOK), ("kmask", NHA), ("cos2", HD),
                     ("sin", HD // 2), ("nsin", HD // 2), ("iota", NEXP), ("iota_far", NEXP),
                     ("by128", NT), ("block", NBLK), ("carry", NEXP * NT), ("neg_half", NT), ("half", NT),
                     ("b_rows", P), ("par0", 1), ("par1", 1)])
VEC, NVEC = columns([("nscale", 2), ("nbias", 2), ("norm1", 2), ("norm2", 2), ("conv_w", 4 * NCH),
                     ("conv_b", NCH), ("dt_b", NCH), ("A_log", NCH * NST), ("D", NCH), ("rezero", 1),
                     ("scale", 1), ("sinks", NH), ("ls_ssm", EMB), ("ls_ffn", EMB)])
ATW, NATW = columns([("qkv_a", 3 * EMB), ("qkv_b", 3 * EMB), ("proj_a", EMB), ("proj_b", EMB),
                     ("g0_a", NEXP), ("g0_b", NEXP), ("g1_a", NEXP), ("g1_b", NEXP), ("phi_a", NX), ("phi_b", NX)])
SSW, NSSW = columns([("in_a", 2 * DIN), ("in_b", 2 * DIN), ("x", NCH * XPJ), ("dt", DIN), ("out", NCH * EMB)])


class Chain:

    def __init__(self, eng, sem):
        self.eng, self.sem, self.base, self.n = eng, sem, 0, 0

    def __call__(self, ins):
        ins.then_inc(self.sem, 1)
        self.n += 1
        return ins

    def sync(self):
        self.eng.wait_ge(self.sem, self.base + self.n)

    def turn(self, i, per):
        self.before = self.base + self.n
        self.base, self.n = self.before + i * per, 0

    def turns(self, n, per):
        assert self.n == per, (self.n, per)
        self.base, self.n = self.before + n * per, 0


def one(ap3, i):
    if isinstance(i, int):
        return ap3[:, i, :]
    return ap3[:, bass.ds(i, 1), :].rearrange("p o f -> p (o f)")


def build(nc, d, out):
    with ExitStack() as ctx:
        def sb(name, shape, dt=F32):
            return ctx.enter_context(nc.sbuf_tensor(name, shape, dt))

        def sem(name):
            return ctx.enter_context(nc.semaphore(name))

        stage_sems = []

        def stage_sem(name):
            stage_sems.append(nc.alloc_semaphore(name))
            return stage_sems[-1]

        def new_sems():
            nc.clear_and_free_semaphores(stage_sems)
            stage_sems.clear()
            nc.all_engine_barrier()

        ring = sb("ring", [P, NSLOT * PAIR_W])
        tail = sb("tail", [P, TAIL])
        h = sb("h", [P, NT, EMB])
        cst = sb("cst", [P, NCST])
        vec = sb("vec", [P, NVEC])
        stats = sb("stats", [P, NT, 2])
        bn = sb("bn", [P, 6])
        mean_var = sb("mean_var", [P, 2])
        h_new = sb("h_new", [P, EMB])
        ln_mean = sb("ln_mean", [P, NT])
        ln_rstd = sb("ln_rstd", [P, NT])
        ln_tmp = sb("ln_tmp", [P, NT])
        row_scale = sb("row_scale", [P, NT])
        psum = ctx.enter_context(nc.psum_tensor("psum", [P, 8 * 512], F32))

        def bank(b, n=512, at=0):
            return psum[:, 512 * b + at:512 * b + at + n]

        def C(name, rows=P):
            a, b = CST[name]
            return cst[0:rows, a:b]

        def V(name, rows=P):
            a, b = VEC[name]
            return vec[0:rows, a:b]

        ident = C("ident")
        x_sorted = nc.dram_tensor("x_sorted", [NBLK * P, EMB], F32).ap()
        y_sorted = nc.dram_tensor("y_sorted", [NBLK * P, EMB], F32).ap()
        y_slots = nc.dram_tensor("y_slots", [NX, NIMG * EMB], F32).ap()

        class Region:

            def __init__(self, buf, at, end):
                self.buf, self.at, self.end = buf, at, end

            def take(self, n, rows=P):
                a = self.at
                self.at += n
                assert self.at <= self.end, (self.at, self.end)
                return self.buf[0:rows, a:a + n]

        MOE0 = 2 * NEXP * HID + NEXP * NFC * EMB
        W13 = 4 * NEXP * HID
        ring_cols = NSLOT * PAIR_W
        t = Region(tail, 0, TAIL)
        m1_w2 = t.take(NEXP * NFC * EMB).rearrange("p (e c n) -> p e c n", e=NEXP, c=NFC)
        ssw = t.take(NSSW)
        atw = t.take(NATW)
        r0 = Region(ring, 0, ring_cols - W13)
        m0_buf = r0.take(MOE0)
        m0_w1a = m0_buf[:, 0:NEXP * HID].rearrange("p (e f) -> p e f", e=NEXP)
        m0_w1b = m0_buf[0:EB + 1, NEXP * HID:2 * NEXP * HID].rearrange("p (e f) -> p e f", e=NEXP)
        m0_w2 = m0_buf[:, 2 * NEXP * HID:MOE0].rearrange("p (e c n) -> p e c n", e=NEXP, c=NFC)
        w13 = ring[:, ring_cols - W13:ring_cols].rearrange("p (k e f) -> p k e f", k=4, e=NEXP)
        m1_w1a, m1_w1b, m1_w3a, m1_w3b = (w13[0:(P, EB, P, EB)[k], k] for k in range(4))
        b2_row = r0.take(HID, 1)
        free0 = r0.at

        def W(name, rows=P):
            a, b = ATW[name]
            return atw[0:rows, a:b]

        def WS(name, rows=P):
            a, b = SSW[name]
            return ssw[0:rows, a:b]

        mo = sb("mo", [P, 2496])
        m = Region(mo, 0, 2496)
        xT_a = m.take(P)
        xT_b = m.take(P)
        hid = m.take(HID)
        hidT = m.take(HID)
        hid2 = m.take(EMB)
        x_n = m.take(EMB)
        slotf = m.take(NT)
        logits = m.take(NT * NEXP)
        oh = m.take(NT * NEXP)
        rt = [m.take(NT * NEXP) for _ in range(3)]
        mx = m.take(NT)
        sb_ = m.take(NEXP + 1)
        blkc = m.take(NEXP)
        bl = m.take(NBLK * NEXP)
        eidf = m.take(NBLK)
        gate = m.take(NT)
        slot_u = sb("slot_u", [P, NT], U32)
        eid = sb("eid", [P, NBLK], I32)
        yout = sb("yout", [P, 2, EMB])

        loaded = {n: sem(n + "_in") for n in ("tok_w", "tok_b", "cst", "vec", "atw", "moe0", "moe0_b2", "ssw", "moe1_w13", "moe1_w2")}
        zeroed, zeros = sem("zeroed"), sem("zeros")

        def ln_scalars(dve, link, pool_done):
            link(dve.tensor_copy(ln_mean[:, :], stats[:, :, 0]))
            link(dve.tensor_scalar(ln_tmp[:, :], stats[:, :, 1], LN_EPS, None, ALU.add))
            link.sync()

        def row_stats(dve, link, x, i, to=h):
            link(dve.bn_stats(bn[:, :], x))
            link.sync()
            link(dve.tensor_scalar(one(to, i), x, 1.0, None, ALU.mult))
            link(dve.bn_aggr(mean_var[:, :], bn[:, :]))
            link.sync()
            link(dve.tensor_scalar(one(stats, i), mean_var[:, :], 1.0, None, ALU.mult))

        xp_all = ring[:, free0:free0 + NPC * NTOK].rearrange("p (c t) -> p c t", c=NPC)
        tokw = ring[:, free0 + NPC * NTOK:free0 + NPC * NTOK + NPC * EMB].rearrange("p (c n) -> p c n", c=NPC)
        tok_b = ring[0:1, free0 + NPC * NTOK + NPC * EMB:free0 + NPC * NTOK + NPC * EMB + EMB]
        NPX = 2
        patches_in = [sem(f"patches_in{n}") for n in range(NPX)]
        tok_mm, tok_done, tok_chain = stage_sem("tok_mm"), stage_sem("tok_done"), stage_sem("tok_chain")

        with nc.Block() as block:
            @block.sync
            def _(sp):
                sp.dma_start(tokw, d["tok_w"]).then_inc(loaded["tok_w"], 16)
                sp.dma_start(tok_b, d["tok_b"]).then_inc(loaded["tok_b"], 16)
                sp.dma_start(cst[:, :], d["cst"]).then_inc(loaded["cst"], 16)
                for n in range(NPX):
                    w = NTOK // NPX
                    sp.dma_start(xp_all[:, :, n * w:(n + 1) * w], d["patches"][:, :, n * w:(n + 1) * w]).then_inc(patches_in[n], 16)
                sp.dma_start(vec[:, :], d["vec"]).then_inc(loaded["vec"], 16)
                sp.dma_start(atw, d["atw"]).then_inc(loaded["atw"], 16)
                sp.dma_start(m0_buf, d["moe0"]).then_inc(loaded["moe0"], 16)
                sp.dma_start(b2_row, d["moe0_b2"]).then_inc(loaded["moe0_b2"], 16)
                sp.dma_start(ssw, d["ssw"]).then_inc(loaded["ssw"], 16)
                sp.dma_start(ring[:, ring_cols - W13:ring_cols], d["moe1_w13"]).then_inc(loaded["moe1_w13"], 16)
                sp.dma_start(m1_w2.rearrange("p e c n -> p (e c n)"), d["moe1_w2"]).then_inc(loaded["moe1_w2"], 16)

            @block.gpsimd
            def _(pool):
                pool.memset(hid[:, :], 0.0).then_inc(zeros, 1)
                pool.wait_ge(zeros, 1)
                for b in range(0, NBLK, NEXP):
                    n = min(NEXP, NBLK - b)
                    pool.dma_start(x_sorted[b * P:(b + n) * P, :].rearrange("(b p) n -> p b n", p=P),
                                   hid[:, 0:n * EMB].rearrange("p (b n) -> p b n", n=EMB)).then_inc(zeroed, 16)
                pool.wait_ge(zeroed, 16 * -(-NBLK // NEXP))

            @block.tensor
            def _(pe):
                for n in ("tok_w", "tok_b", "cst"):
                    pe.wait_ge(loaded[n], 16)
                for i in range(NT):
                    if i % (NT // NPX) == 0:
                        pe.wait_ge(patches_in[i // (NT // NPX)], 16)
                    if i >= 2:
                        pe.wait_ge(tok_done, i - 1)
                    for c in range(NPC):
                        pe.matmul(bank(i % 2, EMB), xp_all[:, c, i * P:(i + 1) * P], tokw[:, c, :],
                                  start=(c == 0), stop=False)
                    pe.matmul(bank(i % 2, EMB), C("ones", 1), tok_b, start=False, stop=True).then_inc(tok_mm, 1)

            @block.vector
            def _(dve):
                link = Chain(dve, tok_chain)
                for i in range(NT):
                    dve.wait_ge(tok_mm, i + 1)
                    dve.tensor_copy(h_new[:, :], bank(i % 2, EMB)).then_inc(tok_done, 1)
                    dve.wait_ge(tok_done, i + 1)
                    row_stats(dve, link, h_new[:, :], i)
                link.sync()

        a = Region(ring, free0, ring_cols - W13)
        xn = a.take(EMB)
        qk_r = a.take(2 * EMB)
        rot_t = a.take(EMB * 2)
        v_sb = [a.take(EMB) for _ in range(2)]
        qT_a, qT_b = a.take(P), a.take(P, EB)
        k_a = a.take(2 * NHA * TOK).rearrange("p (b g k) -> p b g k", b=2, g=NHA)
        k_b = a.take(2 * NHB * TOK, EB).rearrange("p (b g k) -> p b g k", b=2, g=NHB)
        prob = a.take(NH * TOK).rearrange("p (g k) -> p g k", g=NH)
        pT = a.take(NH * P).rearrange("p (g q) -> p g q", g=NH)
        yn = a.take(EMB)
        yT_a, yT_b = a.take(P), a.take(P)
        hmax, hsum, esink, rinv = a.take(NH), a.take(NH), a.take(NH), a.take(NH)

        B_X, B_QK, B_V, B_QKT, B_S, B_PT = 0, 1, 2, 3, 4, 6
        B_Y, B_YT, B_PROJ = 4, 5, 6
        at_chain, at_pre, at_rstd = stage_sem("at_chain"), stage_sem("at_pre"), stage_sem("at_rstd")
        xn_ready, xT_ps, xT_sb, qkv_ps, v_ready, qk_rot, qkT_ps, qk_ready = (
            stage_sem("at_" + n) for n in ("xn", "xT_ps", "xT_sb", "qkv_ps", "v_ready", "qk_rot", "qkT_ps", "qk_ready"))
        q_ready, s_ps, s_sb, p_ready, pT_ps, pT_lo, pT_hi, y_ps, y_ready, yT_ps, yT_sb, pr_ps, h_done, esink_done, sh = (
            stage_sem("at_" + n) for n in ("q_ready", "s_ps", "s_sb", "p_ready", "pT_ps", "pT_lo", "pT_hi", "y_ps", "y_ready",
                                     "yT_ps", "yT_sb", "pr_ps", "h_done", "esink_done", "s_shift"))

        with nc.Block() as block:
            @block.gpsimd
            def _(pool):
                pool.wait_ge(at_pre, 1)
                pool.tensor_tensor(ln_rstd[:, :], ln_tmp[:, :], C("neg_half"), ALU.pow).then_inc(at_rstd, 1)

            @block.tensor
            def _(pe):
                def xT(i):
                    pe.wait_ge(xn_ready, i + 1)
                    pe.transpose(bank(B_X, P), xn[:, 0:P], ident)
                    pe.transpose(bank(B_X, P, P)[0:EB], xn[:, P:EMB], ident).then_inc(xT_ps, 1)

                def qkv(i):
                    pe.wait_ge(xT_sb, i + 1)
                    pe.wait_ge(v_ready, i + 1)
                    for b, n0, n in ((B_QK, 0, 2 * EMB), (B_V, 2 * EMB, EMB)):
                        pe.matmul(bank(b, n), xT_a, W("qkv_a")[:, n0:n0 + n], start=True, stop=False)
                        mm = pe.matmul(bank(b, n), xT_b[0:EB + 1], W("qkv_b", EB + 1)[:, n0:n0 + n], start=False, stop=True)
                    mm.then_inc(qkv_ps, 1)

                def qkT(i):
                    pe.wait_ge(qk_rot, i + 1)
                    pe.transpose(bank(B_QKT, P), qk_r[:, 0:P], ident)
                    pe.transpose(bank(B_QKT, P, P)[0:EB], qk_r[:, P:EMB], ident)
                    pe.transpose(bank(B_QKT, P, 2 * P), qk_r[:, EMB:EMB + P], ident)
                    pe.transpose(bank(B_QKT, P, 3 * P)[0:EB], qk_r[:, EMB + P:2 * EMB], ident).then_inc(qkT_ps, 1)

                def scores(i):
                    pe.wait_ge(q_ready, i + 1)
                    pe.wait_ge(qk_ready, i + 1)
                    for b in range(2):
                        rows = slice(b * TOK, (b + 1) * TOK)
                        pe.matmul(psum[rows, B_S * 512:B_S * 512 + NHA * TOK], qT_a[:, rows],
                                  k_a[:, b].rearrange("p g k -> p (g k)"), start=True, stop=True)
                        mm = pe.matmul(psum[rows, (B_S + 1) * 512:(B_S + 1) * 512 + NHB * TOK], qT_b[:, rows],
                                       k_b[:, b].rearrange("p g k -> p (g k)"), start=True, stop=True)
                    mm.then_inc(s_ps, 1)

                def probs_T(i):
                    pe.wait_ge(p_ready, i + 1)
                    for j in range(NH // 2):
                        tr = pe.transpose(psum[:, B_PT * 512 + j * P:B_PT * 512 + (j + 1) * P],
                                          prob[:, 2 * j:2 * j + 2, :].rearrange("p g k -> p (g k)"), ident)
                    tr.then_inc(pT_ps, 1)

                def attend(i, v):
                    pe.wait_ge(pT_lo, i + 1)
                    pe.wait_ge(pT_hi, i + 1)
                    pe.wait_ge(v_ready, i + 2)
                    for g in range(NH):
                        mm = pe.matmul(bank(B_Y, HD, g * HD), pT[:, g, :], v[:, g * HD:(g + 1) * HD],
                                       start=True, stop=True)
                    mm.then_inc(y_ps, 1)

                def project(i):
                    pe.wait_ge(y_ready, i + 1)
                    pe.transpose(bank(B_YT, P), yn[:, 0:P], ident)
                    pe.transpose(bank(B_YT, P, P)[0:EB], yn[:, P:EMB], ident).then_inc(yT_ps, 1)
                    pe.wait_ge(yT_sb, i + 1)
                    pe.matmul(bank(B_PROJ, EMB), yT_a, W("proj_a"), start=True, stop=False)
                    pe.matmul(bank(B_PROJ, EMB), yT_b[0:EB + 1], W("proj_b", EB + 1), start=False, stop=True).then_inc(pr_ps, 1)

                def turn(i, v, ahead):
                    scores(i)
                    if ahead:
                        xT(i + 1)
                        qkv(i + 1)
                    probs_T(i)
                    attend(i, v)
                    if ahead:
                        qkT(i + 1)
                    project(i)

                for s in (xT_ps, qkv_ps, qkT_ps, s_ps, pT_ps, y_ps):
                    pe.sem_inc(s, 1)
                pe.wait_ge(loaded["atw"], 16)
                xT(0)
                qkv(0)
                qkT(0)
                with pe.Fori(0, NT // 2 - 1) as k:
                    turn(k * 2, v_sb[0], True)
                    turn(k * 2 + 1, v_sb[1], True)
                turn(NT - 2, v_sb[0], True)
                turn(NT - 1, v_sb[1], False)

            @block.scalar
            def _(act):
                def copies_in(i, v):
                    act.wait_ge(qkv_ps, i + 2)
                    act.copy(v, bank(B_V, EMB)).then_inc(v_ready, 1)

                def q_copy(i):
                    act.wait_ge(qkT_ps, i + 2)
                    act.wait_ge(s_ps, i + 1)
                    act.copy(qT_a, bank(B_QKT, P))
                    act.copy(qT_b, bank(B_QKT, P, P)[0:EB]).then_inc(q_ready, 1)

                def softmax(i):
                    act.wait_ge(sh, i + 1)
                    act.activation(esink, hsum, ACT.Exp).then_inc(esink_done, 1)
                    act.activation(prob, prob, ACT.Exp).then_inc(p_ready, 1)

                def pT_copy(i):
                    act.wait_ge(pT_ps, i + 2)
                    act.wait_ge(y_ps, i + 1)
                    src = psum[0:TOK, B_PT * 512:B_PT * 512 + NH // 2 * P].rearrange("p (j q) -> p j q", j=NH // 2)
                    dst = pT.rearrange("p (j two) q -> p j two q", two=2)
                    act.copy(dst[0:TOK, :, 0, 0:TOK], src[:, :, 0:TOK])
                    act.copy(dst[TOK:P, :, 0, TOK:P], src[:, :, TOK:P]).then_inc(pT_lo, 1)

                def yT_copy(i):
                    act.wait_ge(yT_ps, i + 1)
                    act.copy(yT_a, bank(B_YT, P))
                    act.copy(yT_b[0:EB], bank(B_YT, P, P)[0:EB]).then_inc(yT_sb, 1)

                def turn(i, v_next, ahead):
                    softmax(i)
                    if ahead:
                        copies_in(i + 1, v_next)
                    pT_copy(i)
                    if ahead:
                        q_copy(i + 1)
                    yT_copy(i)

                act.preload_act_table(ACT.Exp)
                act.sem_inc(v_ready, 1)
                copies_in(0, v_sb[0])
                q_copy(0)
                with act.Fori(0, NT // 2 - 1) as k:
                    turn(k * 2, v_sb[1], True)
                    turn(k * 2 + 1, v_sb[0], True)
                turn(NT - 2, v_sb[1], True)
                turn(NT - 1, v_sb[0], False)

            @block.vector
            def _(dve):
                link = Chain(dve, at_chain)

                def one2(x, i):
                    return x[:, i:i + 1] if isinstance(i, int) else x[:, bass.ds(i, 1)]

                def norm(i):
                    dve.wait_ge(xT_ps, i + 1)
                    dve.tensor_scalar(xn, one(h, i), one2(ln_mean, i), one2(ln_rstd, i), ALU.subtract, ALU.mult).then_inc(xn_ready, 1)

                def xT_copy(i):
                    dve.wait_ge(xT_ps, i + 2)
                    dve.wait_ge(qkv_ps, i + 1)
                    dve.tensor_scalar(xT_a, bank(B_X, P), V("nscale")[:, 0:1], V("nbias")[:, 0:1], ALU.mult, ALU.add)
                    dve.tensor_scalar(xT_b[0:EB], bank(B_X, P, P)[0:EB], V("nscale", EB)[:, 1:2], V("nbias", EB)[:, 1:2],
                                      ALU.mult, ALU.add).then_inc(xT_sb, 1)

                def rotate(i):
                    dve.wait_ge(qkv_ps, i + 2)
                    dve.wait_ge(qkT_ps, i + 1)
                    g = 2 * NH
                    x = bank(B_QK, 2 * EMB).rearrange("p (g j two) -> p g j two", g=g, two=2)
                    full = bank(B_QK, 2 * EMB).rearrange("p (g f) -> p g f", g=g)
                    t4 = rot_t.rearrange("p (g j two) -> p g j two", g=g, two=2)
                    cos = C("cos2").unsqueeze(1).to_broadcast([P, g, HD])
                    sin = C("sin").unsqueeze(1).to_broadcast([P, g, HD // 2])
                    nsin = C("nsin").unsqueeze(1).to_broadcast([P, g, HD // 2])
                    r = qk_r.rearrange("p (g f) -> p g f", g=g)
                    link(dve.tensor_tensor(r, full, cos, ALU.mult))
                    link(dve.tensor_tensor(t4[:, :, :, 0], x[:, :, :, 1], nsin, ALU.mult))
                    link(dve.tensor_tensor(t4[:, :, :, 1], x[:, :, :, 0], sin, ALU.mult))
                    link.sync()
                    dve.tensor_tensor(qk_r, qk_r, rot_t, ALU.add).then_inc(qk_rot, 1)

                def k_spread(i):
                    dve.wait_ge(q_ready, i + 1)
                    for dst, src, n, rows in ((k_a, bank(B_QKT, P, 2 * P), NHA, P), (k_b, bank(B_QKT, P, 3 * P)[0:EB], NHB, EB)):
                        s = src.rearrange("p (b k) -> p b k", b=2).unsqueeze(2).to_broadcast([rows, 2, n, TOK])
                        w = C("kmask", rows)[:, 0:n].unsqueeze(1).unsqueeze(3).to_broadcast([rows, 2, n, TOK])
                        ins = dve.tensor_tensor(dst, s, w, ALU.mult)
                    ins.then_inc(qk_ready, 1)

                def softmax(i):
                    dve.wait_ge(s_ps, i + 2)
                    dve.wait_ge(pT_ps, i + 1)
                    s = psum[:, B_S * 512:B_S * 512 + NH * TOK].rearrange("p (g k) -> p g k", g=NH)
                    mask = C("causal").unsqueeze(1).to_broadcast([P, NH, TOK])
                    link(dve.tensor_tensor(prob, s, mask, ALU.add))
                    link.sync()
                    link(dve.tensor_reduce(hmax, prob, AX, ALU.max))
                    link.sync()
                    link(dve.tensor_tensor(hmax, hmax, V("sinks"), ALU.max))
                    link.sync()
                    link(dve.tensor_tensor(hsum, V("sinks"), hmax, ALU.subtract))
                    dve.tensor_tensor(prob, prob, hmax.unsqueeze(2).to_broadcast([P, NH, TOK]), ALU.subtract).then_inc(sh, 1)

                def pT_copy(i):
                    dve.wait_ge(pT_ps, i + 2)
                    dve.wait_ge(y_ps, i + 1)
                    src = psum[TOK:P, B_PT * 512:B_PT * 512 + NH // 2 * P].rearrange("p (j q) -> p j q", j=NH // 2)
                    dst = pT.rearrange("p (j two) q -> p j two q", two=2)
                    dve.tensor_copy(dst[0:TOK, :, 1, 0:TOK], src[:, :, 0:TOK])
                    dve.tensor_copy(dst[TOK:P, :, 1, TOK:P], src[:, :, TOK:P]).then_inc(pT_hi, 1)

                def sums(i):
                    dve.wait_ge(p_ready, i + 1)
                    link(dve.tensor_reduce(hsum, prob, AX, ALU.add))
                    link.sync()
                    link(dve.tensor_tensor(hsum, hsum, esink, ALU.add))
                    link.sync()
                    link(dve.reciprocal(rinv, hsum))
                    link.sync()

                def y_norm(i):
                    dve.wait_ge(y_ps, i + 2)
                    dve.tensor_tensor(yn.rearrange("p (g f) -> p g f", g=NH), bank(B_Y, EMB).rearrange("p (g f) -> p g f", g=NH),
                                      rinv.unsqueeze(2).to_broadcast([P, NH, HD]), ALU.mult).then_inc(y_ready, 1)

                def residual(i):
                    dve.wait_ge(pr_ps, i + 1)
                    link(dve.scalar_tensor_tensor(out=h_new[:, :], in0=bank(B_PROJ, EMB), scalar=V("rezero"), in1=one(h, i),
                                                  op0=ALU.mult, op1=ALU.add))
                    link.sync()
                    row_stats(dve, link, h_new[:, :], i)

                def turn(i, ahead):
                    softmax(i)
                    if ahead:
                        norm(i + 1)
                        xT_copy(i + 1)
                    sums(i)
                    pT_copy(i)
                    if ahead:
                        rotate(i + 1)
                        k_spread(i + 1)
                    y_norm(i)
                    residual(i)

                dve.wait_ge(loaded["vec"], 16)
                link(dve.memset(pT, 0.0))
                link(dve.memset(xT_b[EB:EB + 1], 1.0))
                link(dve.memset(yT_b[EB:EB + 1], 1.0))
                ln_scalars(dve, link, None)
                dve.sem_inc(at_pre, 1)
                dve.wait_ge(at_rstd, 1)
                norm(0)
                xT_copy(0)
                rotate(0)
                k_spread(0)
                per = 2 * (3 + 4 + 3 + 5)
                with dve.Fori(0, NT // 2 - 1) as k:
                    link.turn(k, per)
                    turn(k * 2, True)
                    turn(k * 2 + 1, True)
                link.turns(NT // 2 - 1, per)
                turn(NT - 2, True)
                turn(NT - 1, False)
                link.sync()

        def top1_moe(name, src, sub, x_col, gate_w, gate_rows, up, up_rows, down_w, act_fn, gated, u, buf,
                     weights_in, also_sync=None):
            def s(n):
                return stage_sem(f"{name}_{n}")

            reg = Region(*buf)
            xn_all = reg.take(NT * EMB).rearrange("p (i n) -> p i n", i=NT)
            xb_all = reg.take(NBLK * EMB).rearrange("p (b n) -> p b n", b=NBLK)
            nk = len(up)
            xTs = [(xT_a, xT_b), (hid[:, 0:P], hid[:, P:2 * P])]
            x_cur = hid2[:, 0:EMB]
            B_L, B_RANK, B_TOT = 2, 4, 5
            B_H1, B_H3, B_HT, B_Y, B_XT = 0, 2, 4, 6, 7
            chain, pre, rstd, xn_rdy, xT_ps, xT_sb, lg_ps, lg_sb, oh_rdy, rank_ps, route_rdy = (
                s(n) for n in ("chain", "pre", "rstd", "xn", "xT_ps", "xT_sb", "lg_ps", "lg_sb", "onehot", "rank_ps", "routed"))
            scat, sorted_in, cur_rdy, bT_ps, bT_sb, up_ps, hid_rdy, hT_ps, hT_v, hT_a, y_ps, y_rdy, y_st, ex_in, ex_out = (
                s(n) for n in ("scattered", "sorted_in", "cur", "bT_ps", "bT_sb", "up_ps", "hid", "hT_ps", "hT_v", "hT_a",
                               "y_ps", "y_rdy", "y_stored", "exp_in", "exp_out"))
            act_rdy = s("act_rdy")
            gath = [s(f"gathered{i}") for i in range(NT)]
            nL = gate_rows

            with nc.Block() as block:
                @block.sync
                def _(sp):
                    if also_sync:
                        also_sync(sp)
                    sp.wait_ge(scat, 16 * NT)
                    sp.dma_start(xb_all, x_sorted.rearrange("(b p) n -> p b n", p=P)).then_inc(sorted_in, 16)
                    with sp.Fori(0, NBLK) as j:
                        sp.wait_ge(y_rdy, j + 2)
                        sp.dma_start(y_sorted[bass.ds(j * P, P), :], one(xb_all, j)).then_inc(y_st, 16)

                @block.gpsimd
                def _(pool):
                    pool.wait_ge(pre, 1)
                    pool.tensor_tensor(row_scale[:, :], ln_tmp[:, :], C("neg_half"), ALU.pow).then_inc(rstd, 1)
                    pool.wait_ge(zeroed, 16 * -(-NBLK // NEXP))
                    pool.wait_ge(route_rdy, 1)
                    for i in range(NT):
                        pool.indirect_dma_start(x_sorted, bass.IndirectOffsetOnAxis(ap=slot_u[:, i:i + 1], axis=0),
                                                xn_all[:, i, :], None).then_inc(scat, 16)
                    pool.wait_ge(y_st, 16 * NBLK)
                    for i in range(NT):
                        pool.indirect_dma_start(xn_all[:, i, :], None, y_sorted,
                                                bass.IndirectOffsetOnAxis(ap=slot_u[:, i:i + 1], axis=0)).then_inc(gath[i], 16)

                @block.tensor
                def _(pe):
                    for i in range(NT):
                        a_, b_ = xTs[i % 2]
                        pe.wait_ge(xn_rdy, i + 1)
                        pe.transpose(bank(i % 2, P), xn_all[:, i, 0:P], ident)
                        pe.transpose(bank(i % 2, P, P)[0:EB], xn_all[:, i, P:EMB], ident).then_inc(xT_ps, 1)
                        pe.wait_ge(xT_sb, i + 1)
                        if i >= 2:
                            pe.wait_ge(lg_sb, i - 1)
                        pe.matmul(bank(B_L + i % 2, NEXP), a_, W(gate_w + "_a"), start=True, stop=False)
                        pe.matmul(bank(B_L + i % 2, NEXP), b_[0:nL], W(gate_w + "_b", nL), start=False, stop=True).then_inc(lg_ps, 1)
                    pe.wait_ge(oh_rdy, 1)
                    oh_et = oh.rearrange("p (t e) -> p e t", e=NEXP)
                    pe.matmul(bank(B_RANK, NEXP * NT), C("upper"), oh_et, start=True, stop=True)
                    pe.matmul(bank(B_TOT, NEXP * NT), C("ones"), oh_et, start=True, stop=True).then_inc(rank_ps, 1)

                    def expert(j):
                        return pe.value_load(eid[0:1, j:j + 1] if isinstance(j, int) else eid[0:1, bass.ds(j, 1)],
                                             min_val=0, max_val=NEXP - 1)

                    def rows_T(j):
                        pe.wait_ge(cur_rdy, j + 1)
                        pe.wait_ge(bT_sb, j + 1)
                        pe.transpose(bank(B_XT, P), x_cur[:, 0:P], ident)
                        pe.transpose(bank(B_XT, P, P)[0:EB], x_cur[:, P:EMB], ident).then_inc(bT_ps, 1)

                    def up_proj(j):
                        e = expert(j)
                        pe.wait_ge(bT_sb, j + 2)
                        pe.wait_ge(hid_rdy, j + 1)
                        for k, (wa, wb) in enumerate(up):
                            for n0, n in ((0, 512), (512, 256)):
                                o = psum[:, (B_H1, B_H3)[k] * 512 + n0:(B_H1, B_H3)[k] * 512 + n0 + n]
                                pe.matmul(o, xT_a, one(wa, e)[:, n0:n0 + n], start=True, stop=False)
                                mm = pe.matmul(o, xT_b[0:up_rows], one(wb, e)[:, n0:n0 + n], start=False, stop=True)
                        mm.then_inc(up_ps, 1)

                    def hidden_T(j):
                        pe.wait_ge(hid_rdy, j + 2)
                        for c in range(NFC):
                            tr = pe.transpose(psum[:, B_HT * 512 + c * P:B_HT * 512 + (c + 1) * P], hid[:, c * P:(c + 1) * P], ident)
                        tr.then_inc(hT_ps, 1)

                    def down_proj(j):
                        e = expert(j)
                        pe.wait_ge(hT_v, j + 1)
                        pe.wait_ge(hT_a, j + 1)
                        pe.wait_ge(y_rdy, j + 1)
                        if not gated:
                            pe.matmul(bank(B_Y, EMB), C("ones", 1), one(b2_row.rearrange("p (e n) -> p e n", e=NEXP), e),
                                      start=True, stop=False)
                        w2 = down_w[:, bass.ds(e, 1)].rearrange("p o c n -> p (o c) n")
                        for c in range(NFC):
                            mm = pe.matmul(bank(B_Y, EMB), hidT[:, c * P:(c + 1) * P], w2[:, c, :],
                                           start=(gated and c == 0), stop=(c == NFC - 1))
                        mm.then_inc(y_ps, 1)

                    pe.sem_inc(bT_ps, 1)
                    pe.sem_inc(up_ps, 1)
                    pe.sem_inc(hT_ps, 1)
                    pe.sem_inc(y_ps, 1)
                    rows_T(0)
                    for n in weights_in:
                        pe.wait_ge(loaded[n], 16)
                    up_proj(0)
                    rows_T(1)
                    hidden_T(0)
                    with pe.Fori(1, NBLK - 1) as j:
                        up_proj(j)
                        rows_T(j + 1)
                        down_proj(j - 1)
                        hidden_T(j)
                    up_proj(NBLK - 1)
                    down_proj(NBLK - 2)
                    hidden_T(NBLK - 1)
                    down_proj(NBLK - 1)

                @block.scalar
                def _(act):
                    def hidden(j):
                        act.wait_ge(up_ps, j + 2)
                        act.wait_ge(hT_ps, j + 1)
                        f = act.activation(hid, psum[:, B_H1 * 512:B_H1 * 512 + HID], act_fn)
                        f.then_inc(act_rdy if gated else hid_rdy, 1)

                    def hT_copy(j):
                        act.wait_ge(hT_ps, j + 2)
                        act.wait_ge(y_ps, j + 1)
                        act.copy(hidT[:, 512:HID], psum[:, (B_HT + 1) * 512:(B_HT + 1) * 512 + HID - 512]).then_inc(hT_a, 1)

                    if gated:
                        act.wait_ge(ex_in, 1)
                        act.activation(rt[0], rt[0], ACT.Exp).then_inc(ex_out, 1)
                    act.preload_act_table(act_fn)
                    if not gated:
                        act.sem_inc(hid_rdy, 1)
                    with act.Fori(0, NBLK) as j:
                        hidden(j)
                        hT_copy(j)

                @block.vector
                def _(dve):
                    link = Chain(dve, chain)

                    def te(x):
                        return x.rearrange("p (t e) -> p t e", e=NEXP)

                    def et(x):
                        return x.rearrange("p (e t) -> p e t", e=NEXP)

                    def over_e(x):
                        return x.unsqueeze(2).to_broadcast([P, NT, NEXP])

                    def over_t(x):
                        return x.unsqueeze(1).to_broadcast([P, NT, NEXP])

                    if sub is not None:
                        link(dve.tensor_scalar(ln_tmp[:, :], stats[:, :, 1], LN_EPS, None, ALU.add))
                        link(dve.tensor_copy(ln_mean[:, :], stats[:, :, 0]))
                    else:
                        link(dve.tensor_tensor(ln_tmp[:, :], stats[:, :, 0], stats[:, :, 0], ALU.mult))
                        link.sync()
                        link(dve.scalar_tensor_tensor(out=ln_tmp[:, :], in0=ln_tmp[:, :], scalar=RMS_EPS, in1=stats[:, :, 1],
                                                      op0=ALU.add, op1=ALU.add))
                    link(dve.memset(xT_b[EB:EB + 1], 1.0))
                    link(dve.memset(hid[EB:EB + 1, P:2 * P], 1.0))
                    link.sync()
                    dve.sem_inc(pre, 1)
                    dve.wait_ge(rstd, 1)
                    for i in range(NT + 1):
                        if i < NT:
                            if sub is not None:
                                dve.tensor_scalar(xn_all[:, i, :], src[:, i, :], sub[:, i:i + 1], row_scale[:, i:i + 1],
                                                  ALU.subtract, ALU.mult).then_inc(xn_rdy, 1)
                            else:
                                dve.tensor_scalar(xn_all[:, i, :], src[:, i, :], row_scale[:, i:i + 1], None,
                                                  ALU.mult).then_inc(xn_rdy, 1)
                        if i > 0:
                            dve.wait_ge(lg_ps, i)
                            dve.tensor_copy(te(logits)[:, i - 1, :], bank(B_L + (i - 1) % 2, NEXP)).then_inc(lg_sb, 1)
                        if i < NT:
                            a_, b_ = xTs[i % 2]
                            dve.wait_ge(xT_ps, i + 1)
                            if x_col is None:
                                dve.tensor_copy(a_, bank(i % 2, P))
                                dve.tensor_copy(b_[0:EB], bank(i % 2, P, P)[0:EB]).then_inc(xT_sb, 1)
                            else:
                                dve.tensor_scalar(a_, bank(i % 2, P), x_col[:, 0:1], None, ALU.mult)
                                dve.tensor_scalar(b_[0:EB], bank(i % 2, P, P)[0:EB], x_col[0:EB, 1:2], None, ALU.mult).then_inc(xT_sb, 1)
                    dve.wait_ge(lg_sb, NT)
                    v = logits
                    if gated:
                        link(dve.tensor_reduce(mx, te(logits), AX, ALU.max))
                        link.sync()
                        dve.tensor_tensor(te(rt[0]), te(logits), over_e(mx), ALU.subtract).then_inc(ex_in, 1)
                        dve.wait_ge(ex_out, 1)
                        v = rt[0]
                        link(dve.tensor_reduce(gate, te(v), AX, ALU.add))
                        link.sync()
                        link(dve.reciprocal(gate, gate))
                    link(dve.tensor_reduce(mx, te(v), AX, ALU.max))
                    link.sync()
                    if gated:
                        link(dve.tensor_tensor(gate, gate, mx, ALU.mult))
                    link(dve.tensor_tensor(te(rt[1]), te(v), over_e(mx), ALU.is_ge))
                    link.sync()
                    link(dve.scalar_tensor_tensor(out=te(rt[1]), in0=te(rt[1]), scalar=-1000.0, in1=over_t(C("iota_far")),
                                                  op0=ALU.mult, op1=ALU.add))
                    link.sync()
                    link(dve.tensor_reduce(mx, te(rt[1]), AX, ALU.min))
                    link.sync()
                    dve.tensor_tensor(te(oh), over_t(C("iota")), over_e(mx), ALU.is_equal).then_inc(oh_rdy, 1)
                    dve.wait_ge(rank_ps, 1)
                    link(dve.tensor_tensor_scan(rt[0], C("carry"), bank(B_TOT, NEXP * NT), 0.0, ALU.mult, ALU.add))
                    link.sync()
                    link(dve.tensor_tensor(rt[1], rt[0], bank(B_TOT, NEXP * NT), ALU.subtract))
                    link(dve.tensor_tensor(et(rt[2]), et(rt[0])[:, :, NT - 1:NT].to_broadcast([P, NEXP, NT]),
                                           C("by128").unsqueeze(1).to_broadcast([P, NEXP, NT]), ALU.is_gt))
                    link.sync()
                    link(dve.tensor_reduce(blkc, et(rt[2]), AX, ALU.add))
                    link(dve.memset(sb_, 0.0))
                    link.sync()
                    link(dve.tensor_tensor_scan(sb_[:, 1:NEXP + 1], C("ones")[:, 0:NEXP], blkc, 0.0, ALU.mult, ALU.add))
                    link.sync()
                    link(dve.scalar_tensor_tensor(out=et(rt[2]), in0=sb_[:, 0:NEXP].unsqueeze(2).to_broadcast([P, NEXP, NT]),
                                                  scalar=float(P), in1=et(rt[1]), op0=ALU.mult, op1=ALU.add))
                    bl3 = bl.rearrange("p (b e) -> p b e", e=NEXP)[:, :, 1:NEXP]
                    link(dve.tensor_tensor(bl3, C("block").unsqueeze(2).to_broadcast([P, NBLK, NEXP - 1]),
                                           sb_[:, 1:NEXP].unsqueeze(1).to_broadcast([P, NBLK, NEXP - 1]), ALU.is_ge))
                    link.sync()
                    link(dve.tensor_tensor(rt[2], rt[2], bank(B_RANK, NEXP * NT), ALU.add))
                    link(dve.tensor_reduce(eidf, bl3, AX, ALU.add))
                    link.sync()
                    link(dve.tensor_tensor(et(rt[2]), et(rt[2]), oh.rearrange("p (t e) -> p e t", e=NEXP), ALU.mult))
                    link(dve.tensor_copy(eid[:, :], eidf))
                    link.sync()
                    link(dve.tensor_reduce(slotf, rt[2].rearrange("p (e t) -> p t e", e=NEXP), AX, ALU.add))
                    link.sync()
                    link(dve.tensor_copy(slot_u[:, :], slotf))
                    link.sync()
                    dve.sem_inc(route_rdy, 1)

                    def take_rows(j):
                        dve.wait_ge(bT_ps, j + 1)
                        dve.tensor_scalar(x_cur, one(xb_all, j), 1.0, None, ALU.mult).then_inc(cur_rdy, 1)

                    def rows_T(j):
                        dve.wait_ge(bT_ps, j + 2)
                        dve.wait_ge(up_ps, j + 1)
                        if x_col is None:
                            dve.tensor_copy(xT_a, bank(B_XT, P))
                            dve.tensor_copy(xT_b[0:EB], bank(B_XT, P, P)[0:EB]).then_inc(bT_sb, 1)
                        else:
                            dve.tensor_scalar(xT_a, bank(B_XT, P), x_col[:, 0:1], None, ALU.mult)
                            dve.tensor_scalar(xT_b[0:EB], bank(B_XT, P, P)[0:EB], x_col[0:EB, 1:2], None, ALU.mult).then_inc(bT_sb, 1)

                    def hidden(j):
                        if gated:
                            dve.wait_ge(act_rdy, j + 1)
                            dve.tensor_tensor(hid, hid, psum[:, B_H3 * 512:B_H3 * 512 + HID], ALU.mult).then_inc(hid_rdy, 1)

                    def hT_copy(j):
                        dve.wait_ge(hT_ps, j + 2)
                        dve.wait_ge(y_ps, j + 1)
                        dve.tensor_copy(hidT[:, 0:512], bank(B_HT)).then_inc(hT_v, 1)

                    def result(j):
                        dve.wait_ge(y_ps, j + 2)
                        dve.tensor_scalar(one(xb_all, j), bank(B_Y, EMB), 1.0, None, ALU.mult).then_inc(y_rdy, 1)

                    dve.sem_inc(bT_sb, 1)
                    dve.sem_inc(y_rdy, 1)
                    if gated:
                        dve.sem_inc(hid_rdy, 1)
                    dve.wait_ge(sorted_in, 16)
                    take_rows(0)
                    rows_T(0)
                    take_rows(1)
                    hidden(0)
                    rows_T(1)
                    hT_copy(0)
                    with dve.Fori(1, NBLK - 1) as j:
                        take_rows(j + 1)
                        hidden(j)
                        rows_T(j + 1)
                        result(j - 1)
                        hT_copy(j)
                    hidden(NBLK - 1)
                    result(NBLK - 2)
                    hT_copy(NBLK - 1)
                    result(NBLK - 1)
                    for i in range(NT):
                        dve.wait_ge(gath[i], 16)
                        if gated:
                            link(dve.scalar_tensor_tensor(out=xn_all[:, i, :], in0=xn_all[:, i, :], scalar=gate[:, i:i + 1],
                                                          in1=V("ls_ffn"), op0=ALU.mult, op1=ALU.mult))
                            link(dve.tensor_tensor(h_new[:, :], h[:, i, :], u[:, i, :], ALU.add))
                            link.sync()
                            link(dve.tensor_tensor(h_new[:, :], h_new[:, :], xn_all[:, i, :], ALU.add))
                        else:
                            link(dve.tensor_tensor(h_new[:, :], h[:, i, :], xn_all[:, i, :], ALU.add))
                        link.sync()
                        row_stats(dve, link, h_new[:, :], i)
                    link.sync()

        a = Region(ring, free0, ring_cols - W13)
        top1_moe("m0", h, ln_mean, None, "g0", EB + 1, [(m0_w1a, m0_w1b)], EB + 1, m0_w2, ACT.Gelu, False, None,
                 (ring, free0, ring_cols - W13), ("moe0", "moe0_b2"))
        new_sems()

        a = Region(ring, 0, 5 * PAIR_W)
        u_all = ring[:, 5 * PAIR_W:5 * PAIR_W + NT * EMB].rearrange("p (i n) -> p i n", i=NT)
        assert 5 * PAIR_W + NT * EMB <= ring_cols - W13
        in_T = a.take(2 * NTOK)
        xnT_a, xnT_b = in_T[:, 0:NTOK], in_T[0:EB, NTOK:2 * NTOK]
        dBu = [in_T[:, c * HALF:(c + 1) * HALF] for c in range(NCH)]
        xc = a.take(NCH * NTOK).rearrange("p (c t) -> p c t", c=NCH)
        z = a.take(NCH * NTOK).rearrange("p (c t) -> p c t", c=NCH)
        delta = a.take(NCH * NTOK).rearrange("p (c t) -> p c t", c=NCH)
        du = a.take(NCH * NTOK).rearrange("p (c t) -> p c t", c=NCH)
        hc_buf = a.take(NCH * HALF)
        dt_sb = hc_buf[0:DTR, 0:NTOK]
        hc = [hc_buf[:, c * HALF:(c + 1) * HALF] for c in range(NCH)]
        hs_buf = a.take(NCH * HALF)
        sp_t = [hs_buf[:, c * HALF:(c + 1) * HALF] for c in range(2)]
        hs = [hs_buf[:, c * HALF:(c + 1) * HALF] for c in range(NCH)]
        b_buf = a.take(2 * HALF)
        sp_r = [b_buf[:, c * HALF:(c + 1) * HALF] for c in range(2)]
        b_sb = [b_buf[:, c * HALF:(c + 1) * HALF] for c in range(2)]
        bc3 = a.take(HALF, XPJ).bitcast(BF16)
        sel = a.take(2 * NST * P // 2, XPJ).bitcast(BF16).rearrange("p (s m) -> p s m", s=2 * NST)
        neg_A = a.take(NCH * NST)
        diag_D = a.take(NCH * P).rearrange("p (c m) -> p c m", c=NCH)
        bc_r = hid[:, 0:HALF]
        xn2 = [yn2[:, 0:EMB] for yn2 in (hidT[:, 0:EMB], hidT[:, EMB:2 * EMB])]

        def s(n):
            return stage_sem("ss_" + n)

        A_exp = sem("A_exp")
        (sel_in, chain, pre, pw, xn_rdy, xT_ps, xT_sb, xs_ps, xs_rd, z_ps, z_rd, cv_rdy, xc_rdy, bc_ps, bc_rd, dt_ps, ab_rd, l_rdy,
         dt_rd) = (s(n) for n in ("sel_in", "chain", "pre", "pow", "xn", "xT_ps", "xT_sb", "xs_ps", "xs_read", "z_ps", "z_read",
                                  "conv", "xc", "bc_ps", "bc_read", "dt_ps", "abs_read", "log_ready", "dt_read"))

        with nc.Block() as block:
            @block.sync
            def _(sp):
                sp.dma_start(sel.bitcast(U16), d["sel"]).then_inc(sel_in, 16)
                sp.wait_ge(sel_in, 16)

            @block.gpsimd
            def _(pool):
                pool.wait_ge(pre, 1)
                pool.tensor_tensor(ln_rstd[:, :], ln_tmp[:, :], C("neg_half"), ALU.pow).then_inc(pw, 1)
                pool.wait_ge(pre, 2)
                pool.tensor_tensor(row_scale[:, :], ln_tmp[:, :], C("neg_half"), ALU.pow).then_inc(pw, 1)

            @block.tensor
            def _(pe):
                for i in range(NT):
                    pe.wait_ge(xn_rdy, i + 1)
                    if i >= 2:
                        pe.wait_ge(xT_sb, i - 1)
                    pe.transpose(bank(i % 2, P), xn2[i % 2][:, 0:P], ident)
                    pe.transpose(bank(i % 2, P, P)[0:EB], xn2[i % 2][:, P:EMB], ident).then_inc(xT_ps, 1)
                pe.wait_ge(xT_sb, NT)
                pe.wait_ge(loaded["ssw"], 16)
                n = 0
                for c in range(NCH):
                    for hf in range(2):
                        for k, ps, rd in ((0, xs_ps, xs_rd), (1, z_ps, z_rd)):
                            if n >= 2:
                                pe.wait_ge(rd, n - 1)
                            o = bank(2 + 2 * k + n % 2)
                            w0 = (k * NCH + c) * P
                            t = slice(hf * HALF, (hf + 1) * HALF)
                            pe.matmul(o, WS("in_a")[:, w0:w0 + P], xnT_a[:, t], start=True, stop=False)
                            pe.matmul(o, WS("in_b", EB)[:, w0:w0 + P], xnT_b[:, t], start=False, stop=True).then_inc(ps, 1)
                        n += 1
                pe.wait_ge(xc_rdy, 2 * NCH)
                for hf in range(2):
                    for c in range(NCH):
                        mm = pe.matmul(bank(6 + hf)[0:XPJ], WS("x")[:, c * XPJ:(c + 1) * XPJ], xc[:, c, hf * HALF:(hf + 1) * HALF],
                                       start=(c == 0), stop=(c == NCH - 1))
                    mm.then_inc(bc_ps, 1)
                n = 0
                for hf in range(2):
                    pe.wait_ge(bc_rd, hf + 1)
                    for c in range(NCH):
                        if n >= 2:
                            pe.wait_ge(dt_rd, n - 1)
                        pe.matmul(bank(n % 2), WS("dt", DTR)[:, c * P:(c + 1) * P], dt_sb[:, hf * HALF:(hf + 1) * HALF],
                                  start=True, stop=True).then_inc(dt_ps, 1)
                        n += 1

            @block.scalar
            def _(act):
                act.activation(neg_A, V("A_log"), ACT.Exp).then_inc(A_exp, 1)
                n = 0
                for c in range(NCH):
                    for hf in range(2):
                        t = slice(hf * HALF, (hf + 1) * HALF)
                        act.wait_ge(z_ps, n + 1)
                        act.activation(z[:, c, t], bank(4 + n % 2), ACT.Silu).then_inc(z_rd, 1)
                        act.wait_ge(cv_rdy, n + 1)
                        act.activation(xc[:, c, t], xc[:, c, t], ACT.Silu).then_inc(xc_rdy, 1)
                        n += 1
                act.preload_act_table_set("natural_log_exp_and_others")
                n = 0
                for hf in range(2):
                    for c in range(NCH):
                        act.wait_ge(dt_ps, n + 1)
                        if n >= 2:
                            act.wait_ge(dt_rd, n - 1)
                        b = sp_t[n % 2]
                        act.activation(b, bank(n % 2), ACT.Abs, bias=V("dt_b")[:, c:c + 1]).then_inc(ab_rd, 1)
                        act.wait_ge(ab_rd, 3 * n + 1)
                        act.activation(b, b, ACT.Exp, scale=-1.0).then_inc(ab_rd, 1)
                        act.wait_ge(ab_rd, 3 * n + 2)
                        act.activation(b, b, ACT.Ln, bias=1.0).then_inc(ab_rd, 1)
                        n += 1

            @block.vector
            def _(dve):
                link = Chain(dve, chain)
                ln_scalars(dve, link, None)
                dve.sem_inc(pre, 1)
                dve.wait_ge(pw, 1)
                link(dve.tensor_tensor(ln_tmp[:, :], ln_rstd[:, :], ln_rstd[:, :], ALU.mult))
                link.sync()
                link(dve.tensor_tensor(ln_tmp[:, :], ln_tmp[:, :], stats[:, :, 1], ALU.mult))
                link.sync()
                link(dve.tensor_scalar(ln_tmp[:, :], ln_tmp[:, :], RMS_EPS, None, ALU.add))
                link.sync()
                dve.sem_inc(pre, 1)
                dve.wait_ge(pw, 2)
                link(dve.tensor_tensor(row_scale[:, :], row_scale[:, :], ln_rstd[:, :], ALU.mult))
                link.sync()
                for i in range(NT + 1):
                    if i < NT:
                        if i >= 2:
                            dve.wait_ge(xT_ps, i - 1)
                        dve.tensor_scalar(xn2[i % 2], h[:, i, :], ln_mean[:, i:i + 1], row_scale[:, i:i + 1],
                                          ALU.subtract, ALU.mult).then_inc(xn_rdy, 1)
                    if i > 0:
                        j = i - 1
                        dve.wait_ge(xT_ps, j + 1)
                        dve.tensor_scalar(xnT_a[:, j * P:(j + 1) * P], bank(j % 2, P), V("norm1")[:, 0:1], None, ALU.mult)
                        dve.tensor_scalar(xnT_b[:, j * P:(j + 1) * P], bank(j % 2, P, P)[0:EB], V("norm1", EB)[:, 1:2], None,
                                          ALU.mult).then_inc(xT_sb, 1)
                dve.wait_ge(A_exp, 1)
                link(dve.tensor_scalar(neg_A, neg_A, -1.0, None, ALU.mult))
                for c in range(NCH):
                    link(dve.tensor_scalar(diag_D[:, c, :], ident, V("D")[:, c:c + 1], None, ALU.mult))
                n = 0
                for c in range(NCH):
                    for hf in range(2):
                        o = xc[:, c, hf * HALF:(hf + 1) * HALF]
                        x3 = bank(2 + n % 2).rearrange("p (b t) -> p b t", t=TOK)
                        o3 = o.rearrange("p (b t) -> p b t", t=TOK)
                        dve.wait_ge(xs_ps, n + 1)
                        link(dve.tensor_scalar(o, bank(2 + n % 2), V("conv_w")[:, 4 * c + 3:4 * c + 4], V("conv_b")[:, c:c + 1],
                                               ALU.mult, ALU.add))
                        for k in (2, 1, 0):
                            link.sync()
                            lag = 3 - k
                            ins = link(dve.scalar_tensor_tensor(
                                out=o3[:, :, lag:TOK], in0=x3[:, :, 0:TOK - lag], scalar=V("conv_w")[:, 4 * c + k:4 * c + k + 1],
                                in1=o3[:, :, lag:TOK], op0=ALU.mult, op1=ALU.add))
                        link.sync()
                        dve.sem_inc(xs_rd, 1)
                        dve.sem_inc(cv_rdy, 1)
                        n += 1
                for hf in range(2):
                    t = slice(hf * HALF, (hf + 1) * HALF)
                    dve.wait_ge(bc_ps, hf + 1)
                    link(dve.tensor_copy(dt_sb[:, t], bank(6 + hf)[0:DTR]))
                    bc = bank(6 + hf)[BC0:BC0 + 2 * NST]
                    n2 = 2 * NST
                    link(dve.tensor_copy(bc3[0:n2, t], bc))
                    link.sync()
                    link(dve.tensor_tensor(bc_r[n2:2 * n2], bc, bc3[0:n2, t], ALU.subtract))
                    link.sync()
                    link(dve.tensor_copy(bc3[n2:2 * n2, t], bc_r[n2:2 * n2]))
                    link.sync()
                    link(dve.tensor_tensor(bc3[2 * n2:3 * n2, t], bc_r[n2:2 * n2], bc3[n2:2 * n2, t], ALU.subtract))
                    link.sync()
                    dve.sem_inc(bc_rd, 1)
                n = 0
                for hf in range(2):
                    for c in range(NCH):
                        t = slice(hf * HALF, (hf + 1) * HALF)
                        dve.wait_ge(ab_rd, 3 * n + 1)
                        r = sp_r[n % 2]
                        link(dve.tensor_scalar(r, bank(n % 2), V("dt_b")[:, c:c + 1], 0.0, ALU.add, ALU.max))
                        dve.wait_ge(ab_rd, 3 * n + 3)
                        link.sync()
                        link(dve.tensor_tensor(delta[:, c, t], r, sp_t[n % 2], ALU.add))
                        link.sync()
                        dve.tensor_tensor(du[:, c, t], delta[:, c, t], xc[:, c, t], ALU.mult).then_inc(dt_rd, 1)
                        n += 1

        B_DA, B_C, B_B = 3, 5, 7
        (zero_cols, b_ps, b_rd, c_ps, dA_rdy, dBu_rdy, scan_rdy, hc_rdy, y_acc, y_rd) = (
            s(n) for n in ("zero_cols", "b_ps", "b_read", "c_ps", "dA", "dBu", "scan", "hc", "y_acc", "y_read"))
        U = NCH * NST

        with nc.Block() as block:
            @block.tensor
            def _(pe):
                def spread(s_, hf, odd):
                    t = slice(hf * HALF, (hf + 1) * HALF)
                    n = hf * NST
                    pe.wait_ge(b_rd, s_ + n + 1)
                    w = sel[:, bass.ds(s_, 1), :] if not isinstance(s_, int) else sel[:, s_:s_ + 1, :]
                    pe.matmul(bank(B_B), w.rearrange("p o m -> p (o m)"), bc3[:, t], start=True, stop=True).then_inc(b_ps, 1)
                    pe.wait_ge(hc_rdy, (s_ + n) * NCH + 3)
                    w = sel[:, bass.ds(s_ + NST, 1), :] if not isinstance(s_, int) else sel[:, s_ + NST:s_ + NST + 1, :]
                    pe.matmul(bank(B_C + odd), w.rearrange("p o m -> p (o m)"), bc3[:, t], start=True, stop=True).then_inc(c_ps, 1)

                def add_up(s_, hf):
                    for c in range(NCH):
                        pe.wait_ge(hc_rdy, (s_ + hf * NST) * NCH + c + 7)
                        pe.matmul(bank(c), ident, hc[c], start=False, stop=True, skip_group_check=True).then_inc(y_acc, 1)

                for c in range(NCH):
                    pe.sem_inc(y_acc, 1)
                for hf in range(2):
                    if hf:
                        pe.wait_ge(y_rd, 1)
                    for c in range(NCH):
                        pe.matmul(bank(c), diag_D[:, c, :], xc[:, c, hf * HALF:(hf + 1) * HALF], start=True, stop=True)
                    spread(0, hf, 0)
                    with pe.Fori(0, NST // 2 - 1) as k:
                        spread(k * 2 + 1, hf, 1)
                        add_up(k * 2, hf)
                        spread(k * 2 + 2, hf, 0)
                        add_up(k * 2 + 1, hf)
                    spread(NST - 1, hf, 1)
                    add_up(NST - 2, hf)
                    add_up(NST - 1, hf)

            @block.scalar
            def _(act):
                def decay(s_, hf, odd):
                    n = hf * NST
                    act.wait_ge(b_ps, s_ + n + 1)
                    act.wait_ge(dBu_rdy, (s_ + n) * NCH + 3)
                    act.copy(b_sb[odd], bank(B_B)).then_inc(b_rd, 1)
                    for c in range(NCH):
                        act.wait_ge(scan_rdy, (s_ + n) * NCH + c + 2)
                        act.wait_ge(A_exp, 1)
                        b = (odd * NCH + c) % 2
                        j = c * NST + s_
                        scale = neg_A[:, j:j + 1] if isinstance(s_, int) else neg_A[:, bass.ds(j, 1)]
                        act.activation(bank(B_DA + b).rearrange("p (b t) -> p b t", t=TOK)[:, :, 1:TOK],
                                       delta[:, c, hf * HALF:(hf + 1) * HALF].rearrange("p (b t) -> p b t", t=TOK)[:, :, 1:TOK],
                                       ACT.Exp, scale=scale).then_inc(dA_rdy, 1)

                act.preload_act_table(ACT.Exp)
                act.sem_inc(b_rd, 1)
                act.wait_ge(zero_cols, 2)
                for hf in range(2):
                    with act.Fori(0, NST // 2) as k:
                        decay(k * 2, hf, 0)
                        decay(k * 2 + 1, hf, 1)

            @block.gpsimd
            def _(pool):
                def inputs(s_, hf, odd):
                    n = hf * NST
                    pool.wait_ge(b_rd, s_ + n + 2)
                    for c in range(NCH):
                        pool.wait_ge(scan_rdy, (s_ + n) * NCH + c + 1)
                        pool.tensor_tensor(dBu[c], du[:, c, hf * HALF:(hf + 1) * HALF], b_sb[odd], ALU.mult).then_inc(dBu_rdy, 1)

                for _ in range(6):
                    pool.sem_inc(dBu_rdy, 1)
                for hf in range(2):
                    with pool.Fori(0, NST // 2) as k:
                        inputs(k * 2, hf, 0)
                        inputs(k * 2 + 1, hf, 1)

            @block.vector
            def _(dve):
                def scan(s_, hf, odd, c):
                    n = (s_ + hf * NST) * NCH + c
                    dve.wait_ge(dA_rdy, n + 1)
                    dve.wait_ge(hc_rdy, n + 4)
                    dve.wait_ge(dBu_rdy, n + 7)
                    dve.tensor_tensor_scan(hs[c], bank(B_DA + (odd * NCH + c) % 2), dBu[c], 0.0, ALU.mult, ALU.add).then_inc(scan_rdy, 1)

                def times_C(s_, hf, odd, c):
                    n = (s_ + hf * NST) * NCH + c
                    dve.wait_ge(c_ps, s_ + hf * NST + 1)
                    dve.wait_ge(y_acc, n + 1)
                    dve.wait_ge(scan_rdy, n + 4)
                    dve.tensor_tensor(hc[c], hs[c], bank(B_C + odd), ALU.mult).then_inc(hc_rdy, 1)

                def state(s_, hf, odd):
                    scan(s_, hf, odd, 0)
                    scan(s_, hf, odd, 1)
                    times_C(s_, hf, odd, 0)
                    scan(s_, hf, odd, 2)
                    times_C(s_, hf, odd, 1)
                    times_C(s_, hf, odd, 2)

                for b in range(2):
                    dve.memset(bank(B_DA + b).rearrange("p (b t) -> p b t", t=TOK)[:, :, 0:1], 0.0).then_inc(zero_cols, 1)
                for _ in range(3):
                    dve.sem_inc(scan_rdy, 1)
                for _ in range(6):
                    dve.sem_inc(hc_rdy, 1)
                for hf in range(2):
                    with dve.Fori(0, NST // 2) as k:
                        state(k * 2, hf, 0)
                        state(k * 2 + 1, hf, 1)
                    dve.wait_ge(y_acc, 3 + U * (hf + 1))
                    for c in range(NCH):
                        t = slice(hf * HALF, (hf + 1) * HALF)
                        ins = dve.tensor_tensor(z[:, c, t], z[:, c, t], bank(c), ALU.mult)
                    ins.then_inc(y_rd, 1)

        chain2, o_ps, o_rd = s("chain2"), s("o_ps"), s("o_read")
        with nc.Block() as block:
            @block.tensor
            def _(pe):
                for i in range(NT):
                    if i >= 2:
                        pe.wait_ge(o_rd, i - 1)
                    for c in range(NCH):
                        mm = pe.matmul(bank(i % 2, EMB), z[:, c, i * P:(i + 1) * P], WS("out")[:, c * EMB:(c + 1) * EMB],
                                       start=(c == 0), stop=(c == NCH - 1))
                    mm.then_inc(o_ps, 1)

            @block.vector
            def _(dve):
                link = Chain(dve, chain2)
                for i in range(NT):
                    link(dve.tensor_scalar(x_n, h[:, i, :], ln_mean[:, i:i + 1], ln_rstd[:, i:i + 1], ALU.subtract, ALU.mult))
                    dve.wait_ge(o_ps, i + 1)
                    dve.tensor_tensor(h_new[:, :], bank(i % 2, EMB), V("ls_ssm"), ALU.mult).then_inc(o_rd, 1)
                    dve.wait_ge(o_rd, i + 1)
                    link.sync()
                    link(dve.tensor_tensor(h_new[:, :], h_new[:, :], x_n, ALU.add))
                    link.sync()
                    row_stats(dve, link, h_new[:, :], i, u_all)
                link.sync()

        def s(n):
            return stage_sem("so_" + n)

        def slot_parts(k):
            w = ring[:, k * PAIR_W:(k + 1) * PAIR_W]
            return (w[:, 0:2 * HID].rearrange("p (e f) -> p e f", e=2), w[:, 2 * HID:3 * HID],
                    w[:, 3 * HID:PAIR_W].rearrange("p (e c n) -> p e c n", e=2, c=NFC))

        t = Region(tail, 0, NEXP * NFC * EMB + NSSW)
        x_a = t.take(NX * 2 * NIMG)
        x_b = t.take(NX * NIMG)
        c_T = t.take(NTOK, NX)
        xg_a = [t.take(GRP * 2 * NIMG) for _ in range(2)]
        xg_b = [t.take(GRP * NIMG) for _ in range(2)]
        xbias = [t.take(HID + EMB, GRP) for _ in range(2)]
        phin_a, phin_b = t.take(NX), t.take(NX, EB)
        phi_r = t.take(NX)
        x_a4 = x_a.rearrange("p (r a c) -> p r a c", r=NPAIR, a=2)
        x_b3 = x_b.rearrange("p (r c) -> p r c", r=NPAIR)
        xn2 = [hid[:, k * EMB:(k + 1) * EMB] for k in range(2)]
        xTs = [(xT_a, xT_b), (hid[:, 2 * EMB:2 * EMB + P], hid[:, 2 * EMB + P:2 * EMB + 2 * P])]
        ce = [hidT[:, k * NX:(k + 1) * NX] for k in range(2)]
        de = [hidT[0:NX, 2 * NX + k * P:2 * NX + (k + 1) * P] for k in range(2)]
        d_sb = [hidT[:, 6 * NX + k * NX:6 * NX + (k + 1) * NX] for k in range(2)]
        cm, cs = oh[:, 0:2], oh[:, 2:4]
        dm, dsum = oh[0:NX, 4:8], oh[0:NX, 8:12]
        B_LG, B_LGT, B_CT, B_D, B_XS = 2, 3, 4, 5, 6
        slot_in = [sem(f"slot{k}_in") for k in range(NSLOT)]
        def load_pair(eng, p, k):
            return eng.dma_start(ring[:, k * PAIR_W:(k + 1) * PAIR_W], p).then_inc(slot_in[k], 16)

        def first_pairs(sp):
            for k in range(4):
                load_pair(sp, d["pairs"][k], k)

        top1_moe("m1", u_all, None, V("norm2"), "g1", EB, [(m1_w1a, m1_w1b), (m1_w3a, m1_w3b)], EB, m1_w2, ACT.Silu, True, u_all,
                 (ring, 4 * PAIR_W, 5 * PAIR_W), ("moe1_w13", "moe1_w2"), first_pairs)
        new_sems()
        (chain, pre, pw, phi_sq, phi_ps, xn_rdy, xT_ps, xT_sb, lg_ps, cmax, cexp, dshift, dexp, cd_rdy, cT_ps, cT_rd, dT_rd, xs_ps, xs_rd,
         zx) = (s(n) for n in ("chain", "pre", "pow", "phi_sq", "phi_ps", "xn", "xT_ps", "xT_sb", "lg_ps", "cmax", "cexp", "dshift",
                               "dexp", "cd", "cT_ps", "cT_read", "d_sb", "xs_ps", "xs_read", "zeroed"))

        with nc.Block() as block:
            @block.sync
            def _(sp):
                for k in range(4, NSLOT):
                    load_pair(sp, d["pairs"][k], k)

            @block.gpsimd
            def _(pool):
                pool.memset(x_a, 0.0).then_inc(zx, 1)
                pool.memset(x_b, 0.0).then_inc(zx, 1)
                pool.wait_ge(pre, 1)
                pool.tensor_tensor(ln_rstd[:, :], ln_tmp[:, :], C("neg_half"), ALU.pow).then_inc(pw, 1)
                pool.wait_ge(pre, 2)
                pool.tensor_tensor(row_scale[:, :], row_scale[:, :], C("half"), ALU.pow).then_inc(pw, 1)
                pool.wait_ge(pre, 3)
                pool.tensor_tensor(phi_r, phi_r, phin_a, ALU.pow).then_inc(pw, 1)

            @block.tensor
            def _(pe):
                def xT(i):
                    pe.wait_ge(xn_rdy, i + 1)
                    pe.transpose(bank(i % 2, P), xn2[i % 2][:, 0:P], ident)
                    pe.transpose(bank(i % 2, P, P)[0:EB], xn2[i % 2][:, P:EMB], ident).then_inc(xT_ps, 1)

                def logits_of(i):
                    a_, b_ = xTs[i % 2]
                    pe.wait_ge(xT_sb, i + 1)
                    if i >= 1:
                        pe.wait_ge(cexp, i)
                        pe.wait_ge(dshift, i)
                    pe.matmul(bank(B_LG, NX), a_, phin_a, start=True, stop=False)
                    pe.matmul(bank(B_LG, NX), b_[0:EB], phin_b, start=False, stop=True)
                    pe.matmul(bank(B_LGT, P)[0:NX], phin_a, a_, start=True, stop=False)
                    pe.matmul(bank(B_LGT, P)[0:NX], phin_b, b_[0:EB], start=False, stop=True).then_inc(lg_ps, 1)

                def slots_in(i):
                    pe.wait_ge(cd_rdy, i + 1)
                    if i >= 1:
                        pe.wait_ge(cT_rd, i)
                    pe.transpose(bank(B_CT, P)[0:NX], ce[i % 2], ident)
                    pe.transpose(bank(B_D, NX), de[i % 2], ident[0:NX, 0:NX]).then_inc(cT_ps, 1)
                    pe.wait_ge(dT_rd, i + 1)
                    j = i % 4
                    if j == 0 and i:
                        pe.wait_ge(xs_rd, 1)
                    for b in range(2):
                        rows = slice(b * TOK, (b + 1) * TOK)
                        x, w = xn2[i % 2][rows], d_sb[i % 2][rows]
                        w2 = w.rearrange("p (r a) -> p r a", a=2)
                        pe.matmul(bank(B_XS + b, NX, j * NX), x[:, 0:P], w, start=True, stop=True)
                        for a_ in range(2):
                            mm = pe.matmul(bank(B_XS + b, NPAIR, 4 * NX + j * NPAIR)[a_ * EB:(a_ + 1) * EB], x[:, P:EMB], w2[:, :, a_],
                                           start=True, stop=True)
                    mm.then_inc(xs_ps, 1)

                pe.wait_ge(phi_sq, 1)
                pe.matmul(bank(7, NX), C("ones"), phin_a, start=True, stop=False)
                pe.matmul(bank(7, NX), C("ones", EB), phin_b, start=False, stop=True).then_inc(phi_ps, 1)
                xT(0)
                logits_of(0)
                for i in range(NT):
                    if i + 1 < NT:
                        xT(i + 1)
                        logits_of(i + 1)
                    slots_in(i)

            @block.scalar
            def _(act):
                for i in range(NT):
                    k = i % 2
                    act.wait_ge(cmax, i + 1)
                    if i >= 2:
                        act.wait_ge(cT_ps, i - 1)
                    act.activation(ce[k], bank(B_LG, NX), ACT.Exp, bias=cm[:, k:k + 1], accum_out=cs[:, k:k + 1]).then_inc(cexp, 1)
                    act.wait_ge(dshift, i + 1)
                    act.activation(de[k], de[k], ACT.Exp).then_inc(dexp, 1)

            @block.vector
            def _(dve):
                link = Chain(dve, chain)
                ln_scalars(dve, link, None)
                dve.sem_inc(pre, 1)
                dve.wait_ge(pw, 1)
                link(dve.tensor_tensor(ln_tmp[:, :], ln_rstd[:, :], ln_rstd[:, :], ALU.mult))
                link.sync()
                link(dve.scalar_tensor_tensor(out=row_scale[:, :], in0=ln_tmp[:, :], scalar=float(EMB), in1=stats[:, :, 1],
                                              op0=ALU.mult, op1=ALU.mult))
                link.sync()
                dve.sem_inc(pre, 1)
                link(dve.tensor_tensor(phin_a, W("phi_a"), W("phi_a"), ALU.mult))
                link(dve.tensor_tensor(phin_b, W("phi_b", EB), W("phi_b", EB), ALU.mult))
                link.sync()
                dve.sem_inc(phi_sq, 1)
                dve.wait_ge(phi_ps, 1)
                link(dve.tensor_copy(phi_r, bank(7, NX)))
                link(dve.memset(phin_a, 0.5))
                link.sync()
                dve.sem_inc(pre, 1)
                dve.wait_ge(pw, 3)
                link(dve.tensor_scalar(phi_r, phi_r, L2_EPS, None, ALU.max))
                link(dve.tensor_scalar(row_scale[:, :], row_scale[:, :], L2_EPS, None, ALU.max))
                link.sync()
                link(dve.reciprocal(phi_r, phi_r))
                link(dve.reciprocal(row_scale[:, :], row_scale[:, :]))
                link.sync()
                link(dve.tensor_scalar(phi_r, phi_r, V("scale"), None, ALU.mult))
                link(dve.tensor_tensor(row_scale[:, :], row_scale[:, :], ln_rstd[:, :], ALU.mult))
                link.sync()
                link(dve.tensor_tensor(phin_a, W("phi_a"), phi_r, ALU.mult))
                link(dve.tensor_tensor(phin_b, W("phi_b", EB), phi_r[0:EB], ALU.mult))
                link.sync()
                dve.wait_ge(zx, 2)

                def norm(i):
                    if i >= 2:
                        dve.wait_ge(xs_ps, i - 1)
                    dve.tensor_scalar(xn2[i % 2], h[:, i, :], ln_mean[:, i:i + 1], row_scale[:, i:i + 1],
                                      ALU.subtract, ALU.mult).then_inc(xn_rdy, 1)

                def xT_copy(i):
                    a_, b_ = xTs[i % 2]
                    dve.wait_ge(xT_ps, i + 1)
                    dve.tensor_copy(a_, bank(i % 2, P))
                    dve.tensor_copy(b_[0:EB], bank(i % 2, P, P)[0:EB]).then_inc(xT_sb, 1)

                def weights(i):
                    k = i % 2
                    dve.wait_ge(lg_ps, i + 1)
                    link(dve.tensor_reduce(dm[:, 2 * k:2 * k + 2], bank(B_LGT, P)[0:NX].rearrange("p (b m) -> p b m", b=2), AX, ALU.max))
                    dve.tensor_reduce(cm[:, k:k + 1], bank(B_LG, NX), AX, ALU.max, negate=True).then_inc(cmax, 1)
                    link.sync()
                    if i >= 2:
                        dve.wait_ge(cT_ps, i - 1)
                    d3 = de[k].rearrange("p (b m) -> p b m", b=2)

                    def bc(x):
                        return x[:, 2 * k:2 * k + 2].unsqueeze(2).to_broadcast([NX, 2, TOK])

                    dve.tensor_tensor(d3, bank(B_LGT, P)[0:NX].rearrange("p (b m) -> p b m", b=2), bc(dm), ALU.subtract).then_inc(dshift, 1)
                    dve.wait_ge(cexp, i + 1)
                    link(dve.reciprocal(cs[:, k:k + 1], cs[:, k:k + 1]))
                    dve.wait_ge(dexp, i + 1)
                    link(dve.tensor_reduce(dsum[:, 2 * k:2 * k + 2], d3, AX, ALU.add))
                    link.sync()
                    link(dve.reciprocal(dsum[:, 2 * k:2 * k + 2], dsum[:, 2 * k:2 * k + 2]))
                    link(dve.tensor_scalar(ce[k], ce[k], cs[:, k:k + 1], None, ALU.mult))
                    link.sync()
                    dve.tensor_tensor(d3, d3, bc(dsum), ALU.mult).then_inc(cd_rdy, 1)

                def keep(i):
                    dve.wait_ge(cT_ps, i + 1)
                    if i >= 2:
                        dve.wait_ge(xs_ps, i - 1)
                    dve.tensor_copy(d_sb[i % 2], bank(B_D, NX)).then_inc(dT_rd, 1)
                    dve.tensor_copy(c_T[:, i * P:(i + 1) * P], bank(B_CT, P)[0:NX]).then_inc(cT_rd, 1)

                def spread(hf):
                    dve.wait_ge(xs_ps, 4 * (hf + 1))
                    for b in range(2):
                        src = bank(B_XS + b, 4 * NX).rearrange("p (j r a) -> p a r j", j=4, a=2)
                        srb = bank(B_XS + b, 4 * NPAIR, 4 * NX).rearrange("p (j r) -> p r j", j=4)
                        for a_ in range(2):
                            at = a_ * NIMG + hf * HIMG + b
                            end = at + HIMG - 1
                            link(dve.tensor_copy(x_a4[:, :, a_, at:end:2], src[:, a_]))
                            ins = link(dve.tensor_copy(x_b3[a_ * EB:(a_ + 1) * EB, :, at:end:2], srb[a_ * EB:(a_ + 1) * EB]))
                    link.sync()
                    dve.sem_inc(xs_rd, 1)

                norm(0)
                xT_copy(0)
                for i in range(NT):
                    if i + 1 < NT:
                        norm(i + 1)
                        xT_copy(i + 1)
                    weights(i)
                    keep(i)
                    if i % 4 == 3:
                        spread(i // 4)

        (xg_rdy, up_ps, hd_rdy, hT_ps, hT_v, hT_a, y_ps, y_rdy) = (
            s(n) for n in ("xg", "up_ps", "hid", "hidT_ps", "hidT_v", "hidT_a", "y_ps", "y_rdy"))
        bias_in = [s(f"bias{k}_in") for k in range(2)]
        y_out = [s(f"y{k}_out") for k in range(2)]
        B_UP, B_HT, B_YX = 0, 4, 6
        NHF = HID // 2
        y_rows = y_slots.rearrange("n (b m) -> (n b) m", m=EMB)
        pairs = d["pairs"]

        with nc.Block() as block:
            @block.sync
            def _(sp):
                for k in range(2):
                    sp.dma_start(xbias[k], d["x_bias"][k]).then_inc(bias_in[k], 16)
                with sp.Fori(0, NGRP // 2 - 1) as k:
                    for odd in range(2):
                        g = k * 2 + odd
                        sp.wait_ge(y_ps, g + 1)
                        for q in range(QP):
                            load_pair(sp, pairs[bass.ds((g + 2) * QP + q, 1)].rearrange("o p f -> (o p) f"), odd * QP + q)
                        sp.dma_start(xbias[odd], d["x_bias"][bass.ds(g + 2, 1)].rearrange("o e n -> (o e) n")).then_inc(bias_in[odd], 16)

            @block.tensor
            def _(pe):
                def group(g, k, odd):
                    pe.wait_ge(bias_in[odd], (k + 1) * 16)
                    pe.wait_ge(xg_rdy, g + 1)
                    for q in range(QP):
                        pe.wait_ge(slot_in[odd * QP + q], (k + 1) * 16)
                    for nh in range(2):
                        cols = slice(nh * NHF, (nh + 1) * NHF)
                        b = B_UP + 2 * odd + nh
                        pe.matmul(bank(b, NHF), C("b_rows", GRP), xbias[odd][:, cols], start=True, stop=False, skip_group_check=True)
                        for step in range(3):
                            for q in range(QP):
                                w1a, w1b, _ = slot_parts(odd * QP + q)
                                x = xg_b[odd][:, q * 2 * NIMG:(q + 1) * 2 * NIMG] if step == 2 else \
                                    xg_a[odd][:, (2 * q + step) * 2 * NIMG:(2 * q + step + 1) * 2 * NIMG]
                                w = w1b[:, cols] if step == 2 else w1a[:, step, cols]
                                mm = pe.matmul(bank(b, NHF)[32 * q:32 * (q + 1)], x, w, start=False, stop=(step == 2),
                                               skip_group_check=True)
                    mm.then_inc(up_ps, 1)
                    pe.wait_ge(hd_rdy, g + 1)
                    for c in range(NFC):
                        tr = pe.transpose(psum[:, B_HT * 512 + c * P:B_HT * 512 + (c + 1) * P], hid[:, c * P:(c + 1) * P], ident)
                    tr.then_inc(hT_ps, 1)
                    pe.wait_ge(hT_v, g + 1)
                    pe.wait_ge(hT_a, g + 1)
                    o = bank(B_YX + odd, 2 * EMB).rearrange("p (a n) -> p a n", a=2)
                    pe.matmul(o, C("b_rows", GRP), xbias[odd][:, HID:HID + EMB].unsqueeze(1).to_broadcast([GRP, 2, EMB]),
                              start=True, stop=False, skip_group_check=True)
                    for c in range(NFC):
                        for q in range(QP):
                            _, _, w2 = slot_parts(odd * QP + q)
                            mm = pe.matmul(o[32 * q:32 * (q + 1)], hidT[:, c * P + 32 * q:c * P + 32 * (q + 1)], w2[:, :, c, :],
                                           start=False, stop=(c == NFC - 1), skip_group_check=True)
                    mm.then_inc(y_ps, 1)

                with pe.Fori(0, NGRP // 2) as k:
                    group(k * 2, k, 0)
                    group(k * 2 + 1, k, 1)

            @block.scalar
            def _(act):
                def group(g, k, odd):
                    act.wait_ge(up_ps, g + 1)
                    act.activation(hid.rearrange("p (a f) -> p a f", a=2),
                                   psum[:, (B_UP + 2 * odd) * 512:(B_UP + 2 * odd + 2) * 512].rearrange("p (a f) -> p a f", a=2)[:, :, 0:NHF],
                                   ACT.Gelu).then_inc(hd_rdy, 1)
                    act.wait_ge(hT_ps, g + 1)
                    act.copy(hidT[:, 512:HID], bank(B_HT + 1, HID - 512)).then_inc(hT_a, 1)
                    act.wait_ge(y_rdy, g + 1)
                    act.dma_start(y_rows[bass.ds(g * P, P), :], yout[:, odd, :]).then_inc(y_out[odd], 16)

                act.preload_act_table(ACT.Gelu)
                for k in range(2):
                    act.sem_inc(y_out[k], 16)
                with act.Fori(0, NGRP // 2) as k:
                    group(k * 2, k, 0)
                    group(k * 2 + 1, k, 1)
                for k in range(2):
                    act.wait_ge(y_out[k], 16 + 16 * NGRP // 2)

            @block.vector
            def _(dve):
                def inputs(g, odd):
                    dve.tensor_scalar(xg_a[odd], x_a[:, bass.ds(g * GRP * 2 * NIMG, GRP * 2 * NIMG)] if not isinstance(g, int) else
                                      x_a[:, g * GRP * 2 * NIMG:(g + 1) * GRP * 2 * NIMG], 1.0, None, ALU.mult)
                    dve.tensor_scalar(xg_b[odd], x_b[:, bass.ds(g * GRP * NIMG, GRP * NIMG)] if not isinstance(g, int) else
                                      x_b[:, g * GRP * NIMG:(g + 1) * GRP * NIMG], 1.0, None, ALU.mult).then_inc(xg_rdy, 1)

                def group(g, k, odd):
                    dve.wait_ge(hT_ps, g + 1)
                    dve.tensor_copy(hidT[:, 0:512], bank(B_HT)).then_inc(hT_v, 1)
                    dve.wait_ge(y_ps, g + 1)
                    o = bank(B_YX + odd, 2 * EMB)
                    dve.tensor_scalar(y_t, o[:, 0:EMB], C("par0"), None, ALU.mult).then_inc(y_half, 1)
                    dve.wait_ge(y_out[odd], k * 16 + 16)
                    dve.wait_ge(y_half, g + 1)
                    dve.scalar_tensor_tensor(out=yout[:, odd, :], in0=o[:, EMB:2 * EMB], scalar=C("par1"), in1=y_t,
                                             op0=ALU.mult, op1=ALU.add).then_inc(y_rdy, 1)

                y_t = x_n
                y_half = s("y_half")
                inputs(0, 0)
                inputs(1, 1)
                with dve.Fori(0, NGRP // 2 - 1) as k:
                    for odd in range(2):
                        group(k * 2 + odd, k, odd)
                        inputs(k * 2 + odd + 2, odd)
                for odd in range(2):
                    group(NGRP - 2 + odd, NGRP // 2 - 1, odd)

        y_all = ring[0:NX, 0:NIMG * EMB]
        res = ring[:, PAIR_W:PAIR_W + NT * EMB].rearrange("p (i n) -> p i n", i=NT)
        y_in, c_ps, r_rdy, stored = s("y_in"), s("c_ps"), s("result"), s("stored")
        out_t = out.rearrange("(i p) n -> p i n", p=P)
        with nc.Block() as block:
            @block.sync
            def _(sp):
                sp.dma_start(y_all, y_slots).then_inc(y_in, 16)
                for i in range(0, NT, 2):
                    sp.wait_ge(r_rdy, i + 2)
                    sp.dma_start(out_t[:, i:i + 2, :], res[:, i:i + 2, :]).then_inc(stored, 16)
                sp.wait_ge(stored, 16 * NT // 2)

            @block.tensor
            def _(pe):
                pe.wait_ge(y_in, 16)
                for b in range(NIMG):
                    mm = pe.matmul(bank(b // 2, EMB)[(b % 2) * TOK:(b % 2 + 1) * TOK], c_T[:, b * TOK:(b + 1) * TOK],
                                   y_all[:, b * EMB:(b + 1) * EMB], start=True, stop=True)
                    if b % 2:
                        mm.then_inc(c_ps, 1)

            @block.vector
            def _(dve):
                for i in range(NT):
                    dve.wait_ge(c_ps, i + 1)
                    dve.tensor_tensor(res[:, i, :], h[:, i, :], bank(i, EMB), ALU.add).then_inc(r_rdy, 1)


def host_layout(x):
    import numpy as np

    f = np.float32
    n = {k: np.asarray(v) for k, v in x.items()}

    def rows(a, extra=None, rows_=P):
        o = np.zeros((rows_, a.shape[1]), f)
        o[:a.shape[0]] = a
        if extra is not None:
            o[a.shape[0]] = extra
        return o

    def col2(v):
        o = np.zeros((P, 2), f)
        o[:, 0] = v[:P]
        o[:EB, 1] = v[P:]
        return o

    def rep(v):
        return np.broadcast_to(v.reshape(1, -1), (P, v.size)).astype(f)

    def chunks(v):
        return v.reshape(NCH, P, -1).transpose(1, 0, 2).reshape(P, -1)

    d = {}
    img = n["x"].reshape(NIMG, 3, 8, 16, 8, 16)
    feat = img.transpose(3, 5, 1, 0, 2, 4).reshape(NPC, P, NTOK)
    d["patches"] = np.ascontiguousarray(feat.transpose(1, 0, 2))
    d["tok_w"] = np.ascontiguousarray(n["L0_tok_W"].T.reshape(NPC, P, EMB).transpose(1, 0, 2))
    d["tok_b"] = n["L0_tok_b"].reshape(1, EMB)

    c = np.zeros((P, NCST), f)

    def put(name, a, rows_=P):
        i, j = CST[name]
        c[:rows_, i:j] = a

    put("ident", np.eye(P))
    put("upper", np.triu(np.ones((P, P)), 1))
    put("ones", 1.0)
    t = np.arange(P) % TOK
    put("causal", np.where(np.arange(TOK)[None] <= t[:, None], 0.0, -BIG))
    put("kmask", (np.arange(P)[:, None] // HD == np.arange(NHA)[None]) * (1.0 / np.sqrt(f(HD))))
    freqs = f(1.0) / np.power(f(10000.0), np.arange(0, HD, 2, dtype=f) / f(HD)).astype(f)
    ang = np.outer(t.astype(f), freqs).astype(f)
    put("cos2", np.repeat(np.cos(ang), 2, axis=1))
    put("sin", np.sin(ang))
    put("nsin", -np.sin(ang))
    put("iota", np.arange(NEXP)[None])
    put("iota_far", np.arange(NEXP)[None] + 1000.0)
    put("by128", np.arange(NT)[None] * 128.0)
    put("block", np.arange(NBLK)[None])
    carry = np.ones((NEXP, NT))
    carry[:, 0] = 0
    put("carry", carry.reshape(1, -1))
    put("neg_half", -0.5)
    put("half", 0.5)
    put("b_rows", (np.arange(GRP)[:, None] == np.arange(P)[None] // NIMG), GRP)
    put("par0", ((np.arange(P) // NIMG) % 2 == 0)[:, None])
    put("par1", ((np.arange(P) // NIMG) % 2 == 1)[:, None])
    d["cst"] = c
    s = np.zeros((XPJ, 2 * NST, P), f)
    for k in range(2 * NST):
        s[[k, 2 * NST + k, 4 * NST + k], k, :] = 1.0
    d["sel"] = np.where(s > 0, 0x3F80, 0).astype(np.uint16)

    v = np.zeros((P, NVEC), f)

    def putv(name, a):
        i, j = VEC[name]
        v[:, i:j] = a

    putv("nscale", col2(n["L0_attn_norm_scale"]))
    putv("nbias", col2(n["L0_attn_norm_bias"]))
    putv("norm1", col2(n["L1_attn_norm1_w"]))
    putv("norm2", col2(n["L1_attn_norm2_w"]))
    putv("conv_w", chunks(n["L1_attn_conv_w"]))
    putv("conv_b", chunks(n["L1_attn_conv_b"]))
    putv("dt_b", chunks(n["L1_attn_dt_proj_b"]))
    putv("A_log", chunks(n["L1_attn_A_log"]))
    putv("D", chunks(n["L1_attn_D_param"]))
    putv("rezero", rep(n["L0_attn_rezero"]))
    putv("scale", rep(n["L1_ffn_scale"]))
    putv("sinks", rep(n["L0_attn_sinks"]))
    putv("ls_ssm", rep(n["L1_attn_ls_ssm_g"]))
    putv("ls_ffn", rep(n["L1_attn_ls_ffn_g"]))
    d["vec"] = v

    def two(w, b=None):
        return [rows(w[:P]), rows(w[P:], b)]

    d["atw"] = np.concatenate(
        two(n["L0_attn_W_attn"], n["L0_attn_b_attn"]) + two(n["L0_attn_W_proj"], n["L0_attn_b_proj"])
        + two(n["L0_ffn_Wg"], n["L0_ffn_bg"]) + two(n["L1_attn_gate_w"]) + two(n["L1_ffn_phi"][:, :, 0]), axis=1)

    def expert_rows(w, b=None):
        return [np.concatenate([rows(w[e, :P]) for e in range(NEXP)], axis=1),
                np.concatenate([rows(w[e, P:], None if b is None else b[e]) for e in range(NEXP)], axis=1)]

    def down(w):
        return w.reshape(w.shape[0], NFC, P, EMB).transpose(2, 0, 1, 3).reshape(P, -1)

    d["moe0"] = np.concatenate(expert_rows(n["L0_ffn_W1"], n["L0_ffn_b1"]) + [down(n["L0_ffn_W2"])], axis=1)
    d["moe0_b2"] = n["L0_ffn_b2"].reshape(1, NEXP * EMB)
    d["moe1_w13"] = np.concatenate(expert_rows(n["L1_attn_w1"]) + expert_rows(n["L1_attn_w3"]), axis=1)
    d["moe1_w2"] = down(n["L1_attn_w2"])
    xw = np.zeros((DIN, XPJ), f)
    xw[:, :DTR] = n["L1_attn_x_proj_w"][:, :DTR]
    xw[:, BC0:] = n["L1_attn_x_proj_w"][:, DTR:]
    d["ssw"] = np.concatenate(two(n["L1_attn_in_proj_w"]) + [chunks(xw), rows(n["L1_attn_dt_proj_w"]),
                                                             chunks(n["L1_attn_out_proj_w"])], axis=1)
    w1 = n["L1_ffn_w1"].reshape(NPAIR, 2, EMB, HID)
    w2 = n["L1_ffn_w2"].reshape(NPAIR, 2, NFC, P, EMB)
    d["pairs"] = np.concatenate([
        w1[:, :, :P].transpose(0, 2, 1, 3).reshape(NPAIR, P, 2 * HID),
        w1[:, :, P:].reshape(NPAIR, P, HID),
        w2.transpose(0, 3, 1, 2, 4).reshape(NPAIR, P, 2 * NFC * EMB)], axis=2)
    d["x_bias"] = np.concatenate([n["L1_ffn_b1"], n["L1_ffn_b2"]], axis=1).reshape(NGRP, GRP, HID + EMB)
    return {k: np.ascontiguousarray(a) for k, a in d.items()}


def kernel(**inputs):
    import numpy as np
    from concourse import bacc
    from concourse.bass_utils import run_bass_kernel_spmd

    nc = bacc.Bacc("TRN2", target_bir_lowering=False, num_devices=1)
    arrays = host_layout(inputs)
    d = {k: nc.dram_tensor("in_" + k, a.shape, mybir.dt.from_np(a.dtype), kind="ExternalInput").ap() for k, a in arrays.items()}
    out = nc.dram_tensor("out", [NTOK, EMB], F32, kind="ExternalOutput").ap()
    build(nc, d, out)
    r = run_bass_kernel_spmd(nc, [{"in_" + k: a for k, a in arrays.items()}], core_ids=[0])
    return np.asarray(r.results[0]["out"]).reshape(NIMG, TOK, EMB)
```

```python
from contextlib import ExitStack

import concourse.bass as bass
from concourse import mybir

F32 = mybir.dt.float32
BF16 = mybir.dt.bfloat16
I32 = mybir.dt.int32
U16 = mybir.dt.uint16
U32 = mybir.dt.uint32
ALU = mybir.AluOpType
ACT = mybir.ActivationFunctionType
AX = mybir.AxisListType.X

P = 128
EMB = 192
EB = EMB - P
NIMG, TOK = 16, 64
NTOK = NIMG * TOK
NT = NTOK // P
PATCH_F = 768
NPC = PATCH_F // P
NH, HD = 12, 16
NHA = P // HD
NHB = NH - NHA
NEXP = 4
HID = 768
NFC = HID // P
NBLK = NT + NEXP - 1
DIN = 384
NCH = DIN // P
NST = 16
DTR = 48
BC0 = 64
XPJ = BC0 + 2 * NST
HALF = NTOK // 2
HIMG = NIMG // 2
NX = 64
NPAIR = NX // 2
GRP = 8
NGRP = NX // GRP
QP = 4
NSLOT = 8
PART_W = 2 * HID + HID
PAIR_W = 2 * PART_W
assert PART_W == 2 * NFC * EMB
TAIL = 9472
BIG = 1.0e30
AT_WARM = (1,2,10)
LN_EPS, RMS_EPS, L2_EPS = 1e-5, 1e-6, 1e-12


def columns(parts):
    at, out = 0, {}
    for name, n in parts:
        out[name] = (at, at + n)
        at += n
    return out, at


CST, NCST = columns([("ident", P), ("upper", P), ("ones", P), ("causal", TOK), ("kmask", NHA), ("cos2", HD),
                     ("sin", HD // 2), ("nsin", HD // 2), ("iota", NEXP), ("iota_far", NEXP),
                     ("by128", NT), ("block", NBLK), ("carry", NEXP * NT), ("neg_half", NT), ("half", NT),
                     ("b_rows", P), ("par0", 1), ("par1", 1)])
VEC, NVEC = columns([("nscale", 2), ("nbias", 2), ("norm1", 2), ("norm2", 2), ("conv_w", 4 * NCH),
                     ("conv_b", NCH), ("dt_b", NCH), ("A_log", NCH * NST), ("D", NCH), ("rezero", 1),
                     ("scale", 1), ("sinks", NH), ("ls_ssm", EMB), ("ls_ffn", EMB)])
ATW, NATW = columns([("qkv_a", 3 * EMB), ("qkv_b", 3 * EMB), ("proj_a", EMB), ("proj_b", EMB),
                     ("g0_a", NEXP), ("g0_b", NEXP), ("g1_a", NEXP), ("g1_b", NEXP), ("phi_a", NX), ("phi_b", NX)])
SSW, NSSW = columns([("in_a", 2 * DIN), ("in_b", 2 * DIN), ("x", NCH * XPJ), ("dt", DIN), ("out", NCH * EMB)])


class Chain:

    def __init__(self, eng, sem):
        self.eng, self.sem, self.base, self.n = eng, sem, 0, 0

    def __call__(self, ins):
        ins.then_inc(self.sem, 1)
        self.n += 1
        return ins

    def sync(self):
        self.eng.wait_ge(self.sem, self.base + self.n)

    def turn(self, i, per):
        self.before = self.base + self.n
        self.base, self.n = self.before + i * per, 0

    def turns(self, n, per):
        assert self.n == per, (self.n, per)
        self.base, self.n = self.before + n * per, 0


def one(ap3, i):
    if isinstance(i, int):
        return ap3[:, i, :]
    return ap3[:, bass.ds(i, 1), :].rearrange("p o f -> p (o f)")


def build(nc, d, out):
    with ExitStack() as ctx:
        def sb(name, shape, dt=F32):
            return ctx.enter_context(nc.sbuf_tensor(name, shape, dt))

        def sem(name):
            return ctx.enter_context(nc.semaphore(name))

        stage_sems = []

        def stage_sem(name):
            stage_sems.append(nc.alloc_semaphore(name))
            return stage_sems[-1]

        def new_sems():
            nc.clear_and_free_semaphores(stage_sems)
            stage_sems.clear()
            nc.all_engine_barrier()

        ring = sb("ring", [P, NSLOT * PAIR_W])
        tail = sb("tail", [P, TAIL])
        h = sb("h", [P, NT, EMB])
        cst = sb("cst", [P, NCST])
        vec = sb("vec", [P, NVEC])
        stats = sb("stats", [P, NT, 2])
        bn = sb("bn", [P, 6])
        bn_all = sb("bn_all", [P, NT, 6])
        mean_var = sb("mean_var", [P, 2])
        h_new = sb("h_new", [P, EMB])
        ln_mean = sb("ln_mean", [P, NT])
        ln_rstd = sb("ln_rstd", [P, NT])
        ln_tmp = sb("ln_tmp", [P, NT])
        row_scale = sb("row_scale", [P, NT])
        warm16 = sb("warm16", [P, P], BF16)
        psum = ctx.enter_context(nc.psum_tensor("psum", [P, 8 * 512], F32))

        def bank(b, n=512, at=0):
            return psum[:, 512 * b + at:512 * b + at + n]

        def keep_warm(pe, n, b):
            for _ in range(n):
                pe.matmul(bank(b).rearrange("p (r m) -> p r m", m=P), warm16[:, :],
                          warm16[:, :].unsqueeze(1).to_broadcast([P, 512 // P, P]), start=True, stop=True, skip_group_check=True)

        def C(name, rows=P):
            a, b = CST[name]
            return cst[0:rows, a:b]

        def V(name, rows=P):
            a, b = VEC[name]
            return vec[0:rows, a:b]

        ident = C("ident")
        x_sorted = nc.dram_tensor("x_sorted", [NBLK * P, EMB], F32).ap()
        y_sorted = nc.dram_tensor("y_sorted", [NBLK * P, EMB], F32).ap()
        y_slots = nc.dram_tensor("y_slots", [NX, NIMG * EMB], F32).ap()

        class Region:

            def __init__(self, buf, at, end):
                self.buf, self.at, self.end = buf, at, end

            def take(self, n, rows=P):
                a = self.at
                self.at += n
                assert self.at <= self.end, (self.at, self.end)
                return self.buf[0:rows, a:a + n]

        MOE0 = 2 * NEXP * HID + NEXP * NFC * EMB
        W13 = 3 * NEXP * HID
        ring_cols = NSLOT * PAIR_W
        t = Region(tail, 0, TAIL)
        m1_w2 = t.take(NEXP * NFC * EMB).rearrange("p (e c n) -> p e c n", e=NEXP, c=NFC)
        ssw = t.take(NSSW)
        atw = t.take(NATW)
        r0 = Region(ring, 0, ring_cols - W13)
        m0_buf = r0.take(MOE0)
        m0_w1a = m0_buf[:, 0:NEXP * HID].rearrange("p (e f) -> p e f", e=NEXP)
        m0_w1b = m0_buf[0:EB + 1, NEXP * HID:2 * NEXP * HID].rearrange("p (e f) -> p e f", e=NEXP)
        m0_w2 = m0_buf[:, 2 * NEXP * HID:MOE0].rearrange("p (e c n) -> p e c n", e=NEXP, c=NFC)
        w13 = ring[:, ring_cols - W13:ring_cols].rearrange("p (k e f) -> p k e f", k=3, e=NEXP)
        m1_w1a, m1_w3a = w13[:, 0], w13[:, 1]
        m1_w1b, m1_w3b = w13[0:EB, 2], w13[EB:P, 2]
        b2_row = r0.take(HID, 1)
        free0 = r0.at

        def W(name, rows=P):
            a, b = ATW[name]
            return atw[0:rows, a:b]

        def WS(name, rows=P):
            a, b = SSW[name]
            return ssw[0:rows, a:b]

        mo = sb("mo", [P, 2496])
        m = Region(mo, 0, 2496)
        xT_a = m.take(P)
        xT_b = m.take(P)
        hid = m.take(HID)
        hidT = m.take(HID)
        x_cur2 = m.take(2 * P)
        x_n = m.take(EMB)
        slotf = m.take(NT)
        logits = m.take(NT * NEXP)
        oh = m.take(NT * NEXP)
        rt = [m.take(NT * NEXP) for _ in range(3)]
        mx = m.take(NT)
        sb_ = m.take(NEXP + 1)
        blkc = m.take(NEXP)
        bl = m.take(NBLK * NEXP)
        eidf = m.take(NBLK)
        gate = m.take(NT)
        slot_u = sb("slot_u", [P, NT], U32)
        eid = sb("eid", [P, NBLK], I32)
        yout = sb("yout", [P, 2, EMB])

        loaded = {n: sem(n + "_in") for n in ("tok_w", "tok_b", "cst", "vec", "atw", "moe0", "moe0_b2", "ssw", "moe1_w13", "moe1_w2")}
        zeroed = [sem(f"zeroed{k}") for k in range(-(-NBLK // NEXP))]
        zeros = sem("zeros")

        def ln_scalars(dve, link, tiles=slice(0, NT)):
            link(dve.tensor_copy(ln_mean[:, tiles], stats[:, tiles, 0]))
            link(dve.tensor_scalar(ln_tmp[:, tiles], stats[:, tiles, 1], LN_EPS, None, ALU.add))
            link.sync()

        def row_stats(dve, link, x, i, to=h):
            link(dve.bn_stats(bn[:, :], x))
            link.sync()
            link(dve.tensor_scalar(one(to, i), x, 1.0, None, ALU.mult))
            link(dve.bn_aggr(mean_var[:, :], bn[:, :]))
            link.sync()
            link(dve.tensor_scalar(one(stats, i), mean_var[:, :], 1.0, None, ALU.mult))

        xp_all = ring[:, free0:free0 + NPC * NTOK].rearrange("p (c t) -> p c t", c=NPC)
        tokw = ring[:, free0 + NPC * NTOK:free0 + NPC * NTOK + NPC * EMB].rearrange("p (c n) -> p c n", c=NPC)
        tok_b = ring[0:1, free0 + NPC * NTOK + NPC * EMB:free0 + NPC * NTOK + NPC * EMB + EMB]
        NPX = 4
        patches_in = [sem(f"patches_in{n}") for n in range(NPX)]
        tok_mm, tok_done, tok_chain, half_stats, tok_rstd, warm_rdy = (stage_sem(n) for n in ("tok_mm", "tok_done", "tok_chain", "half_stats", "tok_rstd", "warm"))

        with nc.Block() as block:
            @block.sync
            def _(sp):
                def patches(n):
                    w = NTOK // NPX
                    sp.dma_start(xp_all[:, :, n * w:(n + 1) * w], d["patches"][:, :, n * w:(n + 1) * w]).then_inc(patches_in[n], 16)

                sp.dma_start(tokw, d["tok_w"]).then_inc(loaded["tok_w"], 16)
                patches(0)
                sp.dma_start(tok_b, d["tok_b"]).then_inc(loaded["tok_b"], 16)
                sp.dma_start(cst[:, :], d["cst"]).then_inc(loaded["cst"], 16)
                for n in range(1, NPX):
                    patches(n)
                sp.dma_start(vec[:, :], d["vec"]).then_inc(loaded["vec"], 16)
                sp.dma_start(atw, d["atw"]).then_inc(loaded["atw"], 16)
                sp.dma_start(m0_buf, d["moe0"]).then_inc(loaded["moe0"], 16)
                sp.dma_start(b2_row, d["moe0_b2"]).then_inc(loaded["moe0_b2"], 16)
                sp.dma_start(ssw, d["ssw"]).then_inc(loaded["ssw"], 16)
                sp.dma_start(ring[:, ring_cols - W13:ring_cols], d["moe1_w13"]).then_inc(loaded["moe1_w13"], 16)
                sp.dma_start(m1_w2.rearrange("p e c n -> p (e c n)"), d["moe1_w2"]).then_inc(loaded["moe1_w2"], 16)

            @block.gpsimd
            def _(pool):
                pool.memset(warm16[:, :], 0.0).then_inc(warm_rdy, 1)
                pool.memset(hid[:, :], 0.0).then_inc(zeros, 1)
                pool.wait_ge(half_stats, 1)
                pool.tensor_tensor(ln_rstd[:, 0:4], ln_tmp[:, 0:4], C("neg_half")[:, 0:4], ALU.pow).then_inc(tok_rstd, 1)

            @block.scalar
            def _(act):
                act.wait_ge(zeros, 1)
                for b in range(0, NBLK, NEXP):
                    n = min(NEXP, NBLK - b)
                    act.dma_start(x_sorted[b * P:(b + n) * P, :].rearrange("(b p) n -> p b n", p=P),
                                  hid[:, 0:n * EMB].rearrange("p (b n) -> p b n", n=EMB)).then_inc(zeroed[b // NEXP], 16)

            @block.tensor
            def _(pe):
                pe.wait_ge(warm_rdy, 1)
                keep_warm(pe, 14, 2)
                pe.wait_ge(loaded["tok_w"], 16)
                for i in range(NT):
                    if i % (NT // NPX) == 0:
                        pe.wait_ge(patches_in[i // (NT // NPX)], 16)
                    if i >= 2:
                        pe.wait_ge(tok_done, i - 1)
                    for c in range(NPC):
                        pe.matmul(bank(i % 2, EMB), xp_all[:, c, i * P:(i + 1) * P], tokw[:, c, :],
                                  start=(c == 0), stop=False)
                    if i == 0:
                        for n in ("tok_b", "cst"):
                            pe.wait_ge(loaded[n], 16)
                    pe.matmul(bank(i % 2, EMB), C("ones", 1), tok_b, start=False, stop=True).then_inc(tok_mm, 1)

            @block.vector
            def _(dve):
                link = Chain(dve, tok_chain)
                for i in range(NT):
                    dve.wait_ge(tok_mm, i + 1)
                    dve.tensor_copy(h_new[:, :], bank(i % 2, EMB)).then_inc(tok_done, 1)
                    dve.wait_ge(tok_done, i + 1)
                    row_stats(dve, link, h_new[:, :], i)
                    if i % 4 == 3:
                        link.sync()
                        ln_scalars(dve, link, slice(i - 3, i + 1))
                        dve.sem_inc(half_stats, 1)

        a = Region(ring, free0, ring_cols - W13)
        xn = a.take(EMB)
        qk_r = a.take(2 * EMB)
        rot_t = a.take(EMB * 2)
        v_all = a.take(NT * EMB).rearrange("p (i n) -> p i n", i=NT)
        qT_a, qT_b = a.take(P), a.take(P, EB)
        k_a = a.take(2 * NHA * TOK).rearrange("p (b g k) -> p b g k", b=2, g=NHA)
        k_b = a.take(2 * NHB * TOK, EB).rearrange("p (b g k) -> p b g k", b=2, g=NHB)
        prob = a.take(NH * TOK).rearrange("p (g k) -> p g k", g=NH)
        pT = a.take(NH * P).rearrange("p (g q) -> p g q", g=NH)
        yn = a.take(EMB)
        yT_a, yT_b = a.take(P), a.take(P)
        hmax, hsum, esink, rinv = a.take(NH), a.take(NH), a.take(NH), a.take(NH)
        ident16 = a.take(P // 2).bitcast(BF16)
        causal16 = a.take(TOK // 2).bitcast(BF16)

        B_XV, B_QK, B_QKT, B_S, B_PT, B_Y = 0, 1, 2, 3, 5, 7
        X_A, X_B, V_AT = 0, P, 2 * P
        YT_A, YT_B = EMB, EMB + P
        at_chain, at_pre, at_rstd = stage_sem("at_chain"), stage_sem("at_pre"), stage_sem("at_rstd")
        xn_ready, xT_ps, xT_sb, qkv_ps, v_ready, rot_ready, qk_rot, qkT_ps, qk_ready = (
            stage_sem("at_" + n) for n in ("xn", "xT_ps", "xT_sb", "qkv_ps", "v_ready", "rot_ready", "qk_rot", "qkT_ps", "qk_ready"))
        q_ready, s_ps, p_ready, pT_ps, pT_sb, y_ps, y_ready, yT_ps, yT_sb, pr_ps, pr_read, esink_done, sh, mask_ready = (
            stage_sem("at_" + n) for n in ("q_ready", "s_ps", "p_ready", "pT_ps", "pT_sb", "y_ps", "y_ready",
                                     "yT_ps", "yT_sb", "pr_ps", "pr_read", "esink_done", "s_shift", "mask_ready"))

        def all_turns(eng, turn, link=None, per=0):
            turn(-2, (0,))
            turn(-1, (0, 1))
            turn(0, (0, 1, 2))
            with eng.Fori(0, (NT - 4) // 2) as k:
                if link:
                    link.turn(k, per)
                turn(k * 2 + 1, (0, 1, 2, 3), True)
                turn(k * 2 + 2, (0, 1, 2, 3), True)
            if link:
                link.turns((NT - 4) // 2, per)
            turn(NT - 3, (0, 1, 2, 3))
            turn(NT - 2, (1, 2, 3))
            turn(NT - 1, (2, 3))
            turn(NT, (3,))

        with nc.Block() as block:
            @block.gpsimd
            def _(pool):
                def rotated(i):
                    pool.wait_ge(rot_ready, i + 1)
                    pool.tensor_tensor(qk_r, qk_r, rot_t, ALU.add).then_inc(qk_rot, 1)

                def turn(t, steps, inner=False):
                    if 0 in steps:
                        rotated(t + 2)

                pool.tensor_tensor(ln_rstd[:, 4:NT], ln_tmp[:, 4:NT], C("neg_half")[:, 4:NT], ALU.pow).then_inc(at_rstd, 1)
                pool.memset(pT, 0.0).then_inc(at_pre, 1)
                all_turns(pool, turn)

            @block.tensor
            def _(pe):
                def xT(i):
                    pe.wait_ge(xn_ready, i + 1)
                    pe.wait_ge(v_ready, i + 1)
                    pe.transpose(bank(B_XV, P, X_A), xn[:, 0:P], ident)
                    pe.transpose(bank(B_XV, P, X_B)[0:EB], xn[:, P:EMB], ident).then_inc(xT_ps, 1)

                def qkv(i):
                    pe.wait_ge(xT_sb, i + 1)
                    for b, at, n0, n in ((B_QK, 0, 0, 2 * EMB), (B_XV, V_AT, 2 * EMB, EMB)):
                        pe.matmul(bank(b, n, at), xT_a, W("qkv_a")[:, n0:n0 + n], start=True, stop=False)
                        mm = pe.matmul(bank(b, n, at), xT_b[0:EB + 1], W("qkv_b", EB + 1)[:, n0:n0 + n], start=False, stop=True)
                    mm.then_inc(qkv_ps, 1)

                def qkT(i):
                    pe.wait_ge(qk_rot, i + 1)
                    pe.transpose(bank(B_QKT, P), qk_r[:, 0:P], ident)
                    pe.transpose(bank(B_QKT, P, P)[0:EB], qk_r[:, P:EMB], ident)
                    pe.transpose(bank(B_QKT, P, 2 * P), qk_r[:, EMB:EMB + P], ident)
                    pe.transpose(bank(B_QKT, P, 3 * P)[0:EB], qk_r[:, EMB + P:2 * EMB], ident).then_inc(qkT_ps, 1)

                def mask(i):
                    for b, n in ((B_S, NHA), (B_S + 1, NHB)):
                        pe.matmul(bank(b, n * TOK).rearrange("p (g k) -> p g k", g=n), ident16,
                                  causal16.unsqueeze(1).to_broadcast([P, n, TOK]), start=True, stop=False, skip_group_check=True)

                def scores(i):
                    pe.wait_ge(q_ready, i + 1)
                    pe.wait_ge(qk_ready, i + 1)
                    for b in range(2):
                        rows = slice(b * TOK, (b + 1) * TOK)
                        pe.matmul(psum[rows, B_S * 512:B_S * 512 + NHA * TOK], qT_a[:, rows],
                                  k_a[:, b].rearrange("p g k -> p (g k)"), start=False, stop=True, skip_group_check=True)
                        mm = pe.matmul(psum[rows, (B_S + 1) * 512:(B_S + 1) * 512 + NHB * TOK], qT_b[:, rows],
                                       k_b[:, b].rearrange("p g k -> p (g k)"), start=False, stop=True, skip_group_check=True)
                    mm.then_inc(s_ps, 1)

                def probs_T(i):
                    pe.wait_ge(p_ready, i + 1)
                    for j in range(NH // 2):
                        tr = pe.transpose(psum[:, B_PT * 512 + j * P:B_PT * 512 + (j + 1) * P],
                                          prob[:, 2 * j:2 * j + 2, :].rearrange("p g k -> p (g k)"), ident)
                    tr.then_inc(pT_ps, 1)

                def attend(i):
                    pe.wait_ge(pT_sb, i + 1)
                    v = one(v_all, i)
                    pe.wait_ge(pr_read, i + 1)
                    for g in range(NH):
                        mm = pe.matmul(bank(B_Y, HD, g * HD), pT[:, g, :], v[:, g * HD:(g + 1) * HD],
                                       start=True, stop=True)
                    mm.then_inc(y_ps, 1)

                def y_T(i):
                    pe.wait_ge(y_ready, i + 1)
                    pe.transpose(bank(B_Y, P, YT_A), yn[:, 0:P], ident)
                    pe.transpose(bank(B_Y, P, YT_B)[0:EB], yn[:, P:EMB], ident).then_inc(yT_ps, 1)

                def project(i):
                    pe.wait_ge(yT_sb, i + 1)
                    pe.matmul(bank(B_Y, EMB), yT_a, W("proj_a"), start=True, stop=False)
                    pe.matmul(bank(B_Y, EMB), yT_b[0:EB + 1], W("proj_b", EB + 1), start=False, stop=True).then_inc(pr_ps, 1)

                def turn(t, steps, inner=False):
                    if 0 in steps:
                        xT(t + 2)
                    keep_warm(pe, AT_WARM[0], B_PT)
                    if 2 in steps:
                        probs_T(t)
                    keep_warm(pe, AT_WARM[1], B_S)
                    if 1 in steps:
                        mask(t + 1)
                    if 0 in steps:
                        qkv(t + 2)
                    if 3 in steps:
                        y_T(t - 1)
                        project(t - 1)
                    if 1 in steps:
                        scores(t + 1)
                    if 0 in steps:
                        qkT(t + 2)
                    if 2 in steps:
                        attend(t)

                for s in (xT_ps, qkT_ps, s_ps, pT_ps, yT_ps, pr_ps, y_ps):
                    pe.sem_inc(s, 1)
                pe.wait_ge(mask_ready, 1)
                keep_warm(pe, AT_WARM[2], B_S)
                pe.wait_ge(loaded["atw"], 16)
                all_turns(pe, turn)

            @block.scalar
            def _(act):
                def v_copy(i):
                    act.wait_ge(qkv_ps, i + 1)
                    act.wait_ge(at_pre, 1)
                    act.copy(one(v_all, i), bank(B_XV, EMB, V_AT)).then_inc(v_ready, 1)

                def q_copy(i):
                    act.wait_ge(qkT_ps, i + 2)
                    act.wait_ge(s_ps, i + 1)
                    act.copy(qT_a, bank(B_QKT, P))
                    act.copy(qT_b, bank(B_QKT, P, P)[0:EB]).then_inc(q_ready, 1)

                def softmax(i):
                    act.wait_ge(sh, i + 1)
                    act.activation(esink, hsum, ACT.Exp).then_inc(esink_done, 1)
                    act.activation(prob, prob, ACT.Exp).then_inc(p_ready, 1)

                def pT_copy(i):
                    act.wait_ge(pT_ps, i + 2)
                    act.wait_ge(y_ps, i + 1)
                    dst = pT.rearrange("p (j two) q -> p j two q", two=2)
                    for two in range(2):
                        src = psum[two * TOK:(two + 1) * TOK, B_PT * 512:B_PT * 512 + NH // 2 * P].rearrange("p (j q) -> p j q", j=NH // 2)
                        act.copy(dst[0:TOK, :, two, 0:TOK], src[:, :, 0:TOK])
                        ins = act.copy(dst[TOK:P, :, two, TOK:P], src[:, :, TOK:P])
                    ins.then_inc(pT_sb, 1)

                def yT_copy(i):
                    act.wait_ge(yT_ps, i + 2)
                    act.wait_ge(pr_ps, i + 1)
                    act.copy(yT_a, bank(B_Y, P, YT_A))
                    act.copy(yT_b[0:EB], bank(B_Y, P, YT_B)[0:EB]).then_inc(yT_sb, 1)

                def turn(t, steps, inner=False):
                    if 2 in steps:
                        pT_copy(t)
                    if 3 in steps:
                        yT_copy(t - 1)
                    if 0 in steps:
                        v_copy(t + 2)
                        q_copy(t + 2)
                    if 1 in steps:
                        softmax(t + 1)

                act.preload_act_table(ACT.Exp)
                act.sem_inc(v_ready, 1)
                act.wait_ge(at_pre, 1)
                all_turns(act, turn)

            @block.vector
            def _(dve):
                link = Chain(dve, at_chain)

                def one2(x, i):
                    return x[:, i:i + 1] if isinstance(i, int) else x[:, bass.ds(i, 1)]

                def norm(i):
                    dve.wait_ge(xT_ps, i + 1)
                    dve.tensor_scalar(xn, one(h, i), one2(ln_mean, i), one2(ln_rstd, i), ALU.subtract, ALU.mult).then_inc(xn_ready, 1)

                def xT_copy(i):
                    dve.wait_ge(xT_ps, i + 2)
                    dve.wait_ge(qkT_ps, i + 1)
                    dve.tensor_scalar(xT_a, bank(B_XV, P, X_A), V("nscale")[:, 0:1], V("nbias")[:, 0:1], ALU.mult, ALU.add)
                    dve.tensor_scalar(xT_b[0:EB], bank(B_XV, P, X_B)[0:EB], V("nscale", EB)[:, 1:2], V("nbias", EB)[:, 1:2],
                                      ALU.mult, ALU.add).then_inc(xT_sb, 1)

                def rotate(i):
                    dve.wait_ge(qkv_ps, i + 1)
                    dve.wait_ge(qkT_ps, i + 1)
                    g = 2 * NH
                    x = bank(B_QK, 2 * EMB).rearrange("p (g j two) -> p g j two", g=g, two=2)
                    full = bank(B_QK, 2 * EMB).rearrange("p (g f) -> p g f", g=g)
                    t4 = rot_t.rearrange("p (g j two) -> p g j two", g=g, two=2)
                    cos = C("cos2").unsqueeze(1).to_broadcast([P, g, HD])
                    sin = C("sin").unsqueeze(1).to_broadcast([P, g, HD // 2])
                    nsin = C("nsin").unsqueeze(1).to_broadcast([P, g, HD // 2])
                    dve.tensor_tensor(qk_r.rearrange("p (g f) -> p g f", g=g), full, cos, ALU.mult)
                    dve.tensor_tensor(t4[:, :, :, 0], x[:, :, :, 1], nsin, ALU.mult)
                    dve.tensor_tensor(t4[:, :, :, 1], x[:, :, :, 0], sin, ALU.mult).then_inc(rot_ready, 1)

                def k_spread(i):
                    dve.wait_ge(q_ready, i + 1)
                    for dst, src, n, rows in ((k_a, bank(B_QKT, P, 2 * P), NHA, P), (k_b, bank(B_QKT, P, 3 * P)[0:EB], NHB, EB)):
                        s = src.rearrange("p (b k) -> p b k", b=2).unsqueeze(2).to_broadcast([rows, 2, n, TOK])
                        w = C("kmask", rows)[:, 0:n].unsqueeze(1).unsqueeze(3).to_broadcast([rows, 2, n, TOK])
                        ins = dve.tensor_tensor(dst, s, w, ALU.mult)
                    ins.then_inc(qk_ready, 1)

                def softmax(i):
                    dve.wait_ge(s_ps, i + 2)
                    dve.wait_ge(pT_ps, i + 1)
                    s = psum[:, B_S * 512:B_S * 512 + NH * TOK].rearrange("p (g k) -> p g k", g=NH)
                    link(dve.tensor_reduce(hmax, s, AX, ALU.max))
                    link.sync()
                    link(dve.tensor_tensor(hmax, hmax, V("sinks"), ALU.max))
                    link.sync()
                    link(dve.tensor_tensor(hsum, V("sinks"), hmax, ALU.subtract))
                    dve.tensor_tensor(prob, s, hmax.unsqueeze(2).to_broadcast([P, NH, TOK]), ALU.subtract).then_inc(sh, 1)

                def sums(i):
                    dve.wait_ge(p_ready, i + 1)
                    link(dve.tensor_reduce(hsum, prob, AX, ALU.add))
                    link.sync()
                    link(dve.tensor_tensor(hsum, hsum, esink, ALU.add))
                    link.sync()
                    link(dve.reciprocal(rinv, hsum))
                    link.sync()

                def y_norm(i):
                    dve.wait_ge(y_ps, i + 2)
                    dve.wait_ge(yT_ps, i + 1)
                    dve.tensor_tensor(yn.rearrange("p (g f) -> p g f", g=NH), bank(B_Y, EMB).rearrange("p (g f) -> p g f", g=NH),
                                      rinv.unsqueeze(2).to_broadcast([P, NH, HD]), ALU.mult).then_inc(y_ready, 1)

                def residual(i):
                    dve.wait_ge(pr_ps, i + 2)
                    dve.scalar_tensor_tensor(out=h_new[:, :], in0=bank(B_Y, EMB), scalar=V("rezero"), in1=one(h, i),
                                             op0=ALU.mult, op1=ALU.add).then_inc(pr_read, 1)
                    dve.wait_ge(pr_read, i + 2)
                    row_stats(dve, link, h_new[:, :], i)

                def turn(t, steps, inner=False):
                    if 3 in steps:
                        y_norm(t - 1)
                    if 0 in steps:
                        xT_copy(t + 2)
                    if 2 in steps:
                        if 3 in steps:
                            dve.wait_ge(y_ready, t)
                        sums(t)
                    if 0 in steps:
                        if inner or t + 3 < NT:
                            norm(t + 3)
                        rotate(t + 2)
                    if 3 in steps:
                        residual(t - 1)
                    if 1 in steps:
                        softmax(t + 1)
                    if 0 in steps:
                        k_spread(t + 2)

                dve.wait_ge(tok_rstd, 1)
                norm(0)
                dve.wait_ge(loaded["vec"], 16)
                link(dve.tensor_copy(ident16, ident))
                link(dve.tensor_copy(causal16, C("causal")))
                link.sync()
                dve.sem_inc(mask_ready, 1)
                link(dve.memset(xT_b[EB:EB + 1], 1.0))
                link(dve.memset(yT_b[EB:EB + 1], 1.0))
                link.sync()
                dve.sem_inc(pr_read, 1)
                dve.wait_ge(at_rstd, 1)
                all_turns(dve, turn, link, 2 * (3 + 3 + 4))
                link.sync()

        def top1_moe(name, src, sub, x_col, gate_w, gate_rows, up, up_rows, down_w, act_fn, gated, u, buf,
                     weights_in, also_sync=None):
            def s(n):
                return stage_sem(f"{name}_{n}")

            reg = Region(*buf)
            xn_all = reg.take(NT * EMB).rearrange("p (i n) -> p i n", i=NT)
            xb_all = reg.take(NBLK * EMB).rearrange("p (b n) -> p b n", b=NBLK)
            tail_cur = reg.take(HID)[EB:P] if gated else None
            xT_all = reg.buf[:, reg.at - NBLK * EMB:reg.at - NBLK * EMB + 2 * NTOK]
            xTs_a, xTs_b = xT_all[:, 0:NTOK], xT_all[:, NTOK:2 * NTOK]
            x_cur = x_cur2
            NJ = NT // 2
            B_XA, B_XB, B_RANK, B_TOT, B_L = 0, 2, 4, 5, 6
            B_H1, B_H3, B_HT, B_Y, B_XT = 0, 2, 4, 6, 7
            chain, pre, rstd, xn_rdy, xT_ps, xTa_sb, xTb_sb, lg_ps, oh_rdy, rank_ps, route_rdy, ones_rdy, hu_rdy = (
                s(n) for n in ("chain", "pre", "rstd", "xn", "xT_ps", "xTa_sb", "xTb_sb", "lg_ps", "onehot", "rank_ps", "routed", "ones",
                               "h_u"))
            scat, sorted_in, cur_rdy, bT_ps, bT_sb, up_ps, hid_rdy, hT_ps, hT_v, hT_a, y_ps, y_rdy, y_st, ex_in, ex_out = (
                s(n) for n in ("scattered", "sorted_in", "cur", "bT_ps", "bT_sb", "up_ps", "hid", "hT_ps", "hT_v", "hT_a",
                               "y_ps", "y_rdy", "y_stored", "exp_in", "exp_out"))
            tail_rdy = s("tail_rdy")
            act_rdy, scaled, h_rdy, bn_rdy = s("act_rdy"), s("scaled"), s("h_rdy"), s("bn_rdy")
            gath = [s(f"gathered{i}") for i in range(NT)]
            nL = gate_rows

            def expert(eng, j):
                return eng.value_load(eid[0:1, j:j + 1] if isinstance(j, int) else eid[0:1, bass.ds(j, 1)],
                                      min_val=0, max_val=NEXP - 1)

            with nc.Block() as block:
                @block.sync
                def _(sp):
                    if also_sync:
                        also_sync(sp)
                    sp.wait_ge(scat, 16 * NT)
                    sp.dma_start(xb_all, x_sorted.rearrange("(b p) n -> p b n", p=P)).then_inc(sorted_in, 16)
                    with sp.Fori(0, NBLK) as j:
                        sp.wait_ge(y_rdy, j + 2)
                        sp.dma_start(y_sorted[bass.ds(j * P, P), :], one(xb_all, j)).then_inc(y_st, 16)

                @block.gpsimd
                def _(pool):
                    pool.wait_ge(pre, 1)
                    pool.tensor_tensor(row_scale[:, :], ln_tmp[:, :], C("neg_half"), ALU.pow).then_inc(rstd, 1)
                    if not gated:
                        pool.wait_ge(rstd, 1)
                        pool.memset(xTs_b[EB:EB + 1], 1.0).then_inc(ones_rdy, 1)
                    for z_ in zeroed:
                        pool.wait_ge(z_, 16)
                    pool.wait_ge(route_rdy, 1)
                    for i in range(NT):
                        pool.indirect_dma_start(x_sorted, bass.IndirectOffsetOnAxis(ap=slot_u[:, i:i + 1], axis=0),
                                                xn_all[:, i, :], None).then_inc(scat, 16)
                    if gated:
                        for i in range(NT):
                            pool.tensor_tensor(h[:, i, :], h[:, i, :], u[:, i, :], ALU.add).then_inc(hu_rdy, 1)
                    pool.wait_ge(y_st, 16 * NBLK)
                    for i in range(NT):
                        pool.indirect_dma_start(xn_all[:, i, :], None, y_sorted,
                                                bass.IndirectOffsetOnAxis(ap=slot_u[:, i:i + 1], axis=0)).then_inc(gath[i], 16)

                @block.tensor
                def _(pe):
                    keep_warm(pe, 12, 7)
                    for i in range(NT):
                        pe.wait_ge(xn_rdy, i + 1)
                        pe.transpose(bank(B_XA + i // NJ, P, (i % NJ) * P), xn_all[:, i, 0:P], ident)
                        pe.transpose(bank(B_XB + i // NJ, P, (i % NJ) * P)[0:EB], xn_all[:, i, P:EMB], ident).then_inc(xT_ps, 1)
                    if not gated:
                        pe.wait_ge(ones_rdy, 1)
                    for i in range(NT):
                        if i % NJ == 0:
                            pe.wait_ge(xTa_sb, i // NJ + 1)
                            pe.wait_ge(xTb_sb, i // NJ + 1)
                        t = slice(i * P, (i + 1) * P)
                        pe.matmul(bank(B_L, NEXP, i * NEXP), xTs_a[:, t], W(gate_w + "_a"), start=True, stop=False)
                        mm = pe.matmul(bank(B_L, NEXP, i * NEXP), xTs_b[0:nL, t], W(gate_w + "_b", nL), start=False, stop=True)
                    mm.then_inc(lg_ps, 1)
                    pe.wait_ge(oh_rdy, 1)
                    oh_et = oh.rearrange("p (t e) -> p e t", e=NEXP)
                    pe.matmul(bank(B_RANK, NEXP * NT), C("upper"), oh_et, start=True, stop=True)
                    pe.matmul(bank(B_TOT, NEXP * NT), C("ones"), oh_et, start=True, stop=True).then_inc(rank_ps, 1)

                    def rows_T(j):
                        pe.wait_ge(cur_rdy, j + 1)
                        pe.wait_ge(bT_sb, j + 1)
                        pe.transpose(bank(B_XT, P), x_cur[:, 0:P], ident)
                        nt = P if gated else EB
                        pe.transpose(bank(B_XT, P, P)[0:nt], x_cur[:, P:P + nt], ident).then_inc(bT_ps, 1)

                    def up_proj(j, e):
                        pe.wait_ge(bT_sb, j + 2)
                        pe.wait_ge(hid_rdy, j + 1)
                        if gated:
                            pe.wait_ge(tail_rdy, j + 1)
                        for n0, n in ((0, 512), (512, 256)):
                            o = [psum[:, b_ * 512 + n0:b_ * 512 + n0 + n] for b_ in (B_H1, B_H3)]
                            for k, (wa, wb) in enumerate(up):
                                pe.matmul(o[k], xT_a, one(wa, e)[:, n0:n0 + n], start=True, stop=False)
                            for k, (wa, wb) in enumerate(up):
                                rows = slice(k * EB, k * EB + up_rows)
                                w = tail_cur if k else one(wb, e)
                                mm = pe.matmul(o[k], xT_b[rows], w[:, n0:n0 + n], start=False, stop=True)
                        mm.then_inc(up_ps, 1)

                    def hidden_T(j):
                        pe.wait_ge(hid_rdy, j + 2)
                        for c in range(NFC):
                            tr = pe.transpose(psum[:, B_HT * 512 + c * P:B_HT * 512 + (c + 1) * P], hid[:, c * P:(c + 1) * P], ident)
                        tr.then_inc(hT_ps, 1)

                    def down_proj(j, e):
                        pe.wait_ge(hT_v, j + 1)
                        pe.wait_ge(hT_a, j + 1)
                        pe.wait_ge(y_rdy, j + 1)
                        if not gated:
                            pe.matmul(bank(B_Y, EMB), C("ones", 1), one(b2_row.rearrange("p (e n) -> p e n", e=NEXP), e),
                                      start=True, stop=False)
                        w2 = down_w[:, bass.ds(e, 1)].rearrange("p o c n -> p (o c) n")
                        for c in range(NFC):
                            mm = pe.matmul(bank(B_Y, EMB), hidT[:, c * P:(c + 1) * P], w2[:, c, :],
                                           start=(gated and c == 0), stop=(c == NFC - 1))
                        mm.then_inc(y_ps, 1)

                    pe.sem_inc(bT_ps, 1)
                    pe.sem_inc(up_ps, 1)
                    pe.sem_inc(hT_ps, 1)
                    pe.sem_inc(y_ps, 1)
                    rows_T(0)
                    for n in weights_in:
                        pe.wait_ge(loaded[n], 16)
                    up_proj(0, expert(pe, 0))
                    rows_T(1)
                    hidden_T(0)
                    up_proj(1, expert(pe, 1))
                    with pe.Fori(1, NBLK - 1) as j:
                        last, following = expert(pe, j - 1), expert(pe, j + 1)
                        rows_T(j + 1)
                        down_proj(j - 1, last)
                        hidden_T(j)
                        up_proj(j + 1, following)
                    down_proj(NBLK - 2, expert(pe, NBLK - 2))
                    hidden_T(NBLK - 1)
                    down_proj(NBLK - 1, expert(pe, NBLK - 1))

                @block.scalar
                def _(act):
                    def hidden(j):
                        act.wait_ge(up_ps, j + 2)
                        act.wait_ge(hT_ps, j + 1)
                        f = act.activation(hid, psum[:, B_H1 * 512:B_H1 * 512 + HID], act_fn)
                        f.then_inc(act_rdy if gated else hid_rdy, 1)

                    def tail_copy(j):
                        e = expert(act, j)
                        act.copy(tail_cur, one(up[1][1], e)).then_inc(tail_rdy, 1)

                    def hT_copy(j):
                        act.wait_ge(hT_ps, j + 2)
                        act.wait_ge(y_ps, j + 1)
                        act.copy(hidT[:, 512:HID], psum[:, (B_HT + 1) * 512:(B_HT + 1) * 512 + HID - 512]).then_inc(hT_a, 1)

                    for hf in range(2):
                        act.wait_ge(xT_ps, NJ * (hf + 1))
                        b_ = xTs_b[0:EB, hf * HALF:(hf + 1) * HALF]
                        if x_col is None:
                            act.copy(b_, bank(B_XB + hf)[0:EB]).then_inc(xTb_sb, 1)
                        else:
                            act.activation(b_, bank(B_XB + hf)[0:EB], ACT.Identity, scale=x_col[0:EB, 1:2]).then_inc(xTb_sb, 1)
                    if gated:
                        act.wait_ge(ex_in, 1)
                        act.activation(rt[0], rt[0], ACT.Exp).then_inc(ex_out, 1)
                    act.preload_act_table(act_fn)
                    if not gated:
                        act.sem_inc(hid_rdy, 1)
                    if gated:
                        act.wait_ge(route_rdy, 1)
                        for n in weights_in:
                            act.wait_ge(loaded[n], 16)
                        tail_copy(0)
                    with act.Fori(0, NBLK - 1) as j:
                        hidden(j)
                        if gated:
                            tail_copy(j + 1)
                        hT_copy(j)
                    hidden(NBLK - 1)
                    hT_copy(NBLK - 1)

                @block.vector
                def _(dve):
                    link = Chain(dve, chain)

                    def te(x):
                        return x.rearrange("p (t e) -> p t e", e=NEXP)

                    def et(x):
                        return x.rearrange("p (e t) -> p e t", e=NEXP)

                    def over_e(x):
                        return x.unsqueeze(2).to_broadcast([P, NT, NEXP])

                    def over_t(x):
                        return x.unsqueeze(1).to_broadcast([P, NT, NEXP])

                    if sub is not None:
                        link(dve.tensor_scalar(ln_tmp[:, :], stats[:, :, 1], LN_EPS, None, ALU.add))
                        link(dve.tensor_copy(ln_mean[:, :], stats[:, :, 0]))
                    else:
                        link(dve.tensor_tensor(ln_tmp[:, :], stats[:, :, 0], stats[:, :, 0], ALU.mult))
                        link.sync()
                        link(dve.scalar_tensor_tensor(out=ln_tmp[:, :], in0=ln_tmp[:, :], scalar=RMS_EPS, in1=stats[:, :, 1],
                                                      op0=ALU.add, op1=ALU.add))
                    for z_ in zeroed:
                        dve.wait_ge(z_, 16)
                    link(dve.memset(xT_b[EB:EB + 1], 1.0))
                    link.sync()
                    dve.sem_inc(pre, 1)
                    dve.wait_ge(rstd, 1)
                    for i in range(NT):
                        if sub is not None:
                            dve.tensor_scalar(xn_all[:, i, :], src[:, i, :], sub[:, i:i + 1], row_scale[:, i:i + 1],
                                              ALU.subtract, ALU.mult).then_inc(xn_rdy, 1)
                        else:
                            dve.tensor_scalar(xn_all[:, i, :], src[:, i, :], row_scale[:, i:i + 1], None, ALU.mult).then_inc(xn_rdy, 1)
                    for hf in range(2):
                        dve.wait_ge(xT_ps, NJ * (hf + 1))
                        a_ = xTs_a[:, hf * HALF:(hf + 1) * HALF]
                        if x_col is None:
                            dve.tensor_copy(a_, bank(B_XA + hf)).then_inc(xTa_sb, 1)
                        else:
                            dve.tensor_scalar(a_, bank(B_XA + hf), x_col[:, 0:1], None, ALU.mult).then_inc(xTa_sb, 1)
                    dve.wait_ge(lg_ps, 1)
                    link(dve.tensor_copy(logits, bank(B_L, NT * NEXP)))
                    link.sync()
                    v = logits
                    if gated:
                        link(dve.tensor_reduce(mx, te(logits), AX, ALU.max))
                        link.sync()
                        dve.tensor_tensor(te(rt[0]), te(logits), over_e(mx), ALU.subtract).then_inc(ex_in, 1)
                        dve.wait_ge(ex_out, 1)
                        v = rt[0]
                        link(dve.tensor_reduce(gate, te(v), AX, ALU.add))
                        link.sync()
                        link(dve.reciprocal(gate, gate))
                    link(dve.tensor_reduce(mx, te(v), AX, ALU.max))
                    link.sync()
                    if gated:
                        link(dve.tensor_tensor(gate, gate, mx, ALU.mult))
                    link(dve.tensor_tensor(te(rt[1]), te(v), over_e(mx), ALU.is_ge))
                    link.sync()
                    link(dve.scalar_tensor_tensor(out=te(rt[1]), in0=te(rt[1]), scalar=-1000.0, in1=over_t(C("iota_far")),
                                                  op0=ALU.mult, op1=ALU.add))
                    link.sync()
                    link(dve.tensor_reduce(mx, te(rt[1]), AX, ALU.min))
                    link.sync()
                    dve.tensor_tensor(te(oh), over_t(C("iota")), over_e(mx), ALU.is_equal).then_inc(oh_rdy, 1)
                    dve.wait_ge(rank_ps, 1)
                    link(dve.tensor_tensor_scan(rt[0], C("carry"), bank(B_TOT, NEXP * NT), 0.0, ALU.mult, ALU.add))
                    link.sync()
                    link(dve.tensor_tensor(rt[1], rt[0], bank(B_TOT, NEXP * NT), ALU.subtract))
                    link(dve.tensor_tensor(et(rt[2]), et(rt[0])[:, :, NT - 1:NT].to_broadcast([P, NEXP, NT]),
                                           C("by128").unsqueeze(1).to_broadcast([P, NEXP, NT]), ALU.is_gt))
                    link.sync()
                    link(dve.tensor_reduce(blkc, et(rt[2]), AX, ALU.add))
                    link(dve.memset(sb_, 0.0))
                    link.sync()
                    link(dve.tensor_tensor_scan(sb_[:, 1:NEXP + 1], C("ones")[:, 0:NEXP], blkc, 0.0, ALU.mult, ALU.add))
                    link.sync()
                    link(dve.scalar_tensor_tensor(out=et(rt[2]), in0=sb_[:, 0:NEXP].unsqueeze(2).to_broadcast([P, NEXP, NT]),
                                                  scalar=float(P), in1=et(rt[1]), op0=ALU.mult, op1=ALU.add))
                    bl3 = bl.rearrange("p (b e) -> p b e", e=NEXP)[:, :, 1:NEXP]
                    link(dve.tensor_tensor(bl3, C("block").unsqueeze(2).to_broadcast([P, NBLK, NEXP - 1]),
                                           sb_[:, 1:NEXP].unsqueeze(1).to_broadcast([P, NBLK, NEXP - 1]), ALU.is_ge))
                    link.sync()
                    link(dve.tensor_tensor(rt[2], rt[2], bank(B_RANK, NEXP * NT), ALU.add))
                    link(dve.tensor_reduce(eidf, bl3, AX, ALU.add))
                    link.sync()
                    link(dve.tensor_tensor(et(rt[2]), et(rt[2]), oh.rearrange("p (t e) -> p e t", e=NEXP), ALU.mult))
                    link(dve.tensor_copy(eid[:, :], eidf))
                    link.sync()
                    link(dve.tensor_reduce(slotf, rt[2].rearrange("p (e t) -> p t e", e=NEXP), AX, ALU.add))
                    link.sync()
                    link(dve.tensor_copy(slot_u[:, :], slotf))
                    link.sync()
                    dve.sem_inc(route_rdy, 1)

                    def take_rows(j):
                        dve.wait_ge(bT_ps, j + 1)
                        if gated:
                            dve.tensor_scalar(x_cur[:, EMB:2 * P], one(xb_all, j)[:, P:EMB], 1.0, None, ALU.mult)
                        dve.tensor_scalar(x_cur[:, 0:EMB], one(xb_all, j), 1.0, None, ALU.mult).then_inc(cur_rdy, 1)

                    def rows_T(j):
                        dve.wait_ge(bT_ps, j + 2)
                        dve.wait_ge(up_ps, j + 1)
                        if x_col is None:
                            dve.tensor_copy(xT_a, bank(B_XT, P))
                            dve.tensor_copy(xT_b[0:EB], bank(B_XT, P, P)[0:EB]).then_inc(bT_sb, 1)
                        else:
                            dve.tensor_scalar(xT_a, bank(B_XT, P), x_col[:, 0:1], None, ALU.mult)
                            dve.tensor_scalar(xT_b, bank(B_XT, P, P), x_col[:, 1:2], None, ALU.mult).then_inc(bT_sb, 1)

                    def hidden(j):
                        if gated:
                            dve.wait_ge(act_rdy, j + 1)
                            dve.tensor_tensor(hid, hid, psum[:, B_H3 * 512:B_H3 * 512 + HID], ALU.mult).then_inc(hid_rdy, 1)

                    def hT_copy(j):
                        dve.wait_ge(hT_ps, j + 2)
                        dve.wait_ge(y_ps, j + 1)
                        dve.tensor_copy(hidT[:, 0:512], bank(B_HT)).then_inc(hT_v, 1)

                    def result(j):
                        dve.wait_ge(y_ps, j + 2)
                        dve.tensor_scalar(one(xb_all, j), bank(B_Y, EMB), 1.0, None, ALU.mult).then_inc(y_rdy, 1)

                    dve.sem_inc(bT_sb, 1)
                    dve.sem_inc(y_rdy, 1)
                    if gated:
                        dve.sem_inc(hid_rdy, 1)
                    dve.wait_ge(sorted_in, 16)
                    take_rows(0)
                    rows_T(0)
                    take_rows(1)
                    hidden(0)
                    rows_T(1)
                    hT_copy(0)
                    with dve.Fori(1, NBLK - 1) as j:
                        take_rows(j + 1)
                        hidden(j)
                        rows_T(j + 1)
                        result(j - 1)
                        hT_copy(j)
                    hidden(NBLK - 1)
                    result(NBLK - 2)
                    hT_copy(NBLK - 1)
                    result(NBLK - 1)
                    lag = int(gated)
                    for i in range(NT + 2 + lag):
                        if gated and i < NT:
                            dve.wait_ge(gath[i], 16)
                            dve.scalar_tensor_tensor(out=xn_all[:, i, :], in0=xn_all[:, i, :], scalar=gate[:, i:i + 1],
                                                     in1=V("ls_ffn"), op0=ALU.mult, op1=ALU.mult).then_inc(scaled, 1)
                        j = i - lag
                        if 0 <= j < NT:
                            if gated:
                                dve.wait_ge(scaled, j + 1)
                                dve.wait_ge(hu_rdy, j + 1)
                            else:
                                dve.wait_ge(gath[j], 16)
                            dve.tensor_tensor(h[:, j, :], h[:, j, :], xn_all[:, j, :], ALU.add).then_inc(h_rdy, 1)
                        if 0 <= j - 1 < NT:
                            dve.wait_ge(h_rdy, j)
                            dve.bn_stats(bn_all[:, j - 1, :], h[:, j - 1, :]).then_inc(bn_rdy, 1)
                        if 0 <= j - 2 < NT:
                            dve.wait_ge(bn_rdy, j - 1)
                            link(dve.bn_aggr(stats[:, j - 2, :], bn_all[:, j - 2, :]))
                    link.sync()

        a = Region(ring, free0, ring_cols - W13)
        top1_moe("m0", h, ln_mean, None, "g0", EB + 1, [(m0_w1a, m0_w1b)], EB + 1, m0_w2, ACT.Gelu, False, None,
                 (ring, free0, ring_cols - W13), ("moe0", "moe0_b2"))
        new_sems()

        a = Region(ring, 0, 5 * PAIR_W)
        u_all = ring[:, 5 * PAIR_W:5 * PAIR_W + NT * EMB].rearrange("p (i n) -> p i n", i=NT)
        assert 5 * PAIR_W + NT * EMB <= ring_cols - W13
        in_T = a.take(2 * NTOK)
        xnT_a, xnT_b = in_T[:, 0:NTOK], in_T[0:EB, NTOK:2 * NTOK]
        dBu = [in_T[:, c * HALF:(c + 1) * HALF] for c in range(NCH)]
        xc = a.take(NCH * NTOK).rearrange("p (c t) -> p c t", c=NCH)
        z = a.take(NCH * NTOK).rearrange("p (c t) -> p c t", c=NCH)
        delta = a.take(NCH * NTOK).rearrange("p (c t) -> p c t", c=NCH)
        du = a.take(NCH * NTOK).rearrange("p (c t) -> p c t", c=NCH)
        hc_buf = a.take(NCH * HALF)
        dt_sb = hc_buf[0:DTR, 0:NTOK]
        hc = [hc_buf[:, c * HALF:(c + 1) * HALF] for c in range(NCH)]
        hs_buf = a.take(NCH * HALF)
        sp_t = [hs_buf[:, c * HALF:(c + 1) * HALF] for c in range(NCH)]
        hs = [hs_buf[:, c * HALF:(c + 1) * HALF] for c in range(NCH)]
        b_buf = a.take(2 * HALF)
        sp_r = [b_buf[:, c * HALF:(c + 1) * HALF] for c in range(2)]
        b_sb = [b_buf[:, c * HALF:(c + 1) * HALF] for c in range(2)]
        bc3 = a.take(HALF, XPJ).bitcast(BF16)
        sel = a.take(2 * NST * P // 2, XPJ).bitcast(BF16).rearrange("p (s m) -> p s m", s=2 * NST)
        neg_A = a.take(NCH * NST)
        diag_D = a.take(NCH * P).rearrange("p (c m) -> p c m", c=NCH)
        bc_r = hid[:, 0:HALF]
        xn_s = u_all
        NJ = NT // 2
        UNITS = [(hf, c) for hf in range(2) for c in range(NCH)]

        def s(n):
            return stage_sem("ss_" + n)

        A_exp = sem("A_exp")
        (sel_in, chain, pre, pw, xn_rdy, xT_ps, xTa_sb, xTb_sb, xs_ps, xs_rd, z_ps, z_rd, tap, cv_rdy, xc_rdy, bc_ps, bc_rd, dt_ps, ab_rd,
         ex_rdy, ln_rdy, dt_rd, du_rdy) = (s(n) for n in ("sel_in", "chain", "pre", "pow", "xn", "xT_ps", "xTa_sb", "xTb_sb", "xs_ps", "xs_read", "z_ps",
                                          "z_read", "tap", "conv", "xc", "bc_ps", "bc_read", "dt_ps", "abs_read", "exp", "log", "dt_read", "du"))

        def cols(hf):
            return slice(hf * HALF, (hf + 1) * HALF)

        with nc.Block() as block:
            @block.sync
            def _(sp):
                sp.dma_start(sel.bitcast(U16), d["sel"]).then_inc(sel_in, 16)
                sp.wait_ge(sel_in, 16)

            @block.gpsimd
            def _(pool):
                pool.wait_ge(pre, 1)
                pool.tensor_tensor(row_scale[:, :], row_scale[:, :], C("neg_half"), ALU.pow).then_inc(pw, 1)
                pool.tensor_tensor(ln_rstd[:, :], ln_tmp[:, :], C("neg_half"), ALU.pow).then_inc(pw, 1)
                for n, (hf, c) in enumerate(UNITS):
                    pool.wait_ge(dt_rd, n + 1)
                    pool.tensor_tensor(du[:, c, cols(hf)], delta[:, c, cols(hf)], xc[:, c, cols(hf)], ALU.mult).then_inc(du_rdy, 1)

            @block.tensor
            def _(pe):
                keep_warm(pe, 12, 6)
                for i in range(NT):
                    pe.wait_ge(xn_rdy, i + 1)
                    pe.transpose(bank(i // NJ, P, (i % NJ) * P), xn_s[:, i, 0:P], ident)
                    pe.transpose(bank(2 + i // NJ, P, (i % NJ) * P)[0:EB], xn_s[:, i, P:EMB], ident).then_inc(xT_ps, 1)
                pe.wait_ge(loaded["ssw"], 16)
                pe.wait_ge(xTa_sb, 2)
                pe.wait_ge(xTb_sb, 2)

                def in_proj(n, k):
                    ps, rd = ((xs_ps, xs_rd), (z_ps, z_rd))[k]
                    hf, c = UNITS[n]
                    if n >= 2:
                        pe.wait_ge(rd, n - 1)
                    o = bank(2 + 2 * k + n % 2)
                    w0 = (k * NCH + c) * P
                    pe.matmul(o, WS("in_a")[:, w0:w0 + P], xnT_a[:, cols(hf)], start=True, stop=False)
                    pe.matmul(o, WS("in_b", EB)[:, w0:w0 + P], xnT_b[:, cols(hf)], start=False, stop=True).then_inc(ps, 1)

                def x_proj(hf):
                    pe.wait_ge(xc_rdy, NCH * (hf + 1))
                    for c in range(NCH):
                        mm = pe.matmul(bank(6 + hf)[0:XPJ], WS("x")[:, c * XPJ:(c + 1) * XPJ], xc[:, c, cols(hf)],
                                       start=(c == 0), stop=(c == NCH - 1))
                    mm.then_inc(bc_ps, 1)

                in_proj(0, 0)
                in_proj(1, 0)
                for n in range(3):
                    in_proj(n, 1)
                    in_proj(n + 2, 0)
                x_proj(0)
                in_proj(5, 0)
                for n in range(3, 6):
                    in_proj(n, 1)
                x_proj(1)
                for n, (hf, c) in enumerate(UNITS):
                    pe.wait_ge(bc_rd, hf + 1)
                    if n == 0:
                        pe.wait_ge(xs_rd, 6)
                    if n >= 4:
                        pe.wait_ge(dt_rd, n - 3)
                    pe.matmul(bank(n % 4), WS("dt", DTR)[:, c * P:(c + 1) * P], dt_sb[:, cols(hf)],
                              start=True, stop=True).then_inc(dt_ps, 1)

            @block.scalar
            def _(act):
                def z_silu(n):
                    hf, c = UNITS[n]
                    act.wait_ge(z_ps, n + 1)
                    act.activation(z[:, c, cols(hf)], bank(4 + n % 2), ACT.Silu).then_inc(z_rd, 1)

                def first_tap(n):
                    hf, c = UNITS[n]
                    act.wait_ge(xs_ps, n + 1)
                    act.activation(xc[:, c, cols(hf)], bank(2 + n % 2), ACT.Identity, scale=V("conv_w")[:, 4 * c + 3:4 * c + 4],
                                   bias=V("conv_b")[:, c:c + 1]).then_inc(tap, 1)

                def x_silu(n):
                    hf, c = UNITS[n]
                    act.wait_ge(cv_rdy, n + 1)
                    act.activation(xc[:, c, cols(hf)], xc[:, c, cols(hf)], ACT.Silu).then_inc(xc_rdy, 1)

                act.activation(neg_A, V("A_log"), ACT.Exp).then_inc(A_exp, 1)
                act.preload_act_table(ACT.Silu)
                for hf in range(2):
                    act.wait_ge(xT_ps, NJ * (hf + 1))
                    act.activation(xnT_b[:, cols(hf)], bank(2 + hf)[0:EB], ACT.Identity, scale=V("norm1", EB)[:, 1:2]).then_inc(xTb_sb, 1)
                first_tap(0)
                for n in range(4):
                    first_tap(n + 1)
                    if n:
                        z_silu(n - 1)
                    x_silu(n)
                first_tap(5)
                x_silu(4)
                z_silu(3)
                x_silu(5)
                z_silu(4)
                z_silu(5)
                act.preload_act_table_set("natural_log_exp_and_others")
                NU = len(UNITS)
                for n in range(NU + 2):
                    if n < NU:
                        act.wait_ge(dt_ps, n + 1)
                        if n >= 3:
                            act.wait_ge(dt_rd, n - 2)
                        c = UNITS[n][1]
                        act.activation(sp_t[n % 3], bank(n % 4), ACT.Abs, bias=V("dt_b")[:, c:c + 1]).then_inc(ab_rd, 1)
                    if 0 <= n - 1 < NU:
                        act.wait_ge(ab_rd, n)
                        act.activation(sp_t[(n - 1) % 3], sp_t[(n - 1) % 3], ACT.Exp, scale=-1.0).then_inc(ex_rdy, 1)
                    if 0 <= n - 2 < NU:
                        act.wait_ge(ex_rdy, n - 1)
                        act.activation(sp_t[(n - 2) % 3], sp_t[(n - 2) % 3], ACT.Ln, bias=1.0).then_inc(ln_rdy, 1)

            @block.vector
            def _(dve):
                link = Chain(dve, chain)
                ln_scalars(dve, link)
                link(dve.scalar_tensor_tensor(out=row_scale[:, :], in0=ln_tmp[:, :], scalar=RMS_EPS, in1=stats[:, :, 1],
                                              op0=ALU.mult, op1=ALU.add))
                link.sync()
                dve.sem_inc(pre, 1)
                dve.wait_ge(pw, 1)
                for i in range(NT):
                    dve.tensor_scalar(xn_s[:, i, :], h[:, i, :], ln_mean[:, i:i + 1], row_scale[:, i:i + 1],
                                      ALU.subtract, ALU.mult).then_inc(xn_rdy, 1)
                for hf in range(2):
                    dve.wait_ge(xT_ps, NJ * (hf + 1))
                    dve.tensor_scalar(xnT_a[:, cols(hf)], bank(hf), V("norm1")[:, 0:1], None, ALU.mult).then_inc(xTa_sb, 1)
                dve.wait_ge(A_exp, 1)
                link(dve.tensor_scalar(neg_A, neg_A, -1.0, None, ALU.mult))
                for c in range(NCH):
                    link(dve.tensor_scalar(diag_D[:, c, :], ident, V("D")[:, c:c + 1], None, ALU.mult))

                def conv(n):
                    hf, c = UNITS[n]
                    x3 = bank(2 + n % 2).rearrange("p (b t) -> p b t", t=TOK)
                    o3 = xc[:, c, cols(hf)].rearrange("p (b t) -> p b t", t=TOK)
                    dve.wait_ge(tap, n + 1)
                    for k in (2, 1, 0):
                        lag = 3 - k
                        link(dve.scalar_tensor_tensor(
                            out=o3[:, :, lag:TOK], in0=x3[:, :, 0:TOK - lag], scalar=V("conv_w")[:, 4 * c + k:4 * c + k + 1],
                            in1=o3[:, :, lag:TOK], op0=ALU.mult, op1=ALU.add))
                        link.sync()
                    dve.sem_inc(xs_rd, 1)
                    dve.sem_inc(cv_rdy, 1)

                def split(hf):
                    t = cols(hf)
                    dve.wait_ge(bc_ps, hf + 1)
                    link(dve.tensor_copy(dt_sb[:, t], bank(6 + hf)[0:DTR]))
                    bc = bank(6 + hf)[BC0:BC0 + 2 * NST]
                    n2 = 2 * NST
                    link(dve.tensor_copy(bc3[0:n2, t], bc))
                    link.sync()
                    dve.sem_inc(bc_rd, 1)
                    link(dve.tensor_tensor(bc_r[n2:2 * n2], bc, bc3[0:n2, t], ALU.subtract))
                    link.sync()
                    link(dve.tensor_copy(bc3[n2:2 * n2, t], bc_r[n2:2 * n2]))
                    link.sync()
                    link(dve.tensor_tensor(bc3[2 * n2:3 * n2, t], bc_r[n2:2 * n2], bc3[n2:2 * n2, t], ALU.subtract))

                for n in range(5):
                    conv(n)
                split(0)
                conv(5)
                split(1)
                for n, (hf, c) in enumerate(UNITS):
                    t = cols(hf)
                    dve.wait_ge(ab_rd, n + 1)
                    r = sp_r[n % 2]
                    link(dve.tensor_scalar(r, bank(n % 4), V("dt_b")[:, c:c + 1], 0.0, ALU.add, ALU.max))
                    dve.wait_ge(ln_rdy, n + 1)
                    link.sync()
                    dve.tensor_tensor(delta[:, c, t], r, sp_t[n % 3], ALU.add).then_inc(dt_rd, 1)
                link.sync()

        B_DA, B_C, B_B = 3, 5, 7
        (zero_cols, b_ps, b_rd, c_ps, dA_rdy, dBu_rdy, scan_rdy, hc_rdy, y_acc, y_rd) = (
            s(n) for n in ("zero_cols", "b_ps", "b_read", "c_ps", "dA", "dBu", "scan", "hc", "y_acc", "y_read"))
        U = NCH * NST

        with nc.Block() as block:
            @block.tensor
            def _(pe):
                def one_hot(j):
                    w = sel[:, bass.ds(j, 1), :] if not isinstance(j, int) else sel[:, j:j + 1, :]
                    return w.rearrange("p o m -> p (o m)")

                def spread_B(s_, hf):
                    pe.wait_ge(b_rd, s_ + hf * NST + 1)
                    pe.matmul(bank(B_B), one_hot(s_), bc3[:, hf * HALF:(hf + 1) * HALF], start=True, stop=True).then_inc(b_ps, 1)

                def spread_C(s_, hf, odd):
                    pe.wait_ge(hc_rdy, (s_ + hf * NST) * NCH + 3)
                    pe.matmul(bank(B_C + odd), one_hot(s_ + NST), bc3[:, hf * HALF:(hf + 1) * HALF], start=True, stop=True).then_inc(c_ps, 1)

                def add_up(s_, hf):
                    for c in range(NCH):
                        pe.wait_ge(hc_rdy, (s_ + hf * NST) * NCH + c + 7)
                        pe.matmul(bank(c), ident, hc[c], start=False, stop=True, skip_group_check=True).then_inc(y_acc, 1)

                for c in range(NCH):
                    pe.sem_inc(y_acc, 1)
                for hf in range(2):
                    spread_B(0, hf)
                    spread_C(0, hf, 0)
                    spread_B(1, hf)
                    if hf:
                        pe.wait_ge(y_rd, 1)
                    for c in range(NCH):
                        pe.matmul(bank(c), diag_D[:, c, :], xc[:, c, hf * HALF:(hf + 1) * HALF], start=True, stop=True)
                    with pe.Fori(0, NST // 2 - 1) as k:
                        for odd in range(2):
                            spread_C(k * 2 + odd + 1, hf, 1 - odd)
                            spread_B(k * 2 + odd + 2, hf)
                            add_up(k * 2 + odd, hf)
                    spread_C(NST - 1, hf, 1)
                    add_up(NST - 2, hf)
                    add_up(NST - 1, hf)

            @block.scalar
            def _(act):
                def decay(s_, hf, odd):
                    n = hf * NST
                    act.wait_ge(b_ps, s_ + n + 1)
                    act.wait_ge(dBu_rdy, (s_ + n) * NCH + 3)
                    act.copy(b_sb[odd], bank(B_B)).then_inc(b_rd, 1)
                    for c in range(NCH):
                        act.wait_ge(scan_rdy, (s_ + n) * NCH + c + 2)
                        act.wait_ge(A_exp, 1)
                        b = (odd * NCH + c) % 2
                        j = c * NST + s_
                        scale = neg_A[:, j:j + 1] if isinstance(s_, int) else neg_A[:, bass.ds(j, 1)]
                        act.activation(bank(B_DA + b).rearrange("p (b t) -> p b t", t=TOK)[:, :, 1:TOK],
                                       delta[:, c, hf * HALF:(hf + 1) * HALF].rearrange("p (b t) -> p b t", t=TOK)[:, :, 1:TOK],
                                       ACT.Exp, scale=scale).then_inc(dA_rdy, 1)

                act.preload_act_table(ACT.Exp)
                act.sem_inc(b_rd, 1)
                act.wait_ge(zero_cols, 2)
                for hf in range(2):
                    with act.Fori(0, NST // 2) as k:
                        decay(k * 2, hf, 0)
                        decay(k * 2 + 1, hf, 1)

            @block.gpsimd
            def _(pool):
                def inputs(s_, hf, odd):
                    n = hf * NST
                    pool.wait_ge(b_rd, s_ + n + 2)
                    for c in range(NCH):
                        pool.wait_ge(scan_rdy, (s_ + n) * NCH + c + 1)
                        pool.tensor_tensor(dBu[c], du[:, c, hf * HALF:(hf + 1) * HALF], b_sb[odd], ALU.mult).then_inc(dBu_rdy, 1)

                for _ in range(6):
                    pool.sem_inc(dBu_rdy, 1)
                for hf in range(2):
                    with pool.Fori(0, NST // 2) as k:
                        inputs(k * 2, hf, 0)
                        inputs(k * 2 + 1, hf, 1)

            @block.vector
            def _(dve):
                def scan(s_, hf, odd, c):
                    n = (s_ + hf * NST) * NCH + c
                    dve.wait_ge(dA_rdy, n + 1)
                    dve.wait_ge(hc_rdy, n + 4)
                    dve.wait_ge(dBu_rdy, n + 7)
                    dve.tensor_tensor_scan(hs[c], bank(B_DA + (odd * NCH + c) % 2), dBu[c], 0.0, ALU.mult, ALU.add).then_inc(scan_rdy, 1)

                def times_C(s_, hf, odd, c):
                    n = (s_ + hf * NST) * NCH + c
                    dve.wait_ge(c_ps, s_ + hf * NST + 1)
                    dve.wait_ge(y_acc, n + 1)
                    dve.wait_ge(scan_rdy, n + 4)
                    dve.tensor_tensor(hc[c], hs[c], bank(B_C + odd), ALU.mult).then_inc(hc_rdy, 1)

                def state(s_, hf, odd):
                    scan(s_, hf, odd, 0)
                    scan(s_, hf, odd, 1)
                    times_C(s_, hf, odd, 0)
                    scan(s_, hf, odd, 2)
                    times_C(s_, hf, odd, 1)
                    times_C(s_, hf, odd, 2)

                for b in range(2):
                    dve.memset(bank(B_DA + b).rearrange("p (b t) -> p b t", t=TOK)[:, :, 0:1], 0.0).then_inc(zero_cols, 1)
                for _ in range(3):
                    dve.sem_inc(scan_rdy, 1)
                for _ in range(6):
                    dve.sem_inc(hc_rdy, 1)
                for hf in range(2):
                    with dve.Fori(0, NST // 2) as k:
                        state(k * 2, hf, 0)
                        state(k * 2 + 1, hf, 1)
                    dve.wait_ge(y_acc, 3 + U * (hf + 1))
                    for c in range(NCH):
                        t = slice(hf * HALF, (hf + 1) * HALF)
                        ins = dve.tensor_tensor(z[:, c, t], z[:, c, t], bank(c), ALU.mult)
                    ins.then_inc(y_rd, 1)

        chain2, o_ps, o_rd, hn_rdy, u_rdy, bn_rdy = (s(n) for n in ("chain2", "o_ps", "o_read", "hn", "u", "bn"))
        hn_all = in_T[:, 0:NT * EMB].rearrange("p (i n) -> p i n", i=NT)
        with nc.Block() as block:
            @block.tensor
            def _(pe):
                for i in range(NT):
                    if i >= 2:
                        pe.wait_ge(o_rd, i - 1)
                    for c in range(NCH):
                        mm = pe.matmul(bank(i % 2, EMB), z[:, c, i * P:(i + 1) * P], WS("out")[:, c * EMB:(c + 1) * EMB],
                                       start=(c == 0), stop=(c == NCH - 1))
                    mm.then_inc(o_ps, 1)

            @block.gpsimd
            def _(pool):
                for i in range(NT):
                    pool.tensor_scalar(hn_all[:, i, :], h[:, i, :], ln_mean[:, i:i + 1], ln_rstd[:, i:i + 1],
                                       ALU.subtract, ALU.mult).then_inc(hn_rdy, 1)

            @block.vector
            def _(dve):
                link = Chain(dve, chain2)
                for i in range(NT + 3):
                    if i < NT:
                        dve.wait_ge(o_ps, i + 1)
                        dve.tensor_tensor(u_all[:, i, :], bank(i % 2, EMB), V("ls_ssm"), ALU.mult).then_inc(o_rd, 1)
                    if 0 <= i - 1 < NT:
                        dve.wait_ge(o_rd, i)
                        dve.wait_ge(hn_rdy, i)
                        dve.tensor_tensor(u_all[:, i - 1, :], u_all[:, i - 1, :], hn_all[:, i - 1, :], ALU.add).then_inc(u_rdy, 1)
                    if 0 <= i - 2 < NT:
                        dve.wait_ge(u_rdy, i - 1)
                        dve.bn_stats(bn_all[:, i - 2, :], u_all[:, i - 2, :]).then_inc(bn_rdy, 1)
                    if 0 <= i - 3 < NT:
                        dve.wait_ge(bn_rdy, i - 2)
                        link(dve.bn_aggr(stats[:, i - 3, :], bn_all[:, i - 3, :]))
                link.sync()

        def s(n):
            return stage_sem("so_" + n)

        def group_part(odd, part):
            at = (odd * 2 + part) * QP * PART_W
            return ring[:, at:at + QP * PART_W]

        def w1_of(odd, q):
            w = group_part(odd, 0)[:, q * PART_W:(q + 1) * PART_W]
            return w[:, 0:2 * HID].rearrange("p (e f) -> p e f", e=2), w[:, 2 * HID:3 * HID]

        def w2_of(odd, q):
            return group_part(odd, 1)[:, q * PART_W:(q + 1) * PART_W].rearrange("p (e c n) -> p e c n", e=2, c=NFC)

        t = Region(tail, 0, NEXP * NFC * EMB + NSSW)
        x_a = t.take(NX * 2 * NIMG)
        x_b = t.take(NX * NIMG)
        xT_all = t.take(2 * NTOK)
        xTs_a, xTs_b = xT_all[:, 0:NTOK], xT_all[0:EB, NTOK:2 * NTOK]
        c_T = t.take(HALF)
        phi_s = t.take(1)
        phi_n = t.take(1)
        xg_a = [xT_all[:, k * GRP * 2 * NIMG:(k + 1) * GRP * 2 * NIMG] for k in range(2)]
        xg_b = [xT_all[:, (4 + k) * GRP * NIMG:(5 + k) * GRP * NIMG] for k in range(2)]
        x_b0 = t.take(HID + EMB)
        xbias = [x_b0[0:GRP], xT_all[0:GRP, 6 * GRP * NIMG:6 * GRP * NIMG + HID + EMB]]
        sq_a, sq_b = x_b0[:, HALF:HALF + NX], x_b0[0:EB, HALF + NX:HALF + 2 * NX]
        xn_s = atw[:, 0:NT * EMB].rearrange("p (i n) -> p i n", i=NT)
        assert ATW["g0_a"][0] >= NT * EMB
        x_a4 = x_a.rearrange("p (r a c) -> p r a c", r=NPAIR, a=2)
        x_b3 = x_b.rearrange("p (r c) -> p r c", r=NPAIR)
        lgT = hid[:, 0:HALF]
        ce = hidT[:, 0:HALF]
        d_sb = x_b0[:, 0:HALF]
        cm, cs = oh[:, 0:8], oh[:, 8:16]
        dm, dsum = oh[:, 16:24], oh[:, 24:32]
        part_in = [[sem(f"{w}_group{k}_in") for w in ("w1", "w2")] for k in range(2)]

        def load_part(sp, g, odd, part):
            src = d["groups"][part, g] if isinstance(g, int) else d["groups"][part, bass.ds(g, 1)].rearrange("o p f -> (o p) f")
            sp.dma_start(group_part(odd, part), src).then_inc(part_in[odd][part], 16)

        def first_group(sp):
            for part in range(2):
                load_part(sp, 0, 0, part)

        top1_moe("m1", u_all, None, V("norm2"), "g1", EB, [(m1_w1a, m1_w1b), (m1_w3a, m1_w3b)], EB, m1_w2, ACT.Silu, True, u_all,
                 (ring, 4 * PAIR_W, 5 * PAIR_W), ("moe1_w13", "moe1_w2"), first_group)
        new_sems()
        (chain, pre, pw, phi_sq, phi_ps, xn_rdy, xT_ps, xTa_sb, xTb_sb, lgT_ps, lgT_sb, lg_ps, c_sh, c_exp, d_sh, d_exp, c_rdy, d_rdy,
         cT_ps, d_ps, d_cp, xs_ps, zx, sp_a) = (
            s(n) for n in ("chain", "pre", "pow", "phi_sq", "phi_ps", "xn", "xT_ps", "xTa_sb", "xTb_sb", "lgT_ps", "lgT_sb", "lg_ps",
                           "c_shift", "c_exp", "d_shift", "d_exp", "c_rdy", "d_rdy", "cT_ps", "d_ps", "d_copy", "xs_ps", "zeroed",
                           "spread_act"))

        NJ = NT // 2
        B_XA, B_XB, B_LGT, B_LG, B_CT, B_D, B_PHI = 0, 2, 4, 5, 6, 7, 6
        with nc.Block() as block:
            @block.sync
            def _(sp):
                for part in range(2):
                    load_part(sp, 1, 1, part)

            @block.gpsimd
            def _(pool):
                pool.wait_ge(pre, 1)
                pool.tensor_tensor(ln_rstd[:, :], ln_tmp[:, :], C("neg_half"), ALU.pow).then_inc(pw, 1)
                pool.wait_ge(pre, 2)
                pool.tensor_tensor(row_scale[:, :], row_scale[:, :], C("half"), ALU.pow).then_inc(pw, 1)
                pool.wait_ge(phi_ps, 2)
                pool.tensor_tensor(phi_s, phi_n, C("half")[:, 0:1], ALU.pow).then_inc(pw, 1)
                pool.memset(x_a, 0.0).then_inc(zx, 1)
                pool.memset(x_b, 0.0).then_inc(zx, 1)

            @block.tensor
            def _(pe):
                pe.wait_ge(phi_sq, 1)
                for hf in range(2):
                    o = bank(B_PHI, 1)[hf * NX:(hf + 1) * NX]
                    pe.matmul(o, sq_a, C("ones")[:, 0:1], start=True, stop=False)
                    mm = pe.matmul(o, sq_b, C("ones", EB)[:, 0:1], start=False, stop=True)
                mm.then_inc(phi_ps, 1)
                keep_warm(pe, 16, B_LG)
                for i in range(NT):
                    pe.wait_ge(xn_rdy, i + 1)
                    pe.transpose(bank(B_XA + i // NJ, P, (i % NJ) * P), xn_s[:, i, 0:P], ident)
                    pe.transpose(bank(B_XB + i // NJ, P, (i % NJ) * P)[0:EB], xn_s[:, i, P:EMB], ident).then_inc(xT_ps, 1)
                pe.wait_ge(xTa_sb, 2)
                pe.wait_ge(xTb_sb, 2)
                for w, x, first in ((W("phi_a"), xTs_a, True), (W("phi_b", EB), xTs_b, False)):
                    for hf in range(2):
                        mm = pe.matmul(bank(B_LGT)[hf * NX:(hf + 1) * NX], w, x[:, hf * HALF:(hf + 1) * HALF],
                                       start=first, stop=not first)
                mm.then_inc(lgT_ps, 1)
                pe.wait_ge(lgT_sb, 1)
                for j in range(NJ):
                    tr = pe.transpose(bank(B_LG, P, j * P), lgT[:, j * P:(j + 1) * P], ident)
                tr.then_inc(lg_ps, 1)
                pe.wait_ge(d_rdy, 1)
                for j in range(NJ):
                    tr = pe.transpose(bank(B_D, P, j * P), lgT[:, j * P:(j + 1) * P], ident)
                tr.then_inc(d_ps, 1)
                pe.wait_ge(d_cp, 1)
                for hf in range(2):
                    for j in range(NJ):
                        for b in range(2):
                            i, rows, o = hf * NJ + j, slice(b * TOK, (b + 1) * TOK), 2 * hf + b
                            x, w = xn_s[rows, i], d_sb[rows, (2 * j + hf) * NX:(2 * j + hf + 1) * NX]
                            w2 = w.rearrange("p (r a) -> p r a", a=2)
                            pe.matmul(bank(o, NX, j * NX), x[:, 0:P], w, start=True, stop=True)
                            for a_ in range(2):
                                mm = pe.matmul(bank(o, NPAIR, 4 * NX + j * NPAIR)[a_ * EB:(a_ + 1) * EB], x[:, P:EMB], w2[:, :, a_],
                                               start=True, stop=True)
                    mm.then_inc(xs_ps, 1)
                pe.wait_ge(c_rdy, 1)
                for j in range(NJ):
                    tr = pe.transpose(bank(B_CT, P, j * P), ce[:, j * P:(j + 1) * P], ident)
                tr.then_inc(cT_ps, 1)

            def spread(hf, copy):
                for b in range(2):
                    src = bank(2 * hf + b, 4 * NX).rearrange("p (j r a) -> p a r j", j=4, a=2)
                    srb = bank(2 * hf + b, 4 * NPAIR, 4 * NX).rearrange("p (j r) -> p r j", j=4)
                    for a_ in range(2):
                        at = a_ * NIMG + hf * HIMG + b
                        end = at + HIMG - 1
                        copy(x_a4[:, :, a_, at:end:2], src[:, a_])
                        ins = copy(x_b3[a_ * EB:(a_ + 1) * EB, :, at:end:2], srb[a_ * EB:(a_ + 1) * EB])
                return ins

            @block.scalar
            def _(act):
                act.preload_act_table(ACT.Exp)
                for hf in range(2):
                    act.wait_ge(xT_ps, NJ * (hf + 1))
                    act.copy(xTs_b[:, hf * HALF:(hf + 1) * HALF], bank(B_XB + hf)[0:EB]).then_inc(xTb_sb, 1)
                act.wait_ge(d_sh, 1)
                act.activation(lgT, lgT, ACT.Exp).then_inc(d_exp, 1)
                act.wait_ge(c_sh, 1)
                act.activation(ce, ce, ACT.Exp).then_inc(c_exp, 1)
                act.wait_ge(zx, 2)
                act.wait_ge(xs_ps, 2)
                spread(1, act.copy).then_inc(sp_a, 1)
                act.wait_ge(cT_ps, 1)
                act.copy(c_T, bank(B_CT)).then_inc(sp_a, 1)

            @block.vector
            def _(dve):
                link = Chain(dve, chain)
                link(dve.tensor_tensor(sq_a, W("phi_a"), W("phi_a"), ALU.mult))
                link(dve.tensor_tensor(sq_b, W("phi_b", EB), W("phi_b", EB), ALU.mult))
                ln_scalars(dve, link)
                dve.sem_inc(pre, 1)
                dve.sem_inc(phi_sq, 1)
                dve.wait_ge(phi_ps, 1)
                dve.tensor_copy(phi_n, bank(B_PHI, 1)).then_inc(phi_ps, 1)
                dve.wait_ge(pw, 1)
                link(dve.tensor_tensor(ln_tmp[:, :], ln_rstd[:, :], ln_rstd[:, :], ALU.mult))
                link.sync()
                link(dve.scalar_tensor_tensor(out=row_scale[:, :], in0=ln_tmp[:, :], scalar=float(EMB), in1=stats[:, :, 1],
                                              op0=ALU.mult, op1=ALU.mult))
                link.sync()
                dve.sem_inc(pre, 1)
                dve.wait_ge(pw, 2)
                link(dve.tensor_scalar(row_scale[:, :], row_scale[:, :], L2_EPS, None, ALU.max))
                link.sync()
                link(dve.reciprocal(row_scale[:, :], row_scale[:, :]))
                link.sync()
                link(dve.tensor_tensor(row_scale[:, :], row_scale[:, :], ln_rstd[:, :], ALU.mult))
                link.sync()
                for i in range(NT):
                    dve.tensor_scalar(xn_s[:, i, :], h[:, i, :], ln_mean[:, i:i + 1], row_scale[:, i:i + 1],
                                      ALU.subtract, ALU.mult).then_inc(xn_rdy, 1)
                dve.wait_ge(pw, 3)
                link(dve.tensor_scalar(phi_s, phi_s, L2_EPS, None, ALU.max))
                link.sync()
                link(dve.reciprocal(phi_s, phi_s))
                link.sync()
                link(dve.tensor_tensor(phi_s, phi_s, V("scale"), ALU.mult))
                for hf in range(2):
                    dve.wait_ge(xT_ps, NJ * (hf + 1))
                    dve.tensor_copy(xTs_a[:, hf * HALF:(hf + 1) * HALF], bank(B_XA + hf)).then_inc(xTa_sb, 1)
                link.sync()
                dve.wait_ge(lgT_ps, 1)
                dve.tensor_scalar(lgT, bank(B_LGT), phi_s, None, ALU.mult).then_inc(lgT_sb, 1)

                def im(x):
                    return x.rearrange("p (b m) -> p b m", m=TOK)

                def bc(x):
                    return x.unsqueeze(2).to_broadcast([P, 8, TOK])

                dve.wait_ge(lgT_sb, 1)
                link(dve.tensor_reduce(dm, im(lgT), AX, ALU.max))
                link.sync()
                dve.wait_ge(lg_ps, 1)
                dve.tensor_tensor(im(lgT), im(lgT), bc(dm), ALU.subtract).then_inc(d_sh, 1)
                link(dve.tensor_reduce(cm, im(bank(B_LG)), AX, ALU.max))
                link.sync()
                dve.tensor_tensor(im(ce), im(bank(B_LG)), bc(cm), ALU.subtract).then_inc(c_sh, 1)
                dve.wait_ge(d_exp, 1)
                link(dve.tensor_reduce(dsum, im(lgT), AX, ALU.add))
                link.sync()
                link(dve.reciprocal(dsum, dsum))
                link.sync()
                dve.tensor_tensor(im(lgT), im(lgT), bc(dsum), ALU.mult).then_inc(d_rdy, 1)
                dve.wait_ge(c_exp, 1)
                link(dve.tensor_reduce(cs, im(ce), AX, ALU.add))
                link.sync()
                link(dve.reciprocal(cs, cs))
                dve.wait_ge(d_ps, 1)
                dve.tensor_copy(d_sb, bank(B_D)).then_inc(d_cp, 1)
                link.sync()
                dve.tensor_tensor(im(ce), im(ce), bc(cs), ALU.mult).then_inc(c_rdy, 1)
                dve.wait_ge(zx, 2)
                dve.wait_ge(xs_ps, 1)
                link(spread(0, dve.tensor_copy))
                link.sync()

        (xg_rdy, up_ps, hd_rdy, hT_ps, hT_v, hT_a, y_ps, y_rdy) = (
            s(n) for n in ("xg", "up_ps", "hid", "hidT_ps", "hidT_v", "hidT_a", "y_ps", "y_rdy"))
        bias_in = [s(f"bias{k}_in") for k in range(2)]
        y_out = [s(f"y{k}_out") for k in range(2)]
        B_UP, B_HT, B_YX = 0, 4, 6
        NHF = HID // 2
        y_rows = y_slots.rearrange("n (b m) -> (n b) m", m=EMB)

        with nc.Block() as block:
            @block.sync
            def _(sp):
                for k in range(2):
                    sp.dma_start(xbias[k], d["x_bias"][k]).then_inc(bias_in[k], 16)
                with sp.Fori(0, NGRP // 2 - 1) as k:
                    for odd in range(2):
                        g = k * 2 + odd
                        sp.wait_ge(up_ps, g + 1)
                        load_part(sp, g + 2, odd, 0)
                        sp.wait_ge(y_ps, g + 1)
                        sp.dma_start(xbias[odd], d["x_bias"][bass.ds(g + 2, 1)].rearrange("o e n -> (o e) n")).then_inc(bias_in[odd], 16)
                        load_part(sp, g + 2, odd, 1)

            @block.tensor
            def _(pe):
                def group(g, k, odd):
                    pe.wait_ge(bias_in[odd], (k + 1) * 16)
                    pe.wait_ge(xg_rdy, g + 1)
                    pe.wait_ge(part_in[odd][0], (k + 1) * 16)
                    for nh in range(2):
                        cols = slice(nh * NHF, (nh + 1) * NHF)
                        b = B_UP + 2 * odd + nh
                        pe.matmul(bank(b, NHF), C("b_rows", GRP), xbias[odd][:, cols], start=True, stop=False, skip_group_check=True)
                        for step in range(3):
                            for q in range(QP):
                                w1a, w1b = w1_of(odd, q)
                                x = xg_b[odd][:, q * 2 * NIMG:(q + 1) * 2 * NIMG] if step == 2 else \
                                    xg_a[odd][:, (2 * q + step) * 2 * NIMG:(2 * q + step + 1) * 2 * NIMG]
                                w = w1b[:, cols] if step == 2 else w1a[:, step, cols]
                                mm = pe.matmul(bank(b, NHF)[32 * q:32 * (q + 1)], x, w, start=False, stop=(step == 2),
                                               skip_group_check=True)
                    mm.then_inc(up_ps, 1)
                    pe.wait_ge(hd_rdy, g + 1)
                    for c in range(NFC):
                        tr = pe.transpose(psum[:, B_HT * 512 + c * P:B_HT * 512 + (c + 1) * P], hid[:, c * P:(c + 1) * P], ident)
                    tr.then_inc(hT_ps, 1)
                    keep_warm(pe, 12, B_UP + 2 * odd)
                    pe.wait_ge(hT_v, g + 1)
                    pe.wait_ge(hT_a, g + 1)
                    pe.wait_ge(part_in[odd][1], (k + 1) * 16)
                    o = bank(B_YX + odd, 2 * EMB).rearrange("p (a n) -> p a n", a=2)
                    pe.matmul(o, C("b_rows", GRP), xbias[odd][:, HID:HID + EMB].unsqueeze(1).to_broadcast([GRP, 2, EMB]),
                              start=True, stop=False, skip_group_check=True)
                    for c in range(NFC):
                        for q in range(QP):
                            w2 = w2_of(odd, q)
                            mm = pe.matmul(o[32 * q:32 * (q + 1)], hidT[:, c * P + 32 * q:c * P + 32 * (q + 1)], w2[:, :, c, :],
                                           start=False, stop=(c == NFC - 1), skip_group_check=True)
                    mm.then_inc(y_ps, 1)

                keep_warm(pe, 8, B_HT)
                with pe.Fori(0, NGRP // 2) as k:
                    group(k * 2, k, 0)
                    group(k * 2 + 1, k, 1)

            @block.scalar
            def _(act):
                def group(g, k, odd):
                    act.wait_ge(up_ps, g + 1)
                    act.activation(hid.rearrange("p (a f) -> p a f", a=2),
                                   psum[:, (B_UP + 2 * odd) * 512:(B_UP + 2 * odd + 2) * 512].rearrange("p (a f) -> p a f", a=2)[:, :, 0:NHF],
                                   ACT.Gelu).then_inc(hd_rdy, 1)
                    act.wait_ge(hT_ps, g + 1)
                    act.copy(hidT[:, 512:HID], bank(B_HT + 1, HID - 512)).then_inc(hT_a, 1)
                    act.wait_ge(y_rdy, g + 1)
                    act.dma_start(y_rows[bass.ds(g * P, P), :], yout[:, odd, :]).then_inc(y_out[odd], 16)

                act.preload_act_table(ACT.Gelu)
                for k in range(2):
                    act.sem_inc(y_out[k], 16)
                with act.Fori(0, NGRP // 2) as k:
                    group(k * 2, k, 0)
                    group(k * 2 + 1, k, 1)
                for k in range(2):
                    act.wait_ge(y_out[k], 16 + 16 * NGRP // 2)

            @block.vector
            def _(dve):
                def inputs(g, odd):
                    dve.tensor_scalar(xg_a[odd], x_a[:, bass.ds(g * GRP * 2 * NIMG, GRP * 2 * NIMG)] if not isinstance(g, int) else
                                      x_a[:, g * GRP * 2 * NIMG:(g + 1) * GRP * 2 * NIMG], 1.0, None, ALU.mult)
                    dve.tensor_scalar(xg_b[odd], x_b[:, bass.ds(g * GRP * NIMG, GRP * NIMG)] if not isinstance(g, int) else
                                      x_b[:, g * GRP * NIMG:(g + 1) * GRP * NIMG], 1.0, None, ALU.mult).then_inc(xg_rdy, 1)

                def group(g, k, odd):
                    dve.wait_ge(hT_ps, g + 1)
                    dve.tensor_copy(hidT[:, 0:512], bank(B_HT)).then_inc(hT_v, 1)
                    dve.wait_ge(y_ps, g + 1)
                    o = bank(B_YX + odd, 2 * EMB)
                    dve.tensor_scalar(y_t, o[:, 0:EMB], C("par0"), None, ALU.mult).then_inc(y_half, 1)
                    dve.wait_ge(y_out[odd], k * 16 + 16)
                    dve.wait_ge(y_half, g + 1)
                    dve.scalar_tensor_tensor(out=yout[:, odd, :], in0=o[:, EMB:2 * EMB], scalar=C("par1"), in1=y_t,
                                             op0=ALU.mult, op1=ALU.add).then_inc(y_rdy, 1)

                y_t = x_n
                y_half = s("y_half")
                inputs(0, 0)
                inputs(1, 1)
                with dve.Fori(0, NGRP // 2 - 1) as k:
                    for odd in range(2):
                        group(k * 2 + odd, k, odd)
                        inputs(k * 2 + odd + 2, odd)
                for odd in range(2):
                    group(NGRP - 2 + odd, NGRP // 2 - 1, odd)

        y_all = ring[:, 0:HIMG * EMB]
        res = ring[:, PAIR_W:PAIR_W + NT * EMB].rearrange("p (i n) -> p i n", i=NT)
        y_in, c_ps, r_rdy, stored = [s("y0_in"), s("y1_in")], s("c_ps"), s("result"), s("stored")
        out_t = out.rearrange("(i p) n -> p i n", p=P)
        with nc.Block() as block:
            @block.sync
            def _(sp):
                for hf in range(2):
                    sp.dma_start(y_all[hf * NX:(hf + 1) * NX], y_slots[:, hf * HIMG * EMB:(hf + 1) * HIMG * EMB]).then_inc(y_in[hf], 16)
                for i in range(0, NT, 2):
                    sp.wait_ge(r_rdy, i + 2)
                    sp.dma_start(out_t[:, i:i + 2, :], res[:, i:i + 2, :]).then_inc(stored, 16)
                sp.wait_ge(stored, 16 * NT // 2)

            @block.tensor
            def _(pe):
                keep_warm(pe, 16, 7)
                for hf in range(2):
                    pe.wait_ge(y_in[hf], 16)
                    for b in range(HIMG):
                        i = hf * (NT // 2) + b // 2
                        rows = slice(hf * NX, (hf + 1) * NX)
                        mm = pe.matmul(bank(i, EMB)[(b % 2) * TOK:(b % 2 + 1) * TOK], c_T[rows, b * TOK:(b + 1) * TOK],
                                       y_all[rows, b * EMB:(b + 1) * EMB], start=True, stop=True)
                        if b % 2:
                            mm.then_inc(c_ps, 1)

            @block.vector
            def _(dve):
                for i in range(NT):
                    dve.wait_ge(c_ps, i + 1)
                    dve.tensor_tensor(res[:, i, :], h[:, i, :], bank(i, EMB), ALU.add).then_inc(r_rdy, 1)


def host_layout(x):
    import numpy as np

    f = np.float32
    n = {k: np.asarray(v) for k, v in x.items()}

    def rows(a, extra=None, rows_=P):
        o = np.zeros((rows_, a.shape[1]), f)
        o[:a.shape[0]] = a
        if extra is not None:
            o[a.shape[0]] = extra
        return o

    def col2(v):
        o = np.zeros((P, 2), f)
        o[:, 0] = v[:P]
        o[:EB, 1] = v[P:]
        return o

    def rep(v):
        return np.broadcast_to(v.reshape(1, -1), (P, v.size)).astype(f)

    def chunks(v):
        return v.reshape(NCH, P, -1).transpose(1, 0, 2).reshape(P, -1)

    d = {}
    img = n["x"].reshape(NIMG, 3, 8, 16, 8, 16)
    feat = img.transpose(3, 5, 1, 0, 2, 4).reshape(NPC, P, NTOK)
    d["patches"] = np.ascontiguousarray(feat.transpose(1, 0, 2))
    d["tok_w"] = np.ascontiguousarray(n["L0_tok_W"].T.reshape(NPC, P, EMB).transpose(1, 0, 2))
    d["tok_b"] = n["L0_tok_b"].reshape(1, EMB)

    c = np.zeros((P, NCST), f)

    def put(name, a, rows_=P):
        i, j = CST[name]
        c[:rows_, i:j] = a

    put("ident", np.eye(P))
    put("upper", np.triu(np.ones((P, P)), 1))
    put("ones", 1.0)
    t = np.arange(P) % TOK
    put("causal", np.where(np.arange(TOK)[None] <= t[:, None], 0.0, -BIG))
    put("kmask", (np.arange(P)[:, None] // HD == np.arange(NHA)[None]) * (1.0 / np.sqrt(f(HD))))
    freqs = f(1.0) / np.power(f(10000.0), np.arange(0, HD, 2, dtype=f) / f(HD)).astype(f)
    ang = np.outer(t.astype(f), freqs).astype(f)
    put("cos2", np.repeat(np.cos(ang), 2, axis=1))
    put("sin", np.sin(ang))
    put("nsin", -np.sin(ang))
    put("iota", np.arange(NEXP)[None])
    put("iota_far", np.arange(NEXP)[None] + 1000.0)
    put("by128", np.arange(NT)[None] * 128.0)
    put("block", np.arange(NBLK)[None])
    carry = np.ones((NEXP, NT))
    carry[:, 0] = 0
    put("carry", carry.reshape(1, -1))
    put("neg_half", -0.5)
    put("half", 0.5)
    put("b_rows", (np.arange(GRP)[:, None] == np.arange(P)[None] // NIMG), GRP)
    put("par0", ((np.arange(P) // NIMG) % 2 == 0)[:, None])
    put("par1", ((np.arange(P) // NIMG) % 2 == 1)[:, None])
    d["cst"] = c
    s = np.zeros((XPJ, 2 * NST, P), f)
    for k in range(2 * NST):
        s[[k, 2 * NST + k, 4 * NST + k], k, :] = 1.0
    d["sel"] = np.where(s > 0, 0x3F80, 0).astype(np.uint16)

    v = np.zeros((P, NVEC), f)

    def putv(name, a):
        i, j = VEC[name]
        v[:, i:j] = a

    putv("nscale", col2(n["L0_attn_norm_scale"]))
    putv("nbias", col2(n["L0_attn_norm_bias"]))
    putv("norm1", col2(n["L1_attn_norm1_w"]))
    norm2 = col2(n["L1_attn_norm2_w"])
    norm2[EB:, 1] = norm2[:EB, 1]
    putv("norm2", norm2)
    putv("conv_w", chunks(n["L1_attn_conv_w"]))
    putv("conv_b", chunks(n["L1_attn_conv_b"]))
    putv("dt_b", chunks(n["L1_attn_dt_proj_b"]))
    putv("A_log", chunks(n["L1_attn_A_log"]))
    putv("D", chunks(n["L1_attn_D_param"]))
    putv("rezero", rep(n["L0_attn_rezero"]))
    putv("scale", rep(n["L1_ffn_scale"]))
    putv("sinks", rep(n["L0_attn_sinks"]))
    putv("ls_ssm", rep(n["L1_attn_ls_ssm_g"]))
    putv("ls_ffn", rep(n["L1_attn_ls_ffn_g"]))
    d["vec"] = v

    def two(w, b=None):
        return [rows(w[:P]), rows(w[P:], b)]

    d["atw"] = np.concatenate(
        two(n["L0_attn_W_attn"], n["L0_attn_b_attn"]) + two(n["L0_attn_W_proj"], n["L0_attn_b_proj"])
        + two(n["L0_ffn_Wg"], n["L0_ffn_bg"]) + two(n["L1_attn_gate_w"]) + two(n["L1_ffn_phi"][:, :, 0]), axis=1)

    def expert_rows(w, b=None):
        return [np.concatenate([rows(w[e, :P]) for e in range(NEXP)], axis=1),
                np.concatenate([rows(w[e, P:], None if b is None else b[e]) for e in range(NEXP)], axis=1)]

    def down(w):
        return w.reshape(w.shape[0], NFC, P, EMB).transpose(2, 0, 1, 3).reshape(P, -1)

    d["moe0"] = np.concatenate(expert_rows(n["L0_ffn_W1"], n["L0_ffn_b1"]) + [down(n["L0_ffn_W2"])], axis=1)
    d["moe0_b2"] = n["L0_ffn_b2"].reshape(1, NEXP * EMB)
    (w1a, w1b), (w3a, w3b) = expert_rows(n["L1_attn_w1"]), expert_rows(n["L1_attn_w3"])
    d["moe1_w13"] = np.concatenate([w1a, w3a, np.concatenate([w1b[:EB], w3b[:EB]], axis=0)], axis=1)
    d["moe1_w2"] = down(n["L1_attn_w2"])
    xw = np.zeros((DIN, XPJ), f)
    xw[:, :DTR] = n["L1_attn_x_proj_w"][:, :DTR]
    xw[:, BC0:] = n["L1_attn_x_proj_w"][:, DTR:]
    d["ssw"] = np.concatenate(two(n["L1_attn_in_proj_w"]) + [chunks(xw), rows(n["L1_attn_dt_proj_w"]),
                                                             chunks(n["L1_attn_out_proj_w"])], axis=1)
    w1 = n["L1_ffn_w1"].reshape(NPAIR, 2, EMB, HID)
    w2 = n["L1_ffn_w2"].reshape(NPAIR, 2, NFC, P, EMB)
    w1 = np.concatenate([w1[:, :, :P].transpose(0, 2, 1, 3).reshape(NPAIR, P, 2 * HID), w1[:, :, P:].reshape(NPAIR, P, HID)], axis=2)
    w2 = w2.transpose(0, 3, 1, 2, 4).reshape(NPAIR, P, PART_W)
    d["groups"] = np.stack([w.reshape(NGRP, QP, P, PART_W).transpose(0, 2, 1, 3).reshape(NGRP, P, QP * PART_W) for w in (w1, w2)])
    d["x_bias"] = np.concatenate([n["L1_ffn_b1"], n["L1_ffn_b2"]], axis=1).reshape(NGRP, GRP, HID + EMB)
    return {k: np.ascontiguousarray(a) for k, a in d.items()}


def kernel(**inputs):
    import numpy as np
    from concourse import bacc
    from concourse.bass_utils import run_bass_kernel_spmd

    nc = bacc.Bacc("TRN2", target_bir_lowering=False, num_devices=1)
    arrays = host_layout(inputs)
    d = {k: nc.dram_tensor("in_" + k, a.shape, mybir.dt.from_np(a.dtype), kind="ExternalInput").ap() for k, a in arrays.items()}
    out = nc.dram_tensor("out", [NTOK, EMB], F32, kind="ExternalOutput").ap()
    build(nc, d, out)
    r = run_bass_kernel_spmd(nc, [{"in_" + k: a for k, a in arrays.items()}], core_ids=[0])
    return np.asarray(r.results[0]["out"]).reshape(NIMG, TOK, EMB)
```
